# Optimizing a Trainium2 kernel written in Bass

```python
import numpy as np
import jax
import jax.numpy as jnp

def _softmax(x, axis=-1):
    return jax.nn.softmax(x, axis=axis)

def _gelu(x):
    return jax.nn.gelu(x, approximate=True)

def _silu(x):
    return jax.nn.silu(x)

def _sigmoid(x):
    return jax.nn.sigmoid(x)

def _layernorm(x, axis=-1, eps=1e-05):
    m = jnp.mean(x, axis=axis, keepdims=True)
    v = jnp.var(x, axis=axis, keepdims=True)
    return (x - m) / jnp.sqrt(v + eps)

def _scatter_add(tgt, idx, src, axis=0):
    return tgt.at[idx].add(src)

def _segment_sum(src, seg, n):
    return jax.ops.segment_sum(src, seg, n)
kernel_name = 'mk_flamingo_gated_d4_seqx_r8_b1564c'

def setup_inputs(seed: int=0):
    np.random.seed(seed)
    _w = jnp.asarray

    def _rec_inputs():
        import jax
        import jax.numpy as jnp
        _rk = jax.random.key(seed)
        x = -0.0002928 + 1 * jax.random.normal(jax.random.fold_in(_rk, 1), (8, 128, 128), jnp.float32)
        _lenS = 128 - jax.random.randint(jax.random.fold_in(_rk, 7), (8,), 0, max(1, 128 // 4) + 1, jnp.int32)
        _lenS2 = 128 - jax.random.randint(jax.random.fold_in(_rk, 8), (8,), 0, max(1, 128 // 4) + 1, jnp.int32)
        _ctx_1024P = jax.random.normal(jax.random.fold_in(_rk, 11), (8, 16, 128), jnp.float32)
        _ctx_1024c = jax.random.dirichlet(jax.random.fold_in(_rk, 511), 0.3 * jnp.ones((16,), jnp.float32), (8, 128))
        _ctx_1024t = jnp.einsum('bsk,bkd->bsd', _ctx_1024c, _ctx_1024P)
        _ctx_1024t = _ctx_1024t * jax.lax.rsqrt(jnp.mean(jnp.square(_ctx_1024t)) + 1e-12) * 0.953939
        ctx_1024 = -1.39393e-06 + 0.999914 * (_ctx_1024t + 0.3 * jax.random.normal(jax.random.fold_in(_rk, 611), (8, 128, 128), jnp.float32))
        _validS = jnp.arange(128)[None, :] < _lenS[:, None]
        _validS2 = jnp.arange(128)[None, :] < _lenS2[:, None]
        _causal = jnp.tril(jnp.ones((128, 128), dtype=bool))
        mask_BxS2_bk0 = jnp.logical_not(jnp.broadcast_to(_validS2[:, :], (8, 128)))
        _g = jax.random.normal(jax.random.fold_in(_rk, 9001), (2, 4), jnp.float32)
        _g = jnp.sign(_g) * jnp.maximum(jnp.abs(_g), 1.0) + (_g == 0) * 1.0
        g_xattn = _g[0]
        g_ffn = _g[1]
        return (x, ctx_1024, mask_BxS2_bk0, g_xattn, g_ffn)
    x, ctx_1024, mask_BxS2_bk0, g_xattn, g_ffn = _rec_inputs()

    def _L0_xattn_setup():
        import jax, jax.numpy as jnp
        import numpy as np
        import math
        B, SQ, SKV = (2, 256, 256)
        DQ, DKV, H, NH = (128, 128, 128, 16)
        HD = H // NH
        key = jax.random.key(seed)
        ks = jax.random.split(key, 12)
        s = 0.02
        return {'query_input': jax.random.normal(ks[0], (B, SQ, DQ), jnp.float32), 'key_value_input': jax.random.normal(ks[1], (B, SKV, DKV), jnp.float32), 'key_padding_mask': jax.random.randint(ks[2], (B, SKV), 0, 2) > 0, 'Wq': jax.random.normal(ks[3], (DQ, H), jnp.float32) * s, 'bq': jnp.zeros((H,), jnp.float32), 'Wk': jax.random.normal(ks[4], (DKV, H), jnp.float32) * s, 'bk': jnp.zeros((H,), jnp.float32), 'Wv': jax.random.normal(ks[5], (DKV, H), jnp.float32) * s, 'bv': jnp.zeros((H,), jnp.float32), 'Wo': jax.random.normal(ks[6], (H, DQ), jnp.float32) * s, 'bo': jnp.zeros((DQ,), jnp.float32)}
    _L0_xattn_all = _L0_xattn_setup()
    _L0_xattn_in = {k: v for k, v in _L0_xattn_all.items() if k in ('Wq', 'bq', 'Wk', 'bk', 'Wv', 'bv', 'Wo', 'bo')}
    del _L0_xattn_all

    def _L0_ffn_setup():
        import jax, jax.numpy as jnp
        import numpy as np
        B, S, H = (1, 256, 128)
        E, K = (16, 4)
        G, TG = (4, 2)
        I_MOE = 64
        N_SH = 2
        SCALE = 2.5

        def _mlp(x, gw, uw, dw):
            return jax.nn.silu(x @ gw.T) * (x @ uw.T) @ dw.T

        def _route(x2d, router_weight, e_bias):
            T = x2d.shape[0]
            scores = jax.nn.sigmoid(x2d @ router_weight.T)
            sc = scores + e_bias[None, :]
            group_scores = jnp.sum(jax.lax.top_k(sc.reshape(T, G, E // G), 2)[0], axis=-1)
            _, gidx = jax.lax.top_k(group_scores, TG)
            gmask = jnp.zeros((T, G), sc.dtype).at[jnp.arange(T)[:, None], gidx].set(1.0)
            smask = jnp.repeat(gmask, E // G, axis=1)
            masked = jnp.where(smask > 0, sc, 0.0)
            _, tidx = jax.lax.top_k(masked, K)
            tw = jnp.take_along_axis(scores, tidx, axis=1)
            tw = tw / (jnp.sum(tw, axis=-1, keepdims=True) + 1e-20)
            tw = tw * SCALE
            return (tidx, tw)

        def _moe_forward(hidden_states, router_weight, e_bias, gate_w, up_w, down_w, sh_gate_w, sh_up_w, sh_down_w):
            orig_shape = hidden_states.shape
            x = hidden_states.reshape(-1, H)
            T = x.shape[0]
            tidx, tw = _route(x, router_weight, e_bias)
            g = jnp.einsum('th,eih->tei', x, gate_w)
            u = jnp.einsum('th,eih->tei', x, up_w)
            h = jax.nn.silu(g) * u
            yo = jnp.einsum('tei,ehi->teh', h, down_w)
            combine = jnp.zeros((T, E), tw.dtype).at[jnp.arange(T)[:, None], tidx].add(tw)
            routed = jnp.einsum('te,teh->th', combine, yo)
            shared = _mlp(hidden_states.reshape(-1, H), sh_gate_w, sh_up_w, sh_down_w)
            return (routed + shared).reshape(orig_shape)
        key = jax.random.key(seed)
        ks = jax.random.split(key, 9)
        s = 0.02
        return {'hidden_states': jax.random.normal(ks[0], (B, S, H), jnp.float32), 'router_weight': jax.random.normal(ks[1], (E, H), jnp.float32) * s, 'e_bias': jnp.zeros((E,), jnp.float32), 'gate_w': jax.random.normal(ks[2], (E, I_MOE, H), jnp.float32) * s, 'up_w': jax.random.normal(ks[3], (E, I_MOE, H), jnp.float32) * s, 'down_w': jax.random.normal(ks[4], (E, H, I_MOE), jnp.float32) * s, 'sh_gate_w': jax.random.normal(ks[5], (N_SH * I_MOE, H), jnp.float32) * s, 'sh_up_w': jax.random.normal(ks[6], (N_SH * I_MOE, H), jnp.float32) * s, 'sh_down_w': jax.random.normal(ks[7], (H, N_SH * I_MOE), jnp.float32) * s}
    _L0_ffn_all = _L0_ffn_setup()
    _L0_ffn_in = {k: v for k, v in _L0_ffn_all.items() if k in ('router_weight', 'e_bias', 'gate_w', 'up_w', 'down_w', 'sh_gate_w', 'sh_up_w', 'sh_down_w')}
    del _L0_ffn_all

    def _L1_xattn_setup():
        import jax, jax.numpy as jnp
        import numpy as np
        B, S, D = (8, 256, 128)
        key = jax.random.key(seed)
        ks = jax.random.split(key, 13)
        s = 1.0 / np.sqrt(D)
        return {'queries': jax.random.normal(ks[0], (B, S, D), jnp.float32), 'keys': jax.random.normal(ks[1], (B, S, D), jnp.float32), 'values': jax.random.normal(ks[2], (B, S, D), jnp.float32), 'Wq': jax.random.normal(ks[3], (D, D), jnp.float32) * s, 'bq': jnp.zeros((D,), jnp.float32), 'Wk': jax.random.normal(ks[4], (D, D), jnp.float32) * s, 'bk': jnp.zeros((D,), jnp.float32), 'Wv': jax.random.normal(ks[5], (D, D), jnp.float32) * s, 'bv': jnp.zeros((D,), jnp.float32), 'Wg': jax.random.normal(ks[6], (D, D), jnp.float32) * s, 'bg': jnp.zeros((D,), jnp.float32), 'Wo': jax.random.normal(ks[7], (D, D), jnp.float32) * s, 'bo': jnp.zeros((D,), jnp.float32)}
    _L1_xattn_all = _L1_xattn_setup()
    _L1_xattn_in = {k: v for k, v in _L1_xattn_all.items() if k in ('Wq', 'bq', 'Wk', 'bk', 'Wv', 'bv', 'Wg', 'bg', 'Wo', 'bo')}
    del _L1_xattn_all

    def _L1_ffn_setup():
        import jax, jax.numpy as jnp
        import numpy as np
        BITS = 8
        LORA_RANK = 16
        LORA_ALPHA = 32
        SCALING = LORA_ALPHA / LORA_RANK

        def fake_quant_weight(w, bits=BITS):
            qmax = 2.0 ** (bits - 1) - 1
            scale = jnp.max(jnp.abs(w)) / qmax
            wq = jnp.clip(jnp.round(w / scale), -qmax - 1, qmax) * scale
            return w + jax.lax.stop_gradient(wq - w)

        def qat_lora_linear(x, W, b, A, B):
            Wq = fake_quant_weight(W)
            base = jnp.einsum('bsi,oi->bso', x, Wq) + b
            lora = jnp.einsum('bsr,or->bso', jnp.einsum('bsi,ri->bsr', x, A), B)
            return base + SCALING * lora
        key = jax.random.key(seed)
        ks = jax.random.split(key, 9)
        d, f = (128, 512)
        s_in = 1.0 / np.sqrt(d)
        s_ff = 1.0 / np.sqrt(f)
        return {'hidden_states': jax.random.normal(ks[0], (4, 256, d), jnp.float32), 'W_fc': jax.random.normal(ks[1], (f, d), jnp.float32) * s_in, 'b_fc': jnp.zeros((f,), jnp.float32), 'A_fc': jax.random.normal(ks[2], (LORA_RANK, d), jnp.float32) * s_in, 'B_fc': jnp.zeros((f, LORA_RANK), jnp.float32), 'W_proj': jax.random.normal(ks[3], (d, f), jnp.float32) * s_ff, 'b_proj': jnp.zeros((d,), jnp.float32), 'A_proj': jax.random.normal(ks[4], (LORA_RANK, f), jnp.float32) * s_ff, 'B_proj': jnp.zeros((d, LORA_RANK), jnp.float32)}
    _L1_ffn_all = _L1_ffn_setup()
    _L1_ffn_in = {k: v for k, v in _L1_ffn_all.items() if k in ('W_fc', 'b_fc', 'A_fc', 'B_fc', 'W_proj', 'b_proj', 'A_proj', 'B_proj')}
    del _L1_ffn_all

    def _L2_xattn_setup():
        import jax, jax.numpy as jnp
        import numpy as np
        DIM = 128
        HEADS = 8
        DIM_HEAD = 64
        INNER = HEADS * DIM_HEAD
        EPS = 1e-05

        def layernorm(x, w, b):
            mu = jnp.mean(x, axis=-1, keepdims=True)
            var = jnp.var(x, axis=-1, keepdims=True)
            return (x - mu) * jax.lax.rsqrt(var + EPS) * w + b
        key = jax.random.key(seed)
        ks = jax.random.split(key, 7)
        b, n_media, n_lat = (16, 256, 64)
        x = jax.random.normal(ks[0], (b, n_media, DIM), dtype=jnp.float32)
        latents = jax.random.normal(ks[1], (b, n_lat, DIM), dtype=jnp.float32)
        ln_m_w = jnp.ones((DIM,), jnp.float32)
        ln_m_b = jnp.zeros((DIM,), jnp.float32)
        ln_l_w = jnp.ones((DIM,), jnp.float32)
        ln_l_b = jnp.zeros((DIM,), jnp.float32)
        Wq = jax.random.normal(ks[2], (DIM, INNER), dtype=jnp.float32) * DIM ** (-0.5)
        Wkv = jax.random.normal(ks[3], (DIM, 2 * INNER), dtype=jnp.float32) * DIM ** (-0.5)
        Wout = jax.random.normal(ks[4], (INNER, DIM), dtype=jnp.float32) * INNER ** (-0.5)
        return {'x': x, 'latents': latents, 'ln_m_w': ln_m_w, 'ln_m_b': ln_m_b, 'ln_l_w': ln_l_w, 'ln_l_b': ln_l_b, 'Wq': Wq, 'Wkv': Wkv, 'Wout': Wout}
    _L2_xattn_all = _L2_xattn_setup()
    _L2_xattn_in = {k: v for k, v in _L2_xattn_all.items() if k in ('ln_m_w', 'ln_m_b', 'ln_l_w', 'ln_l_b', 'Wq', 'Wkv', 'Wout')}
    del _L2_xattn_all

    def _L2_ffn_setup():
        import jax, jax.numpy as jnp
        import numpy as np
        D = 128
        H = 128
        E = 8
        K = 2
        I = 2 * 128
        ROUTE_SCALE = 1.0
        key = jax.random.key(seed)
        ks = jax.random.split(key, 12)
        s = lambda *sh: 1.0 / np.sqrt(sh[-1])
        return {'x': jax.random.normal(ks[0], (1, 256, D), jnp.float32), 'gate_w': jax.random.normal(ks[1], (E, D), jnp.float32) * s(E, D), 'w1': jax.random.normal(ks[2], (E, H, D), jnp.float32) * s(H, D), 'b1': jax.random.normal(ks[3], (E, H), jnp.float32) * 0.01, 'w2': jax.random.normal(ks[4], (E, D, H), jnp.float32) * s(D, H), 'b2': jax.random.normal(ks[5], (E, D), jnp.float32) * 0.01, 'w3': jax.random.normal(ks[6], (E, H, D), jnp.float32) * s(H, D), 'b3': jax.random.normal(ks[7], (E, H), jnp.float32) * 0.01, 'sw1': jax.random.normal(ks[8], (I, D), jnp.float32) * s(I, D), 'sw2': jax.random.normal(ks[9], (I, D), jnp.float32) * s(I, D), 'sw3': jax.random.normal(ks[10], (D, I), jnp.float32) * s(D, I)}
    _L2_ffn_all = _L2_ffn_setup()
    _L2_ffn_in = {k: v for k, v in _L2_ffn_all.items() if k in ('gate_w', 'w1', 'b1', 'w2', 'b2', 'w3', 'b3', 'sw1', 'sw2', 'sw3')}
    del _L2_ffn_all

    def _L3_xattn_setup():
        import jax, jax.numpy as jnp
        import numpy as np
        EMBED_DIM = 128
        NUM_HEADS = 16
        HEAD_DIM = EMBED_DIM // NUM_HEADS
        B, T, S = (2, 256, 256)
        key = jax.random.key(seed)
        ks = jax.random.split(key, 5)
        scale_w = 1.0 / np.sqrt(EMBED_DIM)
        return {'q': jax.random.normal(ks[0], (B, T, EMBED_DIM), dtype=jnp.float32), 'k': jax.random.normal(ks[1], (B, S, EMBED_DIM), dtype=jnp.float32), 'v': jax.random.normal(ks[2], (B, S, EMBED_DIM), dtype=jnp.float32), 'in_proj_weight': jax.random.normal(ks[3], (3 * EMBED_DIM, EMBED_DIM), dtype=jnp.float32) * scale_w, 'in_proj_bias': jnp.zeros((3 * EMBED_DIM,), dtype=jnp.float32), 'out_w': jax.random.normal(ks[4], (EMBED_DIM, EMBED_DIM), dtype=jnp.float32) * scale_w, 'out_b': jnp.zeros((EMBED_DIM,), dtype=jnp.float32)}
    _L3_xattn_all = _L3_xattn_setup()
    _L3_xattn_in = {k: v for k, v in _L3_xattn_all.items() if k in ('in_proj_weight', 'in_proj_bias', 'out_w', 'out_b')}
    del _L3_xattn_all

    def _L3_ffn_setup():
        import jax, jax.numpy as jnp
        import numpy as np
        from jax import lax
        HIDDEN = 128
        INTER = 64
        E = 64
        K = 6
        G = 8
        TG = 4
        NSH = 2
        ISH = INTER * NSH

        def _moe_forward(hidden_states, gate_w, gate_bias, eg_w, eu_w, ed_w, sg_w, su_w, sd_w):
            B, S, H = hidden_states.shape
            x = hidden_states.reshape(-1, H)
            T = x.shape[0]
            shared = jax.nn.silu(x @ sg_w.T) * (x @ su_w.T) @ sd_w.T
            logits = x @ gate_w.T
            scores = jax.nn.sigmoid(logits) + gate_bias
            group_scores = scores.reshape(T, G, E // G).max(axis=-1)
            _, sel_groups = lax.top_k(group_scores, TG)
            group_mask = jnp.zeros((T, G), scores.dtype).at[jnp.arange(T)[:, None], sel_groups].set(1.0)
            mask = jnp.repeat(group_mask, E // G, axis=1)
            masked_scores = scores * mask
            topk_w, topk_i = lax.top_k(masked_scores, K)
            topk_w = topk_w / (topk_w.sum(axis=-1, keepdims=True) + 1e-08)
            comb = jnp.zeros((T, E), x.dtype).at[jnp.arange(T)[:, None], topk_i].add(topk_w)
            h = jax.nn.silu(jnp.einsum('th,eih->eti', x, eg_w)) * jnp.einsum('th,eih->eti', x, eu_w)
            routed = jnp.einsum('eti,ehi,te->th', h, ed_w, comb)
            return (shared + routed).reshape(B, S, H)
        key = jax.random.key(seed)
        ks = jax.random.split(key, 9)
        s = 0.02
        return {'hidden_states': jax.random.normal(ks[0], (1, 128, HIDDEN), jnp.float32), 'gate_w': jax.random.normal(ks[1], (E, HIDDEN), jnp.float32) * s, 'gate_bias': jnp.zeros((E,), jnp.float32), 'eg_w': jax.random.normal(ks[2], (E, INTER, HIDDEN), jnp.float32) * s, 'eu_w': jax.random.normal(ks[3], (E, INTER, HIDDEN), jnp.float32) * s, 'ed_w': jax.random.normal(ks[4], (E, HIDDEN, INTER), jnp.float32) * s, 'sg_w': jax.random.normal(ks[5], (ISH, HIDDEN), jnp.float32) * s, 'su_w': jax.random.normal(ks[6], (ISH, HIDDEN), jnp.float32) * s, 'sd_w': jax.random.normal(ks[7], (HIDDEN, ISH), jnp.float32) * s}
    _L3_ffn_all = _L3_ffn_setup()
    _L3_ffn_in = {k: v for k, v in _L3_ffn_all.items() if k in ('gate_w', 'gate_bias', 'eg_w', 'eu_w', 'ed_w', 'sg_w', 'su_w', 'sd_w')}
    del _L3_ffn_all
    return {'x': x, 'ctx_1024': ctx_1024, 'mask_BxS2_bk0': mask_BxS2_bk0, 'g_xattn': g_xattn, 'g_ffn': g_ffn, 'L0_xattn_Wq': _L0_xattn_in['Wq'], 'L0_xattn_bq': _L0_xattn_in['bq'], 'L0_xattn_Wk': _L0_xattn_in['Wk'], 'L0_xattn_bk': _L0_xattn_in['bk'], 'L0_xattn_Wv': _L0_xattn_in['Wv'], 'L0_xattn_bv': _L0_xattn_in['bv'], 'L0_xattn_Wo': _L0_xattn_in['Wo'], 'L0_xattn_bo': _L0_xattn_in['bo'], 'L0_ffn_router_weight': _L0_ffn_in['router_weight'], 'L0_ffn_e_bias': _L0_ffn_in['e_bias'], 'L0_ffn_gate_w': _L0_ffn_in['gate_w'], 'L0_ffn_up_w': _L0_ffn_in['up_w'], 'L0_ffn_down_w': _L0_ffn_in['down_w'], 'L0_ffn_sh_gate_w': _L0_ffn_in['sh_gate_w'], 'L0_ffn_sh_up_w': _L0_ffn_in['sh_up_w'], 'L0_ffn_sh_down_w': _L0_ffn_in['sh_down_w'], 'L1_xattn_Wq': _L1_xattn_in['Wq'], 'L1_xattn_bq': _L1_xattn_in['bq'], 'L1_xattn_Wk': _L1_xattn_in['Wk'], 'L1_xattn_bk': _L1_xattn_in['bk'], 'L1_xattn_Wv': _L1_xattn_in['Wv'], 'L1_xattn_bv': _L1_xattn_in['bv'], 'L1_xattn_Wg': _L1_xattn_in['Wg'], 'L1_xattn_bg': _L1_xattn_in['bg'], 'L1_xattn_Wo': _L1_xattn_in['Wo'], 'L1_xattn_bo': _L1_xattn_in['bo'], 'L1_ffn_W_fc': _L1_ffn_in['W_fc'], 'L1_ffn_b_fc': _L1_ffn_in['b_fc'], 'L1_ffn_A_fc': _L1_ffn_in['A_fc'], 'L1_ffn_B_fc': _L1_ffn_in['B_fc'], 'L1_ffn_W_proj': _L1_ffn_in['W_proj'], 'L1_ffn_b_proj': _L1_ffn_in['b_proj'], 'L1_ffn_A_proj': _L1_ffn_in['A_proj'], 'L1_ffn_B_proj': _L1_ffn_in['B_proj'], 'L2_xattn_ln_m_w': _L2_xattn_in['ln_m_w'], 'L2_xattn_ln_m_b': _L2_xattn_in['ln_m_b'], 'L2_xattn_ln_l_w': _L2_xattn_in['ln_l_w'], 'L2_xattn_ln_l_b': _L2_xattn_in['ln_l_b'], 'L2_xattn_Wq': _L2_xattn_in['Wq'], 'L2_xattn_Wkv': _L2_xattn_in['Wkv'], 'L2_xattn_Wout': _L2_xattn_in['Wout'], 'L2_ffn_gate_w': _L2_ffn_in['gate_w'], 'L2_ffn_w1': _L2_ffn_in['w1'], 'L2_ffn_b1': _L2_ffn_in['b1'], 'L2_ffn_w2': _L2_ffn_in['w2'], 'L2_ffn_b2': _L2_ffn_in['b2'], 'L2_ffn_w3': _L2_ffn_in['w3'], 'L2_ffn_b3': _L2_ffn_in['b3'], 'L2_ffn_sw1': _L2_ffn_in['sw1'], 'L2_ffn_sw2': _L2_ffn_in['sw2'], 'L2_ffn_sw3': _L2_ffn_in['sw3'], 'L3_xattn_in_proj_weight': _L3_xattn_in['in_proj_weight'], 'L3_xattn_in_proj_bias': _L3_xattn_in['in_proj_bias'], 'L3_xattn_out_w': _L3_xattn_in['out_w'], 'L3_xattn_out_b': _L3_xattn_in['out_b'], 'L3_ffn_gate_w': _L3_ffn_in['gate_w'], 'L3_ffn_gate_bias': _L3_ffn_in['gate_bias'], 'L3_ffn_eg_w': _L3_ffn_in['eg_w'], 'L3_ffn_eu_w': _L3_ffn_in['eu_w'], 'L3_ffn_ed_w': _L3_ffn_in['ed_w'], 'L3_ffn_sg_w': _L3_ffn_in['sg_w'], 'L3_ffn_su_w': _L3_ffn_in['su_w'], 'L3_ffn_sd_w': _L3_ffn_in['sd_w']}

def reference(x, ctx_1024, mask_BxS2_bk0, g_xattn, g_ffn, L0_xattn_Wq, L0_xattn_bq, L0_xattn_Wk, L0_xattn_bk, L0_xattn_Wv, L0_xattn_bv, L0_xattn_Wo, L0_xattn_bo, L0_ffn_router_weight, L0_ffn_e_bias, L0_ffn_gate_w, L0_ffn_up_w, L0_ffn_down_w, L0_ffn_sh_gate_w, L0_ffn_sh_up_w, L0_ffn_sh_down_w, L1_xattn_Wq, L1_xattn_bq, L1_xattn_Wk, L1_xattn_bk, L1_xattn_Wv, L1_xattn_bv, L1_xattn_Wg, L1_xattn_bg, L1_xattn_Wo, L1_xattn_bo, L1_ffn_W_fc, L1_ffn_b_fc, L1_ffn_A_fc, L1_ffn_B_fc, L1_ffn_W_proj, L1_ffn_b_proj, L1_ffn_A_proj, L1_ffn_B_proj, L2_xattn_ln_m_w, L2_xattn_ln_m_b, L2_xattn_ln_l_w, L2_xattn_ln_l_b, L2_xattn_Wq, L2_xattn_Wkv, L2_xattn_Wout, L2_ffn_gate_w, L2_ffn_w1, L2_ffn_b1, L2_ffn_w2, L2_ffn_b2, L2_ffn_w3, L2_ffn_b3, L2_ffn_sw1, L2_ffn_sw2, L2_ffn_sw3, L3_xattn_in_proj_weight, L3_xattn_in_proj_bias, L3_xattn_out_w, L3_xattn_out_b, L3_ffn_gate_w, L3_ffn_gate_bias, L3_ffn_eg_w, L3_ffn_eu_w, L3_ffn_ed_w, L3_ffn_sg_w, L3_ffn_su_w, L3_ffn_sd_w):
    import jax
    import jax.numpy as jnp

    def _L0_xattn_ref(query_input, key_value_input, key_padding_mask, Wq, bq, Wk, bk, Wv, bv, Wo, bo):
        import jax, jax.numpy as jnp
        import numpy as np
        import math
        B, SQ, SKV = (2, 256, 256)
        DQ, DKV, H, NH = (128, 128, 128, 16)
        HD = H // NH
        b, sq, _ = query_input.shape
        skv = key_value_input.shape[1]
        Q = query_input @ Wq + bq
        K = key_value_input @ Wk + bk
        V = key_value_input @ Wv + bv
        Q = Q.reshape(b, sq, NH, HD).transpose(0, 2, 1, 3)
        K = K.reshape(b, skv, NH, HD).transpose(0, 2, 1, 3)
        V = V.reshape(b, skv, NH, HD).transpose(0, 2, 1, 3)
        scores = jnp.einsum('bhqd,bhkd->bhqk', Q, K) / math.sqrt(HD)
        mask = key_padding_mask[:, None, None, :]
        scores = jnp.where(mask, -jnp.inf, scores)
        attn = jax.nn.softmax(scores, axis=-1)
        out = jnp.einsum('bhqk,bhkd->bhqd', attn, V)
        out = out.transpose(0, 2, 1, 3).reshape(b, sq, H)
        return out @ Wo + bo

    def _L0_ffn_ref(hidden_states, router_weight, e_bias, gate_w, up_w, down_w, sh_gate_w, sh_up_w, sh_down_w):
        import jax, jax.numpy as jnp
        import numpy as np
        B, S, H = (1, 256, 128)
        E, K = (16, 4)
        G, TG = (4, 2)
        I_MOE = 64
        N_SH = 2
        SCALE = 2.5

        def _mlp(x, gw, uw, dw):
            return jax.nn.silu(x @ gw.T) * (x @ uw.T) @ dw.T

        def _route(x2d, router_weight, e_bias):
            T = x2d.shape[0]
            scores = jax.nn.sigmoid(x2d @ router_weight.T)
            sc = scores + e_bias[None, :]
            group_scores = jnp.sum(jax.lax.top_k(sc.reshape(T, G, E // G), 2)[0], axis=-1)
            _, gidx = jax.lax.top_k(group_scores, TG)
            gmask = jnp.zeros((T, G), sc.dtype).at[jnp.arange(T)[:, None], gidx].set(1.0)
            smask = jnp.repeat(gmask, E // G, axis=1)
            masked = jnp.where(smask > 0, sc, 0.0)
            _, tidx = jax.lax.top_k(masked, K)
            tw = jnp.take_along_axis(scores, tidx, axis=1)
            tw = tw / (jnp.sum(tw, axis=-1, keepdims=True) + 1e-20)
            tw = tw * SCALE
            return (tidx, tw)

        def _moe_forward(hidden_states, router_weight, e_bias, gate_w, up_w, down_w, sh_gate_w, sh_up_w, sh_down_w):
            orig_shape = hidden_states.shape
            x = hidden_states.reshape(-1, H)
            T = x.shape[0]
            tidx, tw = _route(x, router_weight, e_bias)
            g = jnp.einsum('th,eih->tei', x, gate_w)
            u = jnp.einsum('th,eih->tei', x, up_w)
            h = jax.nn.silu(g) * u
            yo = jnp.einsum('tei,ehi->teh', h, down_w)
            combine = jnp.zeros((T, E), tw.dtype).at[jnp.arange(T)[:, None], tidx].add(tw)
            routed = jnp.einsum('te,teh->th', combine, yo)
            shared = _mlp(hidden_states.reshape(-1, H), sh_gate_w, sh_up_w, sh_down_w)
            return (routed + shared).reshape(orig_shape)
        return _moe_forward(hidden_states, router_weight, e_bias, gate_w, up_w, down_w, sh_gate_w, sh_up_w, sh_down_w)

    def _L1_xattn_ref(queries, keys, values, Wq, bq, Wk, bk, Wv, bv, Wg, bg, Wo, bo):
        import jax, jax.numpy as jnp
        import numpy as np
        B, S, D = (8, 256, 128)
        q = queries @ Wq + bq
        k = keys @ Wk + bk
        v = values @ Wv + bv
        scores = jnp.einsum('bqd,bkd->bqk', q, k)
        attn = jax.nn.softmax(scores, axis=-1)
        context = jnp.einsum('bqk,bkd->bqd', attn, v)
        gate = jax.nn.sigmoid(queries @ Wg + bg)
        return context * gate @ Wo + bo

    def _L1_ffn_ref(hidden_states, W_fc, b_fc, A_fc, B_fc, W_proj, b_proj, A_proj, B_proj):
        import jax, jax.numpy as jnp
        import numpy as np
        BITS = 8
        LORA_RANK = 16
        LORA_ALPHA = 32
        SCALING = LORA_ALPHA / LORA_RANK

        def fake_quant_weight(w, bits=BITS):
            qmax = 2.0 ** (bits - 1) - 1
            scale = jnp.max(jnp.abs(w)) / qmax
            wq = jnp.clip(jnp.round(w / scale), -qmax - 1, qmax) * scale
            return w + jax.lax.stop_gradient(wq - w)

        def qat_lora_linear(x, W, b, A, B):
            Wq = fake_quant_weight(W)
            base = jnp.einsum('bsi,oi->bso', x, Wq) + b
            lora = jnp.einsum('bsr,or->bso', jnp.einsum('bsi,ri->bsr', x, A), B)
            return base + SCALING * lora
        h = qat_lora_linear(hidden_states, W_fc, b_fc, A_fc, B_fc)
        h = jax.nn.gelu(h, approximate=False)
        h = qat_lora_linear(h, W_proj, b_proj, A_proj, B_proj)
        return h

    def _L2_xattn_ref(x, latents, ln_m_w, ln_m_b, ln_l_w, ln_l_b, Wq, Wkv, Wout):
        import jax, jax.numpy as jnp
        import numpy as np
        DIM = 128
        HEADS = 8
        DIM_HEAD = 64
        INNER = HEADS * DIM_HEAD
        EPS = 1e-05

        def layernorm(x, w, b):
            mu = jnp.mean(x, axis=-1, keepdims=True)
            var = jnp.var(x, axis=-1, keepdims=True)
            return (x - mu) * jax.lax.rsqrt(var + EPS) * w + b
        scale = DIM_HEAD ** (-0.5)
        xn = layernorm(x, ln_m_w, ln_m_b)
        ln = layernorm(latents, ln_l_w, ln_l_b)
        b = xn.shape[0]
        q = ln @ Wq
        kv_input = jnp.concatenate([xn, ln], axis=-2)
        kv = kv_input @ Wkv
        k, v = jnp.split(kv, 2, axis=-1)

        def to_heads(t):
            return t.reshape(b, t.shape[1], HEADS, DIM_HEAD).transpose(0, 2, 1, 3)
        q, k, v = (to_heads(q) * scale, to_heads(k), to_heads(v))
        sim = jnp.einsum('bhid,bhjd->bhij', q, k)
        attn = jax.nn.softmax(sim, axis=-1)
        out = jnp.einsum('bhij,bhjd->bhid', attn, v)
        out = out.transpose(0, 2, 1, 3).reshape(b, out.shape[2], INNER)
        return out @ Wout

    def _L2_ffn_ref(x, gate_w, w1, b1, w2, b2, w3, b3, sw1, sw2, sw3):
        import jax, jax.numpy as jnp
        import numpy as np
        D = 128
        H = 128
        E = 8
        K = 2
        I = 2 * 128
        ROUTE_SCALE = 1.0
        B, S, _ = x.shape
        xt = x.reshape(-1, D)
        logits = xt @ gate_w.T
        scores = jax.nn.softmax(logits.astype(jnp.float32), axis=-1)
        top_vals, idx = jax.lax.top_k(scores, K)
        weights = jnp.take_along_axis(scores, idx, axis=1).astype(x.dtype) * ROUTE_SCALE
        xs = xt[:, None, :] * weights[:, :, None]
        y = jnp.zeros_like(xt)
        for e in range(E):
            mask = (idx == e).astype(x.dtype)
            h = jax.nn.silu(jnp.einsum('tkd,hd->tkh', xs, w1[e]) + b1[e])
            x2 = jnp.einsum('tkh,dh->tkd', h, w2[e]) + b2[e]
            x3 = jnp.einsum('tkd,hd->tkh', xs, w3[e]) + b3[e]
            y = y + jnp.sum(x2 * x3 * mask[:, :, None], axis=1)
        z = jax.nn.silu(xt @ sw1.T) * (xt @ sw2.T) @ sw3.T
        return (y + z).reshape(B, S, D)

    def _L3_xattn_ref(q, k, v, in_proj_weight, in_proj_bias, out_w, out_b):
        import jax, jax.numpy as jnp
        import numpy as np
        EMBED_DIM = 128
        NUM_HEADS = 16
        HEAD_DIM = EMBED_DIM // NUM_HEADS
        B, T, S = (2, 256, 256)
        H, D = (NUM_HEADS, HEAD_DIM)
        w_q, w_k, w_v = jnp.split(in_proj_weight, 3, axis=0)
        b_q, b_k, b_v = jnp.split(in_proj_bias, 3, axis=0)
        qp = q @ w_q.T + b_q
        kp = k @ w_k.T + b_k
        vp = v @ w_v.T + b_v
        bsz, t, _ = qp.shape
        s = kp.shape[1]
        qh = qp.reshape(bsz, t, H, D).transpose(0, 2, 1, 3)
        kh = kp.reshape(bsz, s, H, D).transpose(0, 2, 1, 3)
        vh = vp.reshape(bsz, s, H, D).transpose(0, 2, 1, 3)
        scale = D ** (-0.5)
        attn = jnp.einsum('bhtd,bhsd->bhts', qh, kh) * scale
        attn = jax.nn.softmax(attn, axis=-1)
        ctx = jnp.einsum('bhts,bhsd->bhtd', attn, vh)
        ctx = ctx.transpose(0, 2, 1, 3).reshape(bsz, t, H * D)
        out = ctx @ out_w.T + out_b
        return out

    def _L3_ffn_ref(hidden_states, gate_w, gate_bias, eg_w, eu_w, ed_w, sg_w, su_w, sd_w):
        import jax, jax.numpy as jnp
        import numpy as np
        from jax import lax
        HIDDEN = 128
        INTER = 64
        E = 64
        K = 6
        G = 8
        TG = 4
        NSH = 2
        ISH = INTER * NSH

        def _moe_forward(hidden_states, gate_w, gate_bias, eg_w, eu_w, ed_w, sg_w, su_w, sd_w):
            B, S, H = hidden_states.shape
            x = hidden_states.reshape(-1, H)
            T = x.shape[0]
            shared = jax.nn.silu(x @ sg_w.T) * (x @ su_w.T) @ sd_w.T
            logits = x @ gate_w.T
            scores = jax.nn.sigmoid(logits) + gate_bias
            group_scores = scores.reshape(T, G, E // G).max(axis=-1)
            _, sel_groups = lax.top_k(group_scores, TG)
            group_mask = jnp.zeros((T, G), scores.dtype).at[jnp.arange(T)[:, None], sel_groups].set(1.0)
            mask = jnp.repeat(group_mask, E // G, axis=1)
            masked_scores = scores * mask
            topk_w, topk_i = lax.top_k(masked_scores, K)
            topk_w = topk_w / (topk_w.sum(axis=-1, keepdims=True) + 1e-08)
            comb = jnp.zeros((T, E), x.dtype).at[jnp.arange(T)[:, None], topk_i].add(topk_w)
            h = jax.nn.silu(jnp.einsum('th,eih->eti', x, eg_w)) * jnp.einsum('th,eih->eti', x, eu_w)
            routed = jnp.einsum('eti,ehi,te->th', h, ed_w, comb)
            return (shared + routed).reshape(B, S, H)
        return _moe_forward(hidden_states, gate_w, gate_bias, eg_w, eu_w, ed_w, sg_w, su_w, sd_w)
    x = x + jnp.tanh(g_xattn[0]) * _L0_xattn_ref(_layernorm(x, axis=-1), ctx_1024, mask_BxS2_bk0, L0_xattn_Wq, L0_xattn_bq, L0_xattn_Wk, L0_xattn_bk, L0_xattn_Wv, L0_xattn_bv, L0_xattn_Wo, L0_xattn_bo)
    x = x + jnp.tanh(g_ffn[0]) * _L0_ffn_ref(_layernorm(x, axis=-1), L0_ffn_router_weight, L0_ffn_e_bias, L0_ffn_gate_w, L0_ffn_up_w, L0_ffn_down_w, L0_ffn_sh_gate_w, L0_ffn_sh_up_w, L0_ffn_sh_down_w)
    x = x + jnp.tanh(g_xattn[1]) * _L1_xattn_ref(_layernorm(x, axis=-1), ctx_1024, ctx_1024, L1_xattn_Wq, L1_xattn_bq, L1_xattn_Wk, L1_xattn_bk, L1_xattn_Wv, L1_xattn_bv, L1_xattn_Wg, L1_xattn_bg, L1_xattn_Wo, L1_xattn_bo)
    x = x + jnp.tanh(g_ffn[1]) * _L1_ffn_ref(_layernorm(x, axis=-1), L1_ffn_W_fc, L1_ffn_b_fc, L1_ffn_A_fc, L1_ffn_B_fc, L1_ffn_W_proj, L1_ffn_b_proj, L1_ffn_A_proj, L1_ffn_B_proj)
    x = x + jnp.tanh(g_xattn[2]) * _L2_xattn_ref(ctx_1024, _layernorm(x, axis=-1), L2_xattn_ln_m_w, L2_xattn_ln_m_b, L2_xattn_ln_l_w, L2_xattn_ln_l_b, L2_xattn_Wq, L2_xattn_Wkv, L2_xattn_Wout)
    x = x + jnp.tanh(g_ffn[2]) * _L2_ffn_ref(_layernorm(x, axis=-1), L2_ffn_gate_w, L2_ffn_w1, L2_ffn_b1, L2_ffn_w2, L2_ffn_b2, L2_ffn_w3, L2_ffn_b3, L2_ffn_sw1, L2_ffn_sw2, L2_ffn_sw3)
    x = x + jnp.tanh(g_xattn[3]) * _L3_xattn_ref(_layernorm(x, axis=-1), ctx_1024, ctx_1024, L3_xattn_in_proj_weight, L3_xattn_in_proj_bias, L3_xattn_out_w, L3_xattn_out_b)
    x = x + jnp.tanh(g_ffn[3]) * _L3_ffn_ref(_layernorm(x, axis=-1), L3_ffn_gate_w, L3_ffn_gate_bias, L3_ffn_eg_w, L3_ffn_eu_w, L3_ffn_ed_w, L3_ffn_sg_w, L3_ffn_su_w, L3_ffn_sd_w)
    return x

_drawn_inputs = setup_inputs


def setup_inputs(seed=0):
    import zlib

    import numpy as np

    out = dict(_drawn_inputs(seed))
    spreads = {'L0_xattn_bq': (0.0, 0.8),
     'L0_xattn_bk': (0.0, 2.0),
     'L0_xattn_bv': (0.0, 0.307),
     'L0_xattn_bo': (0.0, 0.1),
     'L0_ffn_e_bias': (0.0, 0.8),
     'L1_xattn_bq': (0.0, 0.1),
     'L1_xattn_bk': (0.0, 2.0),
     'L1_xattn_bv': (0.0, 0.405),
     'L1_xattn_bg': (0.0, 0.411),
     'L1_xattn_bo': (0.0, 0.1),
     'L1_ffn_b_fc': (0.0, 0.271),
     'L1_ffn_B_fc': (0.0, 0.1),
     'L1_ffn_b_proj': (0.0, 0.1),
     'L1_ffn_B_proj': (0.0, 0.1),
     'L2_xattn_ln_m_w': (1.0, 0.6),
     'L2_xattn_ln_m_b': (0.0, 0.344),
     'L2_xattn_ln_l_w': (1.0, 0.554),
     'L2_xattn_ln_l_b': (0.0, 0.3),
     'L3_xattn_in_proj_bias': (0.0, 0.291),
     'L3_xattn_out_b': (0.0, 0.296),
     'L3_ffn_gate_bias': (0.0, 0.8)}
    factors = {'L0_xattn_Wq': 8.0,
     'L0_xattn_Wk': 8.0,
     'L0_ffn_router_weight': 8.0,
     'L0_ffn_gate_w': 8.0,
     'L0_ffn_up_w': 8.0,
     'L0_ffn_down_w': 8.0,
     'L0_ffn_sh_gate_w': 8.0,
     'L0_ffn_sh_up_w': 8.0,
     'L0_ffn_sh_down_w': 8.0,
     'L2_ffn_b1': 60.562,
     'L2_ffn_b2': 40.767,
     'L2_ffn_b3': 54.082,
     'L3_ffn_gate_w': 8.0,
     'L3_ffn_eg_w': 8.0,
     'L3_ffn_eu_w': 8.0,
     'L3_ffn_ed_w': 8.0,
     'L3_ffn_sg_w': 8.0,
     'L3_ffn_su_w': 8.0,
     'L3_ffn_sd_w': 8.0}
    for name, (base, spread) in spreads.items():
        noise = np.random.default_rng([zlib.crc32(name.encode()), seed]).standard_normal(out[name].shape)
        drawn = base * np.exp(spread * noise) if base else spread * noise
        out[name] = jnp.asarray(drawn.astype(out[name].dtype))
    for name, factor in factors.items():
        out[name] = (out[name] * factor).astype(out[name].dtype)
    return out
```

```python
import concourse.bass as bass
from concourse import mybir
from contextlib import ExitStack



def flamingo_kernel(nc, a, out, stages=8):
    f32, bf16 = mybir.dt.float32, mybir.dt.bfloat16
    ACT, ALU, X = mybir.ActivationFunctionType, mybir.AluOpType, mybir.AxisListType.X
    ds = bass.ds

    P, T, B = 128, 1024, 8
    HALF = T // 2
    BH = B // 2
    HEADS, HD = 16, 8
    QUADS = HEADS // 4
    SPLIT = 3
    PAIRS = SPLIT * SPLIT
    MASK_ROW = 96
    EPS = 1e-5
    GELU = ACT.Gelu
    REDUCE_MAX = bass.bass_isa.ReduceOp.max

    ctx = ExitStack()
    with ctx:
        def sb(name, shape, dt=f32):
            return ctx.enter_context(nc.sbuf_tensor(name, shape, dt))

        def signal(name):
            return ctx.enter_context(nc.semaphore(name))

        x = sb("x", [P, 2, HALF])
        context = sb("context", [P, 2, HALF])
        xn = sb("xn", [P, 2, HALF])
        latents = sb("latents", [P, B, 2, P])
        ident = sb("ident", [P, P])
        ident_bf = sb("ident_bf", [P, P], bf16)
        spread_sum = sb("spread_sum", [P, P])
        mean_w = sb("mean_w", [P, P])
        zeros_bf = sb("zeros_bf", [P, HALF], bf16)
        earlier4 = sb("earlier4", [P, 4, 4])
        earlier8 = sb("earlier8", [P, 8, 8])
        N0, N1, N2, N3 = (a[f"mats{n}"].shape[1] for n in range(4))
        mats0, mats1, mats2, mats3 = (sb(f"mats{n}", [P, w]) for n, w in enumerate((N0, N1, N2, N3)))
        lora = sb("lora", [16, 1280])
        cols = sb("cols", [P, a["cols"].shape[1]])
        gates = sb("gates", [P, 8])
        tg = sb("tg", [P, 8])
        tgb = sb("tgb", [P, 8])
        route_bias = sb("route_bias", [P, 80])
        mask_words = sb("mask_words", [HEADS, T // 4], mybir.dt.int32)
        mask_u8 = mask_words[:, :].bitcast(mybir.dt.uint8)
        latent_rows = latents[0:HEADS, :, :, :].rearrange("p b s t -> p (b s t)")
        mask_neg = latent_rows[:, 0:512].bitcast(bf16)
        ones16 = latent_rows[:, 512:1024].bitcast(bf16)
        arena = sb("arena", [P, 20480])
        stack_q = arena[:, 0:8192].bitcast(bf16).rearrange("p (h t) -> p h t", h=HEADS)
        stack_k = arena[:, 8192:16384].bitcast(bf16).rearrange("p (h t) -> p h t", h=HEADS)
        q1 = arena[:, 0:1024].rearrange("p (c t) -> p c t", c=2)
        k1 = arena[:, 1024:2048].rearrange("p (c t) -> p c t", c=2)
        gate1 = arena[:, 2048:3072].rearrange("p (c t) -> p c t", c=2)
        v1 = arena[:, 3072:4096].rearrange("p (b d) -> p b d", b=B)
        k2 = arena[:, 0:8192].rearrange("p (m b k) -> p m b k", m=4, b=B)
        q2 = arena[:, 8192:12288].rearrange("p (m t) -> p m t", m=4)
        v2 = arena[:, 12288:20480].rearrange("p (t d) -> p t d", t=2 * B)
        rt = arena[:, 16384:16384 + 14 * 288].rearrange("p (n v) -> p n v", n=14)
        v_tok = sb("v_tok", [P, B, P])
        head_v = sb("head_v", [P, 2304])
        v_slots = head_v[:, :].rearrange("p (g c) -> p g c", g=2)
        v_slots2 = head_v[:, 0:2048].rearrange("p (t h c) -> p t h c", t=2, h=8)
        q_slot = sb("q_slot", [P, 4, 2, P])
        cen = sb("cen", [P, 2, HALF])
        sq = sb("sq", [P, 2, HALF])
        std = sb("std", [P, 2, HALF])
        wa, wb, wc = (sb(n, [P, 2, HALF]) for n in ("wa", "wb", "wc"))
        pieces = sb("pieces", [P, 2, SPLIT, HALF], bf16)
        row_max = sb("row_max", [P, 2, 4])
        o_sb = sb("o_sb", [P, 4, P])
        o_inv = sb("o_inv", [P, 2, P])
        upd = sb("upd", [P, HALF])
        ring = sb("ring", [P, 4, 384])
        ring_sel = sb("ring_sel", [P, 4, 2, P], bf16)
        select2 = sb("select2", [P, 8, 2, P], bf16)
        comb_pieces = sb("comb_pieces", [P, 8, 256], bf16)
        comb_t = sb("comb_t", [P, 2, T], bf16)
        bank = [ctx.enter_context(nc.psum_tensor(f"bank{n}", [P, 512], f32)) for n in range(8)]

        in_ctx, in_x, in_consts, in_mats1, in_mats2, in_mats3 = (
            signal(n) for n in ("in_ctx", "in_x", "in_consts", "in_mats1", "in_mats2", "in_mats3"))
        prepared = signal("prepared")
        pool_ready = signal("pool_ready")
        tg_ready, tgb_ready = signal("tg_ready"), signal("tgb_ready")
        x_updated = signal("x_updated")
        update_ready = signal("update_ready")
        out_stored = signal("out_stored")
        ln_mean, ln_cen, ln_sq, ln_var, ln_std, ln_inv, ln_scaled, ln_out = (
            signal(n) for n in ("ln_mean", "ln_cen", "ln_sq", "ln_var", "ln_std", "ln_inv",
                                "ln_scaled", "ln_out"))
        dve_chain = signal("dve_chain")
        act_chain = signal("act_chain")

        K0B, Q0B, V0B, O0B = 0, 1, 2, 4
        K3B, Q3B, V3B, O3B = 5, 6, 7, 9
        Q1B, K1B, V1B, G1B, O1B, FCB, PROJB = 10, 11, 12, 13, 14, 15, 19
        LNMW, LNMB, LNLW, LNLB, B1, B2, B3 = 20, 21, 22, 23, 24, 32, 40

        def col(n):
            return cols[:, n:n + 1]

        PER_STAGE = [8, 2, 2, 2, 8, 2, 8, 2]

        def x_count(s, c):
            return sum(PER_STAGE[:s]) + PER_STAGE[s] * (c + 1) // 2

        def whole(t):
            return lambda c: t[:, c, :]

        def latent_half(which):
            return lambda c: latents[:, BH * c:BH * c + BH, which, :]

        NORMS = []
        NORM_OF = {}
        for s in range(8):
            NORM_OF[s] = [len(NORMS)]
            NORMS.append((whole(x), whole(xn), None, ("x", s)))
            if s == 4:
                NORM_OF[s] += [len(NORMS), len(NORMS) + 1]
                NORMS.append((whole(context), latent_half(0), (LNMW, LNMB), ("ctx", s)))
                NORMS.append((whole(xn), latent_half(1), (LNLW, LNLB), ("xn", s)))

        def norm_bank(c):
            return bank[c]

        A_STAGE = [0, 6]
        A_MATS = [mats0, mats3]
        A_BIAS = [(K0B, Q0B, V0B, O0B), (K3B, Q3B, V3B, O3B)]
        a_proj, a_full, a_first, a_rest, a_piece2, a_split = (
            signal(n) for n in ("a_proj", "a_full", "a_first", "a_rest", "a_piece2", "a_split"))
        a_stacked = [signal("a_stacked0"), signal("a_stacked1")]
        a_mask = signal("a_mask")
        a_vproj, a_vtok = signal("a_vproj"), signal("a_vtok")
        a_s, a_max, a_sub, a_exp, a_tr, a_ev, a_pv = (
            signal(n) for n in ("a_scores", "a_max", "a_shifted", "a_exp", "a_transposed",
                                "a_evacuated", "a_pv"))
        a_slots, a_ocopy, a_z, a_inv, a_norm, a_y = (
            signal(n) for n in ("a_slots", "a_ocopy", "a_sums", "a_inverse", "a_normed", "a_y"))
        UNITS = B * QUADS
        SCALE_A = HD ** -0.5

        c_proj, c_slot, c_rec, c_inv = (signal(n) for n in ("c_proj", "c_qslot", "c_rec", "c_inv"))
        c_kq = [signal("c_evac0"), signal("c_evac1")]
        o_bias = signal("o_bias")

        w_in = [signal(f"w_in{s}") for s in range(4)]
        m_logit, m_score, m_comb, m_combT, m_combE = (
            signal(n) for n in ("m_logit", "m_score", "m_comb", "m_comb_t", "m_comb_evac"))
        m_shift = signal("m_shift")
        m_g, m_u, m_cb, m_silu, m_t, m_h, m_down, m_zero = (
            signal(n) for n in ("m_gate", "m_up", "m_weight", "m_silu", "m_prod", "m_hidden", "m_down",
                                "m_zero"))
        MOE = [
            dict(stage=1, E=16, G=4, TG=2, K=4, KT=1, mats=mats0, at=5 * P, bias=0, tri=earlier4),
            dict(stage=7, E=64, G=8, TG=4, K=6, KT=2, mats=mats3, at=5 * P, bias=16, tri=earlier8),
        ]
        for n, m in enumerate(MOE):
            m["n"] = n
            m["pairs"] = m["E"] // 2
            m["units"] = 2 * (m["pairs"] + 1)
            m["u0"] = MOE[0]["units"] if n else 0

        def fills2(e):
            before = sum(1 for q in range(MOE[0]["pairs"] + 1) if (q + 3) % 4 == e % 4)
            return 32 * before + 16 * (e // 4 + 1)

        def moe_units_until(n):
            return sum(m["units"] for m in MOE[:n])

        b_proj, b_evac, b_v, b_vev, b_s, b_p, b_tr, b_pt, b_pv, b_ctx, b_y = (
            signal(n) for n in ("b_proj", "b_evac", "b_v", "b_vev", "b_scores", "b_probs", "b_tr",
                                "b_pt", "b_pv", "b_ctx", "b_y"))
        d_lora, d_up, d_act, d_down, d_rowmax, d_max, d_w = (
            signal(n) for n in ("d_lora", "d_up", "d_act", "d_down", "d_rowmax", "d_max", "d_w"))
        w_max = sb("w_max", [P, 4])
        e_wb, e_xs, e_h1, e_x3, e_mk, e_h, e_x3b, e_u, e_x2, e_v, e_y, e_z, e_sg, e_sh, e_zd = (
            signal(n) for n in ("e_wb", "e_xs", "e_h1", "e_x3", "e_mk", "e_h", "e_x3b", "e_u", "e_x2",
                                "e_v", "e_y", "e_z", "e_sg", "e_sh", "e_zdown"))
        b_e, b_n = signal("b_exp"), signal("b_probs_normed")
        c_half = signal("c_half")
        eps_col = sb("eps_col", [P, 1])
        w_stat = sb("w_stat", [P, 6])
        ROUND = 1.5 * 2.0 ** 23

        def bank2(n):
            return bank[2 + n % 6][:, :]

        def product2(n):
            c, k = n // 20, n % 20
            if k < 8:
                m, g = k // 2, k % 2
                return k2[:, m, BH * c + 2 * g:BH * c + 2 * g + 2, :], 1.0
            if k < 12:
                return q2[:, k - 8, c * HALF:c * HALF + HALF], 64 ** -0.5
            return v2[:, 8 * c + k - 12, :], 1.0

        def hidden1(n):
            return (wa if n % 4 < 2 else wb)[:, n % 2, :]

        block = ctx.enter_context(nc.Block())

        @block.sync
        def _(sp):
            def load(dst, src, done):
                sp.dma_start(dst, src).then_inc(done, 16)

            halves = "p (c t) -> p c t"
            load(mats0[:, :], a["mats0"], in_ctx)
            load(context[:, :, :], a["ctx_t"].rearrange(halves, c=2), in_ctx)
            load(cols[:, :], a["cols"], in_ctx)
            load(x[:, :, :], a["x_t"].rearrange(halves, c=2), in_x)
            load(mask_words[:, :], a["mask"], in_x)
            load(gates[:, :], a["gates"], in_x)
            load(ident[:, :], a["ident"], in_consts)
            load(ident_bf[:, :], a["ident_bf"], in_consts)
            load(spread_sum[:, :], a["spread_sum"], in_consts)
            load(earlier4[:, :, :], a["earlier4"].rearrange("p (i j) -> p i j", i=4), in_consts)
            load(earlier8[:, :, :], a["earlier8"].rearrange("p (i j) -> p i j", i=8), in_consts)
            load(route_bias[:, :], a["route_bias"], in_consts)

            def stack(inst, k):
                n = 4 * inst + k
                sp.wait_ge(a_split, n + 1)
                half = k % 2
                dst = stack_k if k < 2 else stack_q
                for block_ in range(PAIRS):
                    piece = block_ % SPLIT if k < 2 else block_ // SPLIT
                    sp.dma_start(dst[HD * block_:HD * block_ + HD, :, half * HALF:half * HALF + HALF],
                                 pieces[:, n % 2, piece, :]).then_inc(a_stacked[n % 2], 16)

            def fill(m, q, slot):
                w = a["experts0" if m["n"] == 0 else "experts3"]
                s = a["select0" if m["n"] == 0 else "select3"]
                kt = m["KT"]
                sp.dma_start(ring[:, slot, :], w[q]).then_inc(w_in[slot], 16)
                sp.dma_start(ring_sel[:, slot, 0:kt, :], s[q]).then_inc(w_in[slot], 16)

            def fill_dyn(m, q0, j, slot):
                w = a["experts0" if m["n"] == 0 else "experts3"]
                s = a["select0" if m["n"] == 0 else "select3"]
                kt = m["KT"]
                q = q0 + j
                sp.dma_start(ring[:, slot, :], w[ds(q, 1), :, :].squeeze(0)).then_inc(w_in[slot], 16)
                sp.dma_start(ring_sel[:, slot, 0:kt, :],
                             s[ds(q, 1), :, :, :].squeeze(0)).then_inc(w_in[slot], 16)

            def moe_first(n):
                for q in range(4):
                    fill(MOE[n], q, (q + 3) % 4)

            def moe_rest(n):
                m, u0 = MOE[n], moe_units_until(n)
                groups = m["pairs"] // 4
                with sp.Fori(1, groups) as it:
                    for j in range(4):
                        sp.wait_ge(m_down, u0 + 8 * it + 2 * j - 6)
                        fill_dyn(m, 4 * it, j, (j + 3) % 4)
                q = m["pairs"]
                sp.wait_ge(m_down, u0 + 2 * (q - 4) + 2)
                fill(m, q, (q + 3) % 4)

            sp.wait_ge(a_mask, 2)
            sp.wait_ge(pool_ready, 1)
            sp.wait_ge(prepared, 3)
            sp.dma_start(stack_k[MASK_ROW:MASK_ROW + 1, :, :], mask_neg).then_inc(in_x, 16)
            sp.dma_start(stack_q[MASK_ROW:MASK_ROW + 1, :, :], ones16).then_inc(in_x, 16)
            for k in range(4):
                stack(0, k)
            moe_first(0)
            load(mats1[:, :], a["mats1"], in_mats1)
            load(lora[:, :], a["lora"], in_mats1)
            load(mats2[:, :], a["mats2"], in_mats2)
            load(select2[:, :, :, :], a["select2"], in_mats2)
            load(mats3[:, :], a["mats3"], in_mats3)
            if stages > 1:
                moe_rest(0)
            if stages > 5:
                sp.wait_ge(m_down, MOE[0]["units"])
                for e in range(4):
                    sp.dma_start(ring[:, e, :], a["experts2"][e]).then_inc(w_in[e], 16)
                for e in range(4, 8):
                    sp.wait_ge(e_x2, 2 * (e - 4) + 2)
                    sp.dma_start(ring[:, e - 4, :], a["experts2"][e]).then_inc(w_in[e - 4], 16)
            if stages > 6:
                sp.wait_ge(pool_ready, 6)
                sp.wait_ge(prepared, 5)
                for k in range(4):
                    stack(1, k)
            if stages > 7:
                sp.wait_ge(e_x2, 16)
                moe_first(1)
                moe_rest(1)
            for c in range(2):
                sp.wait_ge(x_updated, x_count(stages - 1, c))
                sp.dma_start(out[:, c * HALF:c * HALF + HALF], x[:, c, :]).then_inc(out_stored, 16)
            sp.wait_ge(out_stored, 32)

        @block.gpsimd
        def _(pool):
            def zero_stack():
                nc.gpsimd.memset(arena[64:128, 8192:16384], 0.0).then_inc(pool_ready, 1)

            def ones_around_v(inst):
                nc.gpsimd.memset(head_v[:, :], 0.0).then_inc(pool_ready, 1)
                pool.wait_ge(pool_ready, 2)
                spread = v_slots[:, :, 0:1152].rearrange("p g (h r) -> p g h r", r=144)
                nc.gpsimd.memset(spread[:, :, :, HD:16], 1.0).then_inc(pool_ready, 1)

            zero_stack()
            pool.wait_ge(pool_ready, 1)
            ones_around_v(0)

            def add_update(s, k, c, lo, width, n):
                pool.wait_ge(update_ready, n + 1)
                dst = x[:, c, lo:lo + width] if isinstance(lo, int) else x[:, c, ds(lo, width)]
                nc.gpsimd.tensor_tensor(dst, dst, upd[:, 0:width], ALU.add).then_inc(x_updated, 1)

            def attn_slots(inst, b):
                u0 = UNITS * (inst if inst < 2 else 0)
                spread = v_slots[:, :, 0:1152].rearrange("p g (h r) -> p g h r", r=144)
                src = v_tok[:, b, :] if isinstance(b, int) else v_tok[:, ds(b, 1), :].squeeze(1)
                nc.gpsimd.tensor_copy(spread[:, :, :, 0:HD],
                                      src.rearrange("p (g h d) -> p g h d", g=2, d=HD)).then_inc(a_slots, 1)

            def attn(inst, base_pv, base_slots, before):
                pool.wait_ge(a_vtok, 2 * inst + 2)
                attn_slots(inst, 0)

                def batch(b, last):
                    if not last:
                        pool.wait_ge(a_pv, base_pv + 4 * b + 4)
                        attn_slots(inst, b + 1)
                    pool.wait_ge(update_ready, before + b + 1)
                    xs = x[:, :, :].rearrange("p c t -> p (c t)")
                    dst = xs[:, ds(b * P, P)]
                    nc.gpsimd.tensor_tensor(dst, dst, upd[:, 0:P], ALU.add).then_inc(x_updated, 1)
                with pool.Fori(0, B - 1) as b:
                    batch(b, False)
                batch(B - 1, True)

            pool.wait_ge(in_x, 48)
            pool.wait_ge(pool_ready, 3)
            attn(0, 0, 0, 0)
            n = 8
            if stages > 1:
                for c in range(2):
                    add_update(1, 0, c, 0, HALF, n)
                    n += 1
            if stages > 2:
                for c in range(2):
                    add_update(2, 0, c, 0, HALF, n)
                    n += 1
            if stages > 3:
                pool.wait_ge(d_rowmax, 2)
                nc.gpsimd.partition_all_reduce(w_max[:, 2:4], w_max[:, 0:2], P, REDUCE_MAX).then_inc(d_max, 1)
                for c in range(2):
                    add_update(3, 0, c, 0, HALF, n)
                    n += 1
            if stages > 4:
                nc.gpsimd.memset(q_slot[:, :, :, :], 0.0).then_inc(pool_ready, 1)
                pool.wait_ge(a_pv, UNITS)
                nc.gpsimd.memset(head_v[:, :], 1.0).then_inc(pool_ready, 1)

                def v_slot(b):
                    v = v2[:, ds(2 * b, 2), :].rearrange("p t (h d) -> p t h d", d=64)
                    nc.gpsimd.tensor_copy(v_slots2[:, :, 0:8:2, 0:64], v[:, :, 0:8:2, :])\
                        .then_inc(a_slots, 1)
                    nc.gpsimd.tensor_copy(v_slots2[:, :, 1:8:2, 64:128], v[:, :, 1:8:2, :])\
                        .then_inc(a_slots, 1)
                pool.wait_ge(pool_ready, 5)
                for k in range(2):
                    pool.wait_ge(c_kq[k], 20)
                v_slot(0)

                def batch2(b, last):
                    if not last:
                        pool.wait_ge(a_pv, UNITS + 4 * b + 4)
                        v_slot(b + 1)
                    pool.wait_ge(update_ready, 14 + b + 1)
                    xs = x[:, :, :].rearrange("p c t -> p (c t)")
                    dst = xs[:, ds(b * P, P)]
                    nc.gpsimd.tensor_tensor(dst, dst, upd[:, 0:P], ALU.add).then_inc(x_updated, 1)
                with pool.Fori(0, B - 1) as b:
                    batch2(b, False)
                batch2(B - 1, True)
                n += 8
            if stages > 5:
                pool.wait_ge(a_pv, 2 * UNITS)
                pool.wait_ge(x_updated, n)
                zero_stack()
                pool.wait_ge(pool_ready, 6)
                for e in range(8):
                    for c in range(2):
                        pool.wait_ge(e_v, 2 * e + c + 1)
                        if e == 0:
                            pool.wait_ge(e_z, 2)
                        if e > 0:
                            pool.wait_ge(e_y, 2 * (e - 1) + c + 1)
                        nc.gpsimd.tensor_tensor(cen[:, c, :], cen[:, c, :], wc[:, c, :], ALU.add)\
                            .then_inc(e_y, 1)
                for c in range(2):
                    add_update(5, 0, c, 0, HALF, n)
                    n += 1
            if stages > 6:
                nc.gpsimd.memset(head_v[:, :], 0.0).then_inc(pool_ready, 1)
                pool.wait_ge(pool_ready, 7)
                spread = v_slots[:, :, 0:1152].rearrange("p g (h r) -> p g h r", r=144)
                nc.gpsimd.memset(spread[:, :, :, HD:16], 1.0).then_inc(pool_ready, 1)
                pool.wait_ge(pool_ready, 8)
                attn(1, 2 * UNITS, 0, n)
                n += 8
            if stages > 7:
                for c in range(2):
                    add_update(7, 0, c, 0, HALF, n)
                    n += 1

        @block.tensor
        def _(pe):
            mm = nc.tensor.matmul

            def norm_stats(i, c, last_wait=None):
                src, dst, affine, (kind, s) = NORMS[i]
                if kind == "x" and s > 0:
                    pe.wait_ge(x_updated, x_count(s - 1, c))
                if kind == "x" and s == 0:
                    pe.wait_ge(in_x, 48)
                if kind == "xn":
                    pe.wait_ge(ln_out, 2 * NORM_OF[4][0] + c + 1)
                if i > 0:
                    pe.wait_ge(ln_std, 2 * (i - 1) + c + 1)
                mm(bank[c][:, :], mean_w[:, :], src(c), start=True, stop=True).then_inc(ln_mean, 1)

            def norm_var(i, c):
                pe.wait_ge(ln_sq, 2 * i + c + 1)
                mm(bank[c][:, :], mean_w[:, :], sq[:, c, :], start=True, stop=True).then_inc(ln_var, 1)

            def norm(i):
                for c in range(2):
                    norm_stats(i, c)
                for c in range(2):
                    norm_var(i, c)

            def prep(inst, k):
                n = 4 * inst + k
                w = A_MATS[inst][:, (0 if k < 2 else P):(P if k < 2 else 2 * P)]
                src = context if k < 2 else xn
                if k >= 2:
                    pe.wait_ge(ln_out, 2 * NORM_OF[A_STAGE[inst]][0] + k - 1)
                if n >= 2:
                    pe.wait_ge(a_first, n - 1)
                mm(bank[6 + k % 2][:, :], w, src[:, k % 2, :], start=True, stop=True).then_inc(a_proj, 1)

            def attn_v(inst):
                for c in range(2):
                    for j in range(BH):
                        last = mm(bank[4 + c][:, j * P:j * P + P], context[:, c, j * P:j * P + P],
                                  A_MATS[inst][:, 2 * P:3 * P], start=True, stop=True)
                    last.then_inc(a_vproj, 1)

            def units(base, bb, scores, probs_v, tail):
                def transposes(b, u):
                    pe.wait_ge(a_exp, base + 4 * b + u + 1)
                    if not (base == 0 and isinstance(b, int) and b == 0 and u < 2):
                        pe.wait_ge(a_ev, base + 4 * b + u - 1)
                    for j in range(4):
                        last = nc.tensor.transpose(bank[2 + u % 2][:, j * P:j * P + P],
                                                   wb[:, u % 2, j * P:j * P + P], ident[:, :])
                    last.then_inc(a_tr, 1)

                def batch(b, first, last):
                    for u in range(4):
                        if u < 2:
                            scores(b, u + 2)
                        elif not last:
                            scores(b + 1, u - 2)
                        transposes(b, u)
                        if u > 0:
                            probs_v(b, u - 1)
                        elif not first:
                            probs_v(b - 1, 3)
                        if not first:
                            tail(b - 1, u)
                scores(0, 0)
                scores(0, 1)
                batch(0, True, False)
                with pe.Fori(1, B - 1) as b:
                    batch(b, False, False)
                batch(B - 1, False, True)
                probs_v(B - 1, 3)
                for u in range(4):
                    tail(B - 1, u)

            def attn(inst):
                base, bb = (0, 0) if inst == 0 else (2 * UNITS, 3 * B)
                tb = B * inst
                w = A_MATS[inst]
                pe.wait_ge(a_stacked[0], 288 * (inst + 1))
                pe.wait_ge(a_stacked[1], 288 * (inst + 1))
                if inst == 0:
                    pe.wait_ge(in_x, 80)
                    pe.wait_ge(in_consts, 96)

                def scores(b, u):
                    if not (base == 0 and isinstance(b, int) and b == 0 and u < 2):
                        pe.wait_ge(a_sub, base + 4 * b + u - 1)
                    for j in range(4):
                        tok = ds(b * P, P)
                        last = mm(bank[u % 2][:, j * P:j * P + P], stack_q[:, 4 * u + j, tok],
                                  stack_k[:, 4 * u + j, tok], start=True, stop=True)
                    last.then_inc(a_s, 1)

                def probs_v(b, u):
                    pe.wait_ge(a_ev, base + 4 * b + u + 1)
                    if u == 0:
                        pe.wait_ge(a_slots, bb + b + 1)
                        if not (tb == 0 and isinstance(b, int) and b == 0):
                            pe.wait_ge(a_ocopy, tb + b)
                    g = u // 2
                    for j in range(4):
                        h = 4 * (u % 2) + j
                        last = mm(bank[4][:, g * P:g * P + P], v_slots[:, g, h * P:h * P + P],
                                  wc[:, u % 2, j * P:j * P + P], start=(h == 0), stop=(h == 7))
                    last.then_inc(a_pv, 1)

                def tail(b, u):
                    if u == 1:
                        pe.wait_ge(a_ocopy, tb + b + 1)
                        if not (tb == 0 and isinstance(b, int) and b == 0):
                            pe.wait_ge(update_ready, (0 if inst == 0 else x_count(5, 1)) + b)
                        mm(bank[6][:, 0:2 * P], spread_sum[:, :], o_sb[:, 0:2, :],
                           start=True, stop=True).then_inc(a_z, 1)
                    if u == 3:
                        pe.wait_ge(a_norm, tb + b + 1)
                        for g in range(2):
                            last = mm(bank[6][:, 2 * P:3 * P], w[:, (3 + g) * P:(4 + g) * P],
                                      o_sb[:, 2 + g, :], start=(g == 0), stop=(g == 1))
                        last.then_inc(a_y, 1)
                units(base, bb, scores, probs_v, tail)

            def bias_through_o(inst):
                vb = A_BIAS[inst][2]
                for g in range(2):
                    last = mm(bank[7][:, 0:1], A_MATS[inst][:, (3 + g) * P:(4 + g) * P],
                              col(vb + g), start=(g == 0), stop=(g == 1))
                last.then_inc(o_bias, 1)

            def moe(n):
                m = MOE[n]
                u0, kt = moe_units_until(n), m["KT"]
                for c in range(2):
                    pe.wait_ge(ln_out, 2 * NORM_OF[m["stage"]][0] + c + 1)
                    for j in range(BH):
                        last = mm(bank[4 + c][:, j * P:j * P + P], xn[:, c, j * P:j * P + P],
                                  m["mats"][:, m["at"]:m["at"] + P], start=True, stop=True)
                    last.then_inc(m_logit, 1)
                for c in range(2):
                    mm(bank[6 + c][:, :], zeros_bf[:, 0:P], zeros_bf[:, :], start=True, stop=False)

                def front(slot, c, weighed, fill_count):
                    pe.wait_ge(w_in[slot], fill_count)
                    mm(bank[c][:, :], ring[:, slot, 0:P], xn[:, c, :], start=True, stop=True)\
                        .then_inc(m_g, 1)
                    mm(bank[2 + c][:, :], ring[:, slot, P:2 * P], xn[:, c, :], start=True, stop=True)\
                        .then_inc(m_u, 1)
                    if weighed:
                        for k in range(kt):
                            last = mm(bank[4 + c][:, :], ring_sel[:, slot, k, :],
                                      comb_t[:, k, c * HALF:c * HALF + HALF],
                                      start=(k == 0), stop=(k == kt - 1))
                        last.then_inc(m_cb, 1)

                def down(slot, c, unit, stop=False):
                    pe.wait_ge(m_h, unit + 1)
                    mm(bank[6 + c][:, :], ring[:, slot, 2 * P:3 * P], wc[:, c, :],
                       start=False, stop=stop).then_inc(m_down, 1)

                def filled(slot, more):
                    before = 32 * sum(
                        1 for mm_ in MOE[:n] for q in range(mm_["pairs"] + 1) if (q + 3) % 4 == slot)
                    return before + (32 if n else 0) + 32 * more

                front(3, 0, False, filled(3, 1))
                front(3, 1, False, filled(3, 1))
                down(3, 0, u0)
                for c in range(2):
                    pe.wait_ge(m_comb, 4 * n + c + 1)
                    for k in range(kt):
                        for j in range(BH):
                            last = nc.tensor.transpose(
                                bank[4 + c][:, :].bitcast(bf16)[:, (k * BH + j) * P:(k * BH + j) * P + P],
                                comb_pieces[:, BH * c + j, k * P:k * P + P], ident_bf[:, :])
                    last.then_inc(m_combT, 1)
                pe.wait_ge(m_combE, 4 * n + 2)
                with pe.Fori(0, m["pairs"] // 4) as it:
                    for k in range(8):
                        slot, c = k // 2, k % 2
                        front(slot, c, True, filled(slot, 0) + 32 * it + (64 if slot == 3 else 32))
                        down((slot + 3) % 4 if c == 0 else slot, 1 - c, u0 + 8 * it + k + 1)
                mm(bank[6][:, :], zeros_bf[:, 0:P], zeros_bf[:, :], start=False, stop=True)\
                    .then_inc(m_zero, 1)
                down(3, 1, u0 + m["units"] - 1, stop=True)

            pe.wait_ge(in_ctx, 48)
            pe.wait_ge(prepared, 1)
            prep(0, 0)
            prep(0, 1)
            norm(0)
            attn_v(0)
            prep(0, 2)
            prep(0, 3)
            pe.wait_ge(a_vtok, 2)
            pe.wait_ge(a_first, 4)
            bias_through_o(0)
            attn(0)
            if stages > 1:
                norm(NORM_OF[1][0])
                moe(0)
            if stages > 2:
                w = mats1
                pe.wait_ge(in_mats1, 32)
                norm(NORM_OF[2][0])
                pe.wait_ge(x_updated, x_count(1, 1))
                for c in range(2):
                    mm(bank[2 + c][:, :], w[:, P:2 * P], context[:, c, :], start=True, stop=True)\
                        .then_inc(b_proj, 1)
                for c in range(2):
                    for j in range(BH):
                        last = mm(bank[4 + c][:, j * P:j * P + P], context[:, c, j * P:j * P + P],
                                  w[:, 2 * P:3 * P], start=True, stop=True)
                    last.then_inc(b_v, 1)
                for c in range(2):
                    pe.wait_ge(ln_out, 2 * NORM_OF[2][0] + c + 1)
                    mm(bank[6 + c][:, :], w[:, 0:P], xn[:, c, :], start=True, stop=True).then_inc(b_proj, 1)
                for c in range(2):
                    pe.wait_ge(b_evac, c + 1)
                    mm(bank[2 + c][:, :], w[:, 3 * P:4 * P], xn[:, c, :], start=True, stop=True)\
                        .then_inc(b_proj, 1)
                for c in range(2):
                    pe.wait_ge(b_evac, 3 + c)
                    for j in range(BH):
                        last = mm(bank[c][:, j * P:j * P + P], q1[:, c, j * P:j * P + P],
                                  k1[:, c, j * P:j * P + P], start=True, stop=True)
                    last.then_inc(b_s, 1)
                pe.wait_ge(b_vev, 2)
                for c in range(2):
                    pe.wait_ge(b_n, c + 1)
                    for j in range(BH):
                        last = nc.tensor.transpose(bank[4 + c][:, j * P:j * P + P],
                                                   wb[:, c, j * P:j * P + P], ident[:, :])
                    last.then_inc(b_tr, 1)
                for c in range(2):
                    pe.wait_ge(b_pt, c + 1)
                    for j in range(BH):
                        last = mm(bank[6 + c][:, j * P:j * P + P], v1[:, BH * c + j, :],
                                  wc[:, c, j * P:j * P + P], start=True, stop=True)
                    last.then_inc(b_pv, 1)
                for c in range(2):
                    pe.wait_ge(b_ctx, c + 1)
                    mm(bank[c][:, :], w[:, 4 * P:5 * P], wa[:, c, :], start=True, stop=True)\
                        .then_inc(b_y, 1)
            if stages > 3:
                for c in range(2):
                    pe.wait_ge(update_ready, 12)
                mm(bank[2][:, :], lora[:, 0:P], lora[:, P:5 * P], start=True, stop=True).then_inc(d_lora, 1)
                for j in range(4):
                    last = mm(bank[3][:, j * P:j * P + P], lora[:, 5 * P + j * P:5 * P + j * P + P],
                              lora[:, 9 * P:10 * P], start=True, stop=True)
                last.then_inc(d_lora, 1)
                norm(NORM_OF[3][0])
                pe.wait_ge(d_w, 2)
                for c in range(2):
                    pe.wait_ge(ln_out, 2 * NORM_OF[3][0] + c + 1)

                def up(m_):
                    f, c = m_ // 2, m_ % 2
                    if m_ >= 4:
                        pe.wait_ge(d_act, m_ - 3)
                    mm(bank[2 + m_ % 4][:, :], mats1[:, (5 + f) * P:(6 + f) * P], xn[:, c, :],
                       start=True, stop=True).then_inc(d_up, 1)

                up(0)
                up(1)
                for m_ in range(8):
                    f, c = m_ // 2, m_ % 2
                    if m_ + 2 < 8:
                        up(m_ + 2)
                    pe.wait_ge(d_act, m_ + 1)
                    mm(bank[6 + c][:, :], mats1[:, (9 + f) * P:(10 + f) * P], hidden1(m_),
                       start=(f == 0), stop=(f == 3)).then_inc(d_down, 1)
            if stages > 4:
                w = mats2
                pe.wait_ge(in_mats2, 32)
                i0, i1, i2 = NORM_OF[4]
                norm(i0)
                norm(i1)
                norm(i2)
                pe.wait_ge(update_ready, 14)
                n = 0

                def put(n):
                    if n >= 6:
                        pe.wait_ge(c_kq[n % 2], (n - 6) // 2 + 1)
                    return bank[2 + n % 6]
                flat = latents[:, :, :, :].rearrange("p b s t -> p (b s t)")
                for c in range(2):
                    pe.wait_ge(ln_out, 2 * i2 + c + 1)
                    for m_ in range(4):
                        for g in range(2):
                            gg = 2 * c + g
                            mm(put(n)[:, :], w[:, (4 + m_) * P:(5 + m_) * P],
                               flat[:, gg * 512:gg * 512 + 512], start=True, stop=True).then_inc(c_proj, 1)
                            n += 1
                    for m_ in range(4):
                        mm(put(n)[:, :], w[:, m_ * P:(m_ + 1) * P],
                           latents[:, BH * c:BH * c + BH, 1, :], start=True, stop=True)\
                            .then_inc(c_proj, 1)
                        n += 1
                    for t in range(8):
                        tile = 8 * c + t
                        mm(put(n)[:, :], flat[:, tile * P:tile * P + P], w[:, 8 * P:12 * P],
                           start=True, stop=True).then_inc(c_proj, 1)
                        n += 1
                for k in range(2):
                    pe.wait_ge(c_kq[k], 20)
                base, bb = UNITS, B

                def scores2(b, u):
                    if u == 0:
                        pe.wait_ge(c_slot, 2 * b + 2)
                    pe.wait_ge(a_sub, base + 4 * b + u - 1)
                    for j in range(2):
                        last = mm(bank[u % 2][:, j * 256:j * 256 + 256], q_slot[:, u, j, :],
                                  k2[:, u, ds(b, 1), :].squeeze(1), start=True, stop=True)
                    last.then_inc(a_s, 1)

                def probs_v2(b, u):
                    pe.wait_ge(a_ev, base + 4 * b + u + 1)
                    if u == 0:
                        pe.wait_ge(a_slots, B + 2 * b + 2)
                    if u % 2 == 0 and not (isinstance(b, int) and b == 0):
                        pe.wait_ge(c_inv, 2 * b + u // 2 - 1)
                    for j in range(2):
                        for t in range(2):
                            last = mm(bank[4 + u // 2][:, (2 * (u % 2) + j) * P:(2 * (u % 2) + j) * P + P],
                                      v_slots2[:, t, 2 * u + j, :],
                                      wc[:, u % 2, (2 * j + t) * P:(2 * j + t) * P + P],
                                      start=(t == 0), stop=(t == 1))
                    last.then_inc(a_pv, 1)

                def tail2(b, u):
                    if u == 2:
                        pe.wait_ge(c_inv, 2 * b + 2)
                        if not (isinstance(b, int) and b == 0):
                            pe.wait_ge(update_ready, 14 + b)
                        for g in range(4):
                            last = mm(bank[6][:, 0:P], w[:, (12 + g) * P:(13 + g) * P], o_sb[:, g, :],
                                      start=(g == 0), stop=(g == 3))
                        last.then_inc(a_y, 1)
                units(base, bb, scores2, probs_v2, tail2)
            if stages > 5:
                w = mats2
                norm(NORM_OF[5][0])
                for c in range(2):
                    pe.wait_ge(ln_out, 2 * NORM_OF[5][0] + c + 1)
                    for j in range(BH):
                        last = mm(bank[4 + c][:, j * P:j * P + P], xn[:, c, j * P:j * P + P],
                                  w[:, 16 * P:17 * P], start=True, stop=True)
                    last.then_inc(m_logit, 1)
                def shared_down(k):
                    f, c = k // 2, k % 2
                    pe.wait_ge(e_sh, k + 1)
                    mm(bank[6 + c][:, :], w[:, (21 + f) * P:(22 + f) * P], wc[:, c, :],
                       start=(f == 0), stop=(f == 1)).then_inc(e_zd, 1)
                for f in range(2):
                    for c in range(2):
                        k = 2 * f + c
                        if k >= 2:
                            pe.wait_ge(e_sh, k - 1)
                        mm(bank[c][:, :], w[:, (17 + f) * P:(18 + f) * P], xn[:, c, :],
                           start=True, stop=True).then_inc(e_h1, 1)
                        mm(bank[2 + c][:, :], w[:, (19 + f) * P:(20 + f) * P], xn[:, c, :],
                           start=True, stop=True).then_inc(e_x3, 1)
                        if k >= 1:
                            shared_down(k - 1)
                shared_down(3)
                for c in range(2):
                    pe.wait_ge(m_comb, 2 + c + 1)
                    for j in range(BH):
                        last = nc.tensor.transpose(
                            bank[4 + c][:, :].bitcast(bf16)[:, j * P:j * P + P],
                            comb_pieces[:, BH * c + j, 0:P], ident_bf[:, :])
                    last.then_inc(m_combT, 1)
                pe.wait_ge(m_combE, 4)
                pe.wait_ge(e_z, 2)

                def late(e, c):
                    pe.wait_ge(e_h, 2 * e + c + 1)
                    if (e, c) != (0, 0):
                        pe.wait_ge(e_v, 2 * e + c)
                    mm(bank[6][:, :], ring[:, e % 4, 2 * P:3 * P], wb[:, c, :], start=True, stop=True)\
                        .then_inc(e_x2, 1)

                for e in range(8):
                    for c in range(2):
                        k = 2 * e + c
                        sel = comb_t[:, 0, c * HALF:c * HALF + HALF]
                        if k >= 1:
                            pe.wait_ge(e_xs, k)
                        mm(bank[4][:, :], select2[:, e, 0, :], sel, start=True, stop=True).then_inc(e_wb, 1)
                        if k >= 1:
                            late((k - 1) // 2, (k - 1) % 2)
                        pe.wait_ge(w_in[e % 4], fills2(e))
                        pe.wait_ge(e_xs, k + 1)
                        mm(bank[c][:, :], ring[:, e % 4, 0:P], wa[:, c, :], start=True, stop=True)\
                            .then_inc(e_h1, 1)
                        mm(bank[2 + c][:, :], ring[:, e % 4, P:2 * P], wa[:, c, :], start=True, stop=True)\
                            .then_inc(e_x3, 1)
                        if k >= 1:
                            pe.wait_ge(e_u, k)
                        mm(bank[5][:, :], select2[:, e, 1, :], sel, start=True, stop=True).then_inc(e_mk, 1)
                late(7, 1)
            if stages > 6:
                pe.wait_ge(in_mats3, 16)
                pe.wait_ge(e_v, 16)
                prep(1, 0)
                prep(1, 1)
                attn_v(1)
                norm(NORM_OF[6][0])
                prep(1, 2)
                prep(1, 3)
                pe.wait_ge(a_first, 8)
                pe.wait_ge(a_vtok, 4)
                bias_through_o(1)
                attn(1)
            if stages > 7:
                norm(NORM_OF[7][0])
                moe(1)

        @block.scalar
        def _(act):
            fn = nc.scalar.activation

            def norm(i):
                for c in range(2):
                    act.wait_ge(ln_cen, 2 * i + c + 1)
                    fn(sq[:, c, :], cen[:, c, :], ACT.Square).then_inc(ln_sq, 1)
                for c in range(2):
                    act.wait_ge(ln_var, 2 * i + c + 1)
                    fn(std[:, c, :], bank[c][:, :], ACT.Sqrt, bias=eps_col[:, :]).then_inc(ln_std, 1)

            def prep(inst, k):
                n = 4 * inst + k
                bias = col(A_BIAS[inst][0] if k < 2 else A_BIAS[inst][1])
                act.wait_ge(a_proj, n + 1)
                if n >= 2:
                    act.wait_ge(a_rest, n - 1)
                    act.wait_ge(a_stacked[n % 2], 144 * (n // 2))
                fn(wa[:, k % 2, :], bank[6 + k % 2][:, :], ACT.Identity, bias=bias).then_inc(a_full, 1)
                fn(pieces[:, n % 2, 0, :], bank[6 + k % 2][:, :], ACT.Identity, bias=bias)\
                    .then_inc(a_first, 1)

            def v_token_major(inst):
                for c in range(2):
                    act.wait_ge(a_vproj, 2 * inst + c + 1)
                    fn(v_tok[:, BH * c:BH * c + BH, :], bank[4 + c][:, :], ACT.Copy).then_inc(a_vtok, 1)

            def update(s, src, n, width):
                if n is not None:
                    act.wait_ge(x_updated, n)
                if s in (0, 2, 3, 6):
                    fn(upd[:, 0:width], src, ACT.Identity, bias=tgb[:, s:s + 1], scale=tg[:, s:s + 1])\
                        .then_inc(update_ready, 1)
                else:
                    fn(upd[:, 0:width], src, ACT.Copy, scale=tg[:, s:s + 1]).then_inc(update_ready, 1)

            def units(base, s, before, y, scale, y_before):
                def exp(b, u):
                    act.wait_ge(a_sub, base + 4 * b + u + 1)
                    if not (base == 0 and isinstance(b, int) and b == 0 and u < 2):
                        act.wait_ge(a_tr, base + 4 * b + u - 1)
                    fn(wb[:, u % 2, :], wa[:, u % 2, :], ACT.Exp, scale=scale).then_inc(a_exp, 1)

                def evac(b, u):
                    act.wait_ge(a_tr, base + 4 * b + u + 1)
                    if not (base == 0 and isinstance(b, int) and b == 0 and u < 2):
                        act.wait_ge(a_pv, base + 4 * b + u - 1)
                    fn(wc[:, u % 2, :], bank[2 + u % 2][:, :], ACT.Copy).then_inc(a_ev, 1)

                def batch_update(b):
                    act.wait_ge(a_y, y_before + b + 1)
                    skip = before == 0 and isinstance(b, int) and b == 0
                    update(s, y, None if skip else before + b, P)

                def batch(b, first, last):
                    for u in range(4):
                        if u < 3:
                            exp(b, u + 1)
                        elif not last:
                            exp(b + 1, 0)
                        evac(b, u)
                    if not first:
                        batch_update(b - 1)
                exp(0, 0)
                batch(0, True, False)
                with act.Fori(1, B - 1) as b:
                    batch(b, False, False)
                batch(B - 1, False, True)
                batch_update(B - 1)

            def moe(n):
                m = MOE[n]
                u0, s = moe_units_until(n), m["stage"]
                for c in range(2):
                    act.wait_ge(m_logit, 4 * n + c + 1)
                    fn(rt[:, c, 0:4 * m["E"]].rearrange("p (t e) -> p t e", t=4),
                       bank[4 + c][:, :].rearrange("p (t e) -> p t e", t=4)[:, :, 0:m["E"]],
                       ACT.Sigmoid).then_inc(m_score, 1)
                nc.scalar.preload_act_table(ACT.Silu)

                def silu(c, unit, first):
                    act.wait_ge(m_g, unit + 1)
                    if not first:
                        act.wait_ge(m_t, unit - 1)
                    fn(wa[:, c, :], bank[c][:, :], ACT.Silu).then_inc(m_silu, 1)
                silu(0, u0, n == 0)
                silu(1, u0 + 1, n == 0)
                with act.Fori(0, m["pairs"] // 4) as it:
                    for k in range(8):
                        silu(k % 2, u0 + 2 + 8 * it + k, False)
                before = x_count(s - 1, 1)
                for c in range(2):
                    if c == 0:
                        act.wait_ge(m_zero, n + 1)
                    else:
                        act.wait_ge(m_down, u0 + m["units"])
                    update(s, bank[6 + c][:, :], before + c, HALF)

            act.wait_ge(in_x, 48)
            fn(tg[:, :], gates[:, :], ACT.Tanh).then_inc(tg_ready, 1)
            act.wait_ge(in_ctx, 48)
            act.wait_ge(prepared, 4)
            prep(0, 0)
            prep(0, 1)
            norm(0)
            v_token_major(0)
            prep(0, 2)
            prep(0, 3)
            act.wait_ge(tgb_ready, 3)
            act.wait_ge(tg_ready, 1)
            nc.scalar.preload_act_table(ACT.Exp)
            units(0, 0, 0, bank[6][:, 2 * P:3 * P], SCALE_A, 0)
            if stages > 1:
                norm(NORM_OF[1][0])
                moe(0)
            if stages > 2:
                norm(NORM_OF[2][0])
                for c in range(2):
                    act.wait_ge(b_proj, c + 1)
                    fn(k1[:, c, :], bank[2 + c][:, :], ACT.Identity, bias=col(K1B)).then_inc(b_evac, 1)
                for c in range(2):
                    act.wait_ge(b_proj, 3 + c)
                    fn(q1[:, c, :], bank[6 + c][:, :], ACT.Identity, bias=col(Q1B)).then_inc(b_evac, 1)
                for c in range(2):
                    act.wait_ge(b_proj, 5 + c)
                    fn(gate1[:, c, :], bank[2 + c][:, :], ACT.Sigmoid, bias=col(G1B)).then_inc(b_evac, 1)
                for c in range(2):
                    act.wait_ge(b_p, c + 1)
                    fn(wb[:, c, :], wa[:, c, :], ACT.Exp).then_inc(b_e, 1)
                for c in range(2):
                    act.wait_ge(b_tr, c + 1)
                    fn(wc[:, c, :], bank[4 + c][:, :], ACT.Copy).then_inc(b_pt, 1)
                for c in range(2):
                    act.wait_ge(b_y, c + 1)
                    update(2, bank[c][:, :], 10 + c, HALF)
            if stages > 3:
                norm(NORM_OF[3][0])
                for n in range(8):
                    act.wait_ge(d_up, n + 1)
                    if n >= 4:
                        act.wait_ge(d_down, n - 3)
                    fn(hidden1(n), bank[2 + n % 4][:, :], GELU, bias=col(FCB + n // 2)).then_inc(d_act, 1)
                for c in range(2):
                    act.wait_ge(d_down, 7 + c)
                    update(3, bank[6 + c][:, :], 12 + c, HALF)
            if stages > 4:
                for i in NORM_OF[4]:
                    norm(i)
                for n in range(0, 40, 2):
                    act.wait_ge(c_proj, n + 1)
                    dst, scale = product2(n)
                    fn(dst, bank2(n), ACT.Copy, scale=scale).then_inc(c_kq[0], 1)
                nc.scalar.preload_act_table(ACT.Exp)
                units(UNITS, 4, 14, bank[6][:, 0:P], 1.0, B)
            if stages > 5:
                norm(NORM_OF[5][0])
                for c in range(2):
                    act.wait_ge(m_shift, c + 1)
                    fn(rt[:, c, 0:32], rt[:, c, 0:32], ACT.Exp).then_inc(m_score, 1)
                for k in range(4):
                    act.wait_ge(e_h1, k + 1)
                    if k >= 2:
                        act.wait_ge(e_sh, k - 1)
                    fn(wb[:, k % 2, :], bank[k % 2][:, :], ACT.Silu).then_inc(e_sg, 1)
                act.wait_ge(e_sh, 4)
                for k in range(16):
                    e, c = k // 2, k % 2
                    act.wait_ge(e_h1, 4 + k + 1)
                    if k >= 2:
                        act.wait_ge(e_x2, k - 1)
                    fn(wb[:, c, :], bank[c][:, :], ACT.Silu, bias=col(B1 + e)).then_inc(e_h, 1)
                    act.wait_ge(e_x3, 4 + k + 1)
                    if k >= 2:
                        act.wait_ge(e_u, k - 1)
                    fn(sq[:, c, :], bank[2 + c][:, :], ACT.Identity, bias=col(B3 + e)).then_inc(e_x3b, 1)
                for c in range(2):
                    act.wait_ge(e_y, 15 + c)
                    update(5, cen[:, c, :], 22 + c, HALF)
            if stages > 6:
                prep(1, 0)
                prep(1, 1)
                v_token_major(1)
                norm(NORM_OF[6][0])
                prep(1, 2)
                prep(1, 3)
                act.wait_ge(tgb_ready, 4)
                nc.scalar.preload_act_table(ACT.Exp)
                units(2 * UNITS, 6, 24, bank[6][:, 2 * P:3 * P], SCALE_A, 2 * B)
            if stages > 7:
                norm(NORM_OF[7][0])
                moe(1)

        @block.vector
        def _(dve):
            v = nc.vector
            chain = [0]

            def link(ins):
                chain[0] += 1
                ins.then_inc(dve_chain, 1)
                dve.wait_ge(dve_chain, chain[0])

            def norm(i):
                src, dst, affine, _ = NORMS[i]
                for c in range(2):
                    dve.wait_ge(ln_mean, 2 * i + c + 1)
                    if i > 0:
                        dve.wait_ge(ln_out, 2 * (i - 1) + c + 1)
                    v.tensor_tensor(cen[:, c, :], src(c), bank[c][:, :], ALU.subtract).then_inc(ln_cen, 1)
                for c in range(2):
                    n = 2 * i + c + 1
                    dve.wait_ge(ln_std, n)
                    v.reciprocal(std[:, c, :], std[:, c, :]).then_inc(ln_inv, 1)
                    dve.wait_ge(ln_inv, n)
                    if affine is None:
                        v.tensor_tensor(dst(c), cen[:, c, :], std[:, c, :], ALU.mult).then_inc(ln_out, 1)
                    else:
                        link(v.tensor_tensor(cen[:, c, :], cen[:, c, :], std[:, c, :], ALU.mult))
                        v.tensor_scalar(dst(c), cen[:, c, :].rearrange("p (b t) -> p b t", b=BH),
                                        col(affine[0]), col(affine[1]), ALU.mult, ALU.add)\
                            .then_inc(ln_out, 1)

            def prep(inst, k):
                n = 4 * inst + k
                dve.wait_ge(a_full, n + 1)
                dve.wait_ge(a_first, n + 1)
                v.tensor_tensor(wb[:, k % 2, :], wa[:, k % 2, :], pieces[:, n % 2, 0, :], ALU.subtract)\
                    .then_inc(a_rest, 1)
                dve.wait_ge(a_rest, n + 1)
                v.tensor_copy(pieces[:, n % 2, 1, :], wb[:, k % 2, :]).then_inc(a_piece2, 1)
                dve.wait_ge(a_piece2, n + 1)
                v.tensor_tensor(pieces[:, n % 2, 2, :], wb[:, k % 2, :], pieces[:, n % 2, 1, :],
                                ALU.subtract).then_inc(a_split, 1)

            def units(base, heads, extra):
                def unit(b, u):
                    n = base + 4 * b + u
                    s = bank[u % 2][:, :].rearrange("p (h k) -> p h k", h=heads)
                    dve.wait_ge(a_s, n + 1)
                    v.tensor_reduce(row_max[:, u % 2, 0:heads], s, X, ALU.max).then_inc(a_max, 1)
                    dve.wait_ge(a_max, n + 1)
                    if not (base == 0 and isinstance(b, int) and b == 0 and u < 2):
                        dve.wait_ge(a_exp, n - 1)
                    v.tensor_tensor(wa[:, u % 2, :].rearrange("p (h k) -> p h k", h=heads), s,
                                    row_max[:, u % 2, 0:heads].unsqueeze(2)
                                    .to_broadcast([P, heads, 512 // heads]), ALU.subtract)\
                        .then_inc(a_sub, 1)

                def batch(b, first, last):
                    for u in range(4):
                        unit(b, u)
                        extra(b, u, first, last)
                batch(0, True, False)
                with dve.Fori(1, B - 1) as b:
                    batch(b, False, False)
                batch(B - 1, False, True)
                for u in range(4):
                    extra(B, u, False, None)

            def attn(inst):
                base, tb = (0 if inst == 0 else 2 * UNITS), B * inst
                yb = 0 if inst == 0 else 2 * B

                def extra(b, u, first, last):
                    if first:
                        return
                    if u == 0:
                        dve.wait_ge(a_pv, base + 4 * b)
                        v.tensor_copy(o_sb[:, 0:2, :], bank[4][:, 0:2 * P]).then_inc(a_ocopy, 1)
                    if u == 1:
                        dve.wait_ge(a_z, tb + b)
                        v.reciprocal(o_inv[:, :, :], bank[6][:, 0:2 * P]).then_inc(a_inv, 1)
                        dve.wait_ge(a_inv, tb + b)
                        dve.wait_ge(a_ocopy, tb + b)
                        if not (inst == 0 and isinstance(b, int) and b == 1):
                            dve.wait_ge(a_y, yb + b - 1)
                        v.tensor_tensor(o_sb[:, 2:4, :], o_sb[:, 0:2, :], o_inv[:, :, :], ALU.mult)\
                            .then_inc(a_norm, 1)
                units(base, 4, extra)

            def attn2():
                base = UNITS

                def q_fill(b):
                    tok = ds(b * P, P)
                    v.tensor_copy(q_slot[0:64, :, 0, :], q2[0:64, :, tok]).then_inc(c_slot, 1)
                    v.tensor_copy(q_slot[64:128, :, 1, :], q2[64:128, :, tok]).then_inc(c_slot, 1)

                def extra(b, u, first, last):
                    if last is None:
                        if u == 0:
                            finish(b - 1, 1)
                        return
                    if u == 1 and not last:
                        dve.wait_ge(a_s, base + 4 * b + 4)
                        q_fill(b + 1)
                    if u == 0 and not first:
                        finish(b - 1, 1)
                    if u == 3:
                        finish(b, 0)

                def finish(b, p):
                    o = bank[4 + p][:, :].rearrange("p (m j q) -> p m j q", m=2, j=2)
                    dve.wait_ge(a_pv, base + 4 * b + 2 * p + 2)
                    if not (p == 0 and isinstance(b, int) and b == 0):
                        dve.wait_ge(c_inv, 2 * b + p)
                        dve.wait_ge(c_half, 2 * b + p)
                    v.reciprocal(o_inv[0:64, :, :], o[64:128, :, 0, :]).then_inc(c_rec, 1)
                    v.reciprocal(o_inv[64:128, :, :], o[0:64, :, 1, :]).then_inc(c_rec, 1)
                    dve.wait_ge(c_rec, 4 * b + 2 * p + 2)
                    if p == 0:
                        dve.wait_ge(a_y, B + b)
                    v.tensor_tensor(o_sb[0:64, 2 * p:2 * p + 2, :], o[0:64, :, 0, :],
                                    o_inv[0:64, :, :], ALU.mult).then_inc(c_half, 1)
                    v.tensor_tensor(o_sb[64:128, 2 * p:2 * p + 2, :], o[64:128, :, 1, :],
                                    o_inv[64:128, :, :], ALU.mult).then_inc(c_inv, 1)
                dve.wait_ge(pool_ready, 4)
                for k in range(2):
                    dve.wait_ge(c_kq[k], 20)
                q_fill(0)
                units(base, 2, extra)

            def ranks(vals, g, tri, s0):
                shape = [P, 4, g, g]
                def square(n):
                    return rt[:, n, 0:4 * g * g].rearrange("p (t i j) -> p t i j", t=4, i=g)
                mine = vals.unsqueeze(3).to_broadcast(shape)
                other = vals.unsqueeze(2).to_broadcast(shape)
                more, same = square(s0), square(s0 + 1)
                v.tensor_tensor(more, other, mine, ALU.is_gt)
                link(v.tensor_tensor(same, other, mine, ALU.is_equal))
                link(v.tensor_tensor(same, same, tri[:, :, :].unsqueeze(1).to_broadcast(shape), ALU.mult))
                link(v.tensor_tensor(more, more, same, ALU.add))
                rank = rt[:, s0 + 2, 0:4 * g].rearrange("p (t i) -> p t i", t=4)
                link(v.tensor_reduce(rank, more, X, ALU.add))
                return rank

            def grid(n, e):
                return rt[:, n, 0:4 * e].rearrange("p (t e) -> p t e", t=4)

            def split_weights(comb, e, c, tmp):
                rest = grid(tmp, e)
                dst = comb_pieces[:, BH * c:BH * c + BH, :]
                link(v.tensor_copy(dst[:, :, 0:e], comb))
                link(v.tensor_tensor(rest, comb, dst[:, :, 0:e], ALU.subtract))
                link(v.tensor_copy(dst[:, :, e:2 * e], rest))
                return v.tensor_tensor(dst[:, :, 2 * e:3 * e], rest, dst[:, :, e:2 * e], ALU.subtract)

            def route(n, c):
                m = MOE[n]
                E, G, K = m["E"], m["G"], m["K"]
                size = E // G
                dve.wait_ge(m_score, 4 * n + c + 1)
                score = grid(c, E)
                bias = route_bias[:, m["bias"]:m["bias"] + E].unsqueeze(1).to_broadcast([P, 4, E])
                biased = grid(2, E)
                link(v.tensor_tensor(biased, score, bias, ALU.add))
                groups = biased.rearrange("p t (g s) -> p t g s", g=G)
                best = grid(3, G)
                if n == 0:
                    pair = groups.rearrange("p t g (a b) -> p t g a b", a=2)
                    pair = biased.rearrange("p t (g a b) -> p (t g) a b", g=G, a=2)
                    hi = rt[:, 4, 0:32].rearrange("p (x a) -> p x a", a=2)
                    lo = rt[:, 5, 0:32].rearrange("p (x a) -> p x a", a=2)
                    v.tensor_tensor(hi, pair[:, :, :, 0], pair[:, :, :, 1], ALU.max)
                    link(v.tensor_tensor(lo, pair[:, :, :, 0], pair[:, :, :, 1], ALU.min))
                    t1, t2, t3 = (rt[:, k, 0:16] for k in (6, 7, 8))
                    v.tensor_tensor(t1, hi[:, :, 0], hi[:, :, 1], ALU.max)
                    v.tensor_tensor(t2, hi[:, :, 0], hi[:, :, 1], ALU.min)
                    link(v.tensor_tensor(t3, lo[:, :, 0], lo[:, :, 1], ALU.max))
                    link(v.tensor_tensor(t2, t2, t3, ALU.max))
                    link(v.tensor_tensor(rt[:, 3, 0:16], t1, t2, ALU.add))
                else:
                    link(v.tensor_reduce(best, groups, X, ALU.max))
                rank = ranks(best, G, m["tri"], 4)
                keep = grid(7, G)
                link(v.tensor_scalar(keep, rank, float(m["TG"]) - 0.5, None, ALU.is_lt))
                width = E + 8 - K
                ext = rt[:, 8, 0:4 * width].rearrange("p (t e) -> p t e", t=4)
                cut = rt[:, 9, 0:4 * width].rearrange("p (t e) -> p t e", t=4)
                v.memset(ext[:, :, E:width], 3e38)
                for t in range(4):
                    ins = v.tensor_tensor(ext[:, t, 0:E].rearrange("p (g s) -> p g s", g=G),
                                          groups[:, t, :, :],
                                          keep[:, t, :].unsqueeze(2).to_broadcast([P, G, size]), ALU.mult)
                link(ins)
                top = rt[:, 10, 0:32].rearrange("p (t k) -> p t k", t=4)
                for t in range(4):
                    ins = v.max(top[:, t, :], ext[:, t, :])
                link(ins)
                for t in range(4):
                    ins = v.match_replace(cut[:, t, :], top[:, t, :], ext[:, t, :], -3e38)
                link(ins)
                chosen = grid(11, E)
                link(v.tensor_scalar(chosen, cut[:, :, 0:E], -1e38, None, ALU.is_lt))
                weight = score if n == 0 else ext[:, :, 0:E]
                picked = grid(12, E)
                link(v.tensor_tensor(picked, weight, chosen, ALU.mult))
                total = rt[:, 13, 0:4]
                link(v.tensor_reduce(total, picked, X, ALU.add))
                link(v.tensor_scalar(total, total, 1e-20 if n == 0 else 1e-8, None, ALU.add))
                link(v.reciprocal(total, total))
                link(v.tensor_tensor(picked, picked, total.unsqueeze(2).to_broadcast([P, 4, E]), ALU.mult))
                if n == 0:
                    link(v.tensor_scalar(picked, picked, 2.5, None, ALU.mult))
                split_weights(picked, E, c, 11).then_inc(m_comb, 1)

            def weights_out(n, c, kt):
                dve.wait_ge(m_combT, 2 * n + c + 1)
                v.tensor_copy(comb_t[:, 0:kt, c * HALF:c * HALF + HALF],
                              bank[4 + c][:, :].bitcast(bf16)[:, 0:kt * HALF]
                              .rearrange("p (k t) -> p k t", k=kt)).then_inc(m_combE, 1)

            def moe(n):
                m = MOE[n]
                u0, kt = moe_units_until(n), m["KT"]

                def products(c, unit, weighed, first):
                    dve.wait_ge(m_silu, unit + 1)
                    dve.wait_ge(m_u, unit + 1)
                    v.tensor_tensor(wb[:, c, :], wa[:, c, :], bank[2 + c][:, :], ALU.mult).then_inc(m_t, 1)
                    dve.wait_ge(m_t, unit + 1)
                    if not first:
                        dve.wait_ge(m_down, unit - 1)
                    if weighed:
                        dve.wait_ge(m_cb, unit - 2 * n - 1)
                        v.tensor_tensor(wc[:, c, :], wb[:, c, :], bank[4 + c][:, :], ALU.mult)\
                            .then_inc(m_h, 1)
                    else:
                        v.tensor_copy(wc[:, c, :], wb[:, c, :]).then_inc(m_h, 1)
                for c in range(2):
                    route(n, c)
                for c in range(2):
                    products(c, u0 + c, False, n == 0)
                for c in range(2):
                    weights_out(2 * n, c, kt)
                with dve.Fori(0, m["pairs"] // 4) as it:
                    for k in range(8):
                        products(k % 2, u0 + 2 + 8 * it + k, True, False)

            v.memset(mean_w[:, :], 1.0 / P).then_inc(prepared, 1)
            v.memset(zeros_bf[:, :], 0.0).then_inc(prepared, 1)
            v.memset(arena[64:128, 0:8192], 0.0).then_inc(prepared, 1)
            v.memset(eps_col[:, :], EPS).then_inc(prepared, 1)
            v.memset(ones16, 1.0).then_inc(a_mask, 1)
            dve.wait_ge(in_x, 48)
            v.tensor_scalar(mask_neg, mask_u8, -1e30, None, ALU.mult).then_inc(a_mask, 1)
            prep(0, 0)
            prep(0, 1)
            norm(0)
            prep(0, 2)
            prep(0, 3)
            v.memset(comb_pieces[:, :, :], 0.0)
            dve.wait_ge(tg_ready, 1)
            v.tensor_tensor(tgb[:, 2:3], tg[:, 2:3], col(O1B), ALU.mult).then_inc(tgb_ready, 1)
            v.tensor_tensor(tgb[:, 3:4], tg[:, 3:4], col(PROJB), ALU.mult).then_inc(tgb_ready, 1)
            dve.wait_ge(o_bias, 1)
            v.tensor_scalar(tgb[:, 0:1], bank[7][:, 0:1], col(O0B), tg[:, 0:1], ALU.add, ALU.mult)\
                .then_inc(tgb_ready, 1)
            attn(0)
            if stages > 1:
                norm(NORM_OF[1][0])
                moe(0)
            if stages > 2:
                norm(NORM_OF[2][0])
                for c in range(2):
                    dve.wait_ge(b_v, c + 1)
                    v.tensor_copy(v1[:, BH * c:BH * c + BH, :], bank[4 + c][:, :]).then_inc(b_vev, 1)
                for c in range(2):
                    s = bank[c][:, :].rearrange("p (b k) -> p b k", b=BH)
                    wide = [P, BH, P]
                    dve.wait_ge(b_s, c + 1)
                    link(v.tensor_reduce(row_max[:, c, :], s, X, ALU.max))
                    v.tensor_tensor(wa[:, c, :].rearrange("p (b k) -> p b k", b=BH), s,
                                    row_max[:, c, :].unsqueeze(2).to_broadcast(wide),
                                    ALU.subtract).then_inc(b_p, 1)
                for c in range(2):
                    e = wb[:, c, :].rearrange("p (b k) -> p b k", b=BH)
                    dve.wait_ge(b_e, c + 1)
                    link(v.tensor_reduce(row_max[:, c, :], e, X, ALU.add))
                    link(v.reciprocal(row_max[:, c, :], row_max[:, c, :]))
                    v.tensor_tensor(e, e, row_max[:, c, :].unsqueeze(2).to_broadcast(wide), ALU.mult)\
                        .then_inc(b_n, 1)
                for c in range(2):
                    dve.wait_ge(b_pv, c + 1)
                    dve.wait_ge(b_evac, 5 + c)
                    v.scalar_tensor_tensor(wa[:, c, :], bank[6 + c][:, :], col(V1B), gate1[:, c, :],
                                           ALU.add, ALU.mult).then_inc(b_ctx, 1)
            if stages > 3:
                for n in range(2):
                    w = mats1[:, (5 + 4 * n) * P:(9 + 4 * n) * P]
                    v.tensor_reduce(w_max[:, n:n + 1], w, X, ALU.max, apply_absolute_value=True)\
                        .then_inc(d_rowmax, 1)
                dve.wait_ge(d_max, 1)
                scale, inv, neg = w_stat[:, 0:2], w_stat[:, 2:4], w_stat[:, 4:6]
                link(v.tensor_scalar(scale, w_max[:, 2:4], 1.0 / 127.0, None, ALU.mult))
                v.reciprocal(inv, scale)
                link(v.tensor_scalar(neg, scale, -1.0, None, ALU.mult))
                for n in range(2):
                    w = mats1[:, (5 + 4 * n) * P:(9 + 4 * n) * P]
                    s1, i1_, n1 = scale[:, n:n + 1], inv[:, n:n + 1], neg[:, n:n + 1]
                    q, e = sq[:, 0, :], sq[:, 1, :]
                    link(v.tensor_scalar(q, w, i1_, None, ALU.mult))
                    link(v.scalar_tensor_tensor(e, q, n1, w, ALU.mult, ALU.add))
                    link(v.scalar_tensor_tensor(q, e, i1_, q, ALU.mult, ALU.add))
                    link(v.tensor_scalar(q, q, ROUND, ROUND, ALU.add, ALU.subtract))
                    link(v.tensor_scalar(q, q, 127.0, -128.0, ALU.min, ALU.max))
                    link(v.scalar_tensor_tensor(e, q, s1, w, ALU.mult, ALU.subtract))
                    link(v.tensor_tensor(w, w, e, ALU.add))
                    dve.wait_ge(d_lora, n + 1)
                    v.scalar_tensor_tensor(w, bank[2 + n][:, :], 2.0, w, ALU.mult, ALU.add)\
                        .then_inc(d_w, 1)
                norm(NORM_OF[3][0])
            if stages > 4:
                for i in NORM_OF[4]:
                    norm(i)
                for n in range(1, 40, 2):
                    dve.wait_ge(c_proj, n + 1)
                    dst, scale = product2(n)
                    v.tensor_scalar(dst, bank2(n), scale, None, ALU.mult).then_inc(c_kq[1], 1)
                attn2()
            if stages > 5:
                v.memset(arena[64:128, 0:8192], 0.0).then_inc(prepared, 1)
                norm(NORM_OF[5][0])

                def softmax_route(c):
                    logits = bank[4 + c][:, :].rearrange("p (t e) -> p t e", t=4)[:, :, 0:8]
                    top = rt[:, 2 + c, 0:4]
                    dve.wait_ge(m_logit, 2 + c + 1)
                    link(v.tensor_reduce(top, logits, X, ALU.max))
                    v.tensor_tensor(grid(c, 8), logits, top.unsqueeze(2).to_broadcast([P, 4, 8]),
                                    ALU.subtract).then_inc(m_shift, 1)

                def pick(c):
                    dve.wait_ge(m_score, 2 + c + 1)
                    score, total = grid(c, 8), rt[:, 2 + c, 0:4]
                    link(v.tensor_reduce(total, score, X, ALU.add))
                    link(v.reciprocal(total, total))
                    link(v.tensor_tensor(score, score, total.unsqueeze(2).to_broadcast([P, 4, 8]), ALU.mult))
                    rank = ranks(score, 8, earlier8, 4)
                    v.tensor_scalar(comb_pieces[:, BH * c:BH * c + BH, 24:32], rank, 1.5, None, ALU.is_lt)
                    split_weights(score, 8, c, 8).then_inc(m_comb, 1)

                def shared(k):
                    dve.wait_ge(e_sg, k + 1)
                    dve.wait_ge(e_x3, k + 1)
                    if k >= 2:
                        dve.wait_ge(e_zd, k - 1)
                    v.tensor_tensor(wc[:, k % 2, :], wb[:, k % 2, :], bank[2 + k % 2][:, :], ALU.mult)\
                        .then_inc(e_sh, 1)
                for c in range(2):
                    softmax_route(c)
                for c in range(2):
                    pick(c)
                for k in range(4):
                    shared(k)
                for c in range(2):
                    dve.wait_ge(e_zd, 3 + c)
                    v.tensor_copy(cen[:, c, :], bank[6 + c][:, :]).then_inc(e_z, 1)
                for c in range(2):
                    weights_out(1, c, 1)

                def late(k):
                    e, c = k // 2, k % 2
                    dve.wait_ge(e_x2, k + 1)
                    dve.wait_ge(e_u, k + 1)
                    if k >= 2:
                        dve.wait_ge(e_y, k - 1)
                    v.scalar_tensor_tensor(wc[:, c, :], bank[6][:, :], col(B2 + e), std[:, c, :],
                                           ALU.add, ALU.mult).then_inc(e_v, 1)
                for k in range(16):
                    e, c = k // 2, k % 2
                    dve.wait_ge(e_wb, k + 1)
                    if k >= 2:
                        dve.wait_ge(e_x3, 4 + k - 1)
                    v.tensor_tensor(wa[:, c, :], xn[:, c, :], bank[4][:, :], ALU.mult).then_inc(e_xs, 1)
                    if k >= 1:
                        late(k - 1)
                    dve.wait_ge(e_x3b, k + 1)
                    dve.wait_ge(e_mk, k + 1)
                    v.tensor_tensor(std[:, c, :], sq[:, c, :], bank[5][:, :], ALU.mult).then_inc(e_u, 1)
                late(15)
            if stages > 6:
                prep(1, 0)
                prep(1, 1)
                norm(NORM_OF[6][0])
                prep(1, 2)
                prep(1, 3)
                dve.wait_ge(o_bias, 2)
                v.tensor_scalar(tgb[:, 6:7], bank[7][:, 0:1], col(O3B), tg[:, 6:7], ALU.add, ALU.mult)\
                    .then_inc(tgb_ready, 1)
                attn(1)
            if stages > 7:
                norm(NORM_OF[7][0])
                moe(1)




def kernel(**inputs):
    import numpy as _np
    import ml_dtypes as _ml
    import concourse.bacc as _bacc
    from concourse import mybir as _mybir
    from concourse.bass_utils import run_bass_kernel_spmd as _run

    I = {name: _np.asarray(value) for name, value in inputs.items()}
    P, T, D, HEADS, HD = 128, 1024, 128, 16, 8

    def columns(*vectors):
        return _np.stack(vectors, axis=1)

    def dim_major(w):
        return w.reshape(*w.shape[:-1], HEADS, HD).swapaxes(-1, -2).reshape(w.shape)

    def head_slots(w):
        out = _np.zeros((2, 8, 16) + w.shape[1:], w.dtype)
        out[:, :, :HD] = w.reshape((2, 8, HD) + w.shape[1:])
        return out.reshape((2, P) + w.shape[1:])

    def row_chunks(w):
        return w.reshape(-1, P, w.shape[1]).transpose(1, 0, 2).reshape(P, -1)

    def padded(w, width=P):
        return _np.pad(w, ((0, 0), (0, width - w.shape[1])))

    def expert_pairs(gate, up, down, shared_gate, shared_up, shared_down):
        e, i, h = gate.shape
        def in_major(w, shared):
            pairs = w.reshape(e // 2, 2 * i, h).transpose(0, 2, 1)
            return _np.concatenate([shared.T[None], pairs])
        downs = down.transpose(0, 2, 1).reshape(e // 2, 2 * i, h)
        downs = _np.concatenate([shared_down.T[None], downs])
        return _np.concatenate([in_major(gate, shared_gate), in_major(up, shared_up), downs], axis=2)

    qw, kw, vw = _np.split(I["L3_xattn_in_proj_weight"], 3, axis=0)
    qb, kb, vb = _np.split(I["L3_xattn_in_proj_bias"], 3)
    arrays = {
        "x_t": I["x"].reshape(T, D).T,
        "ctx_t": I["ctx_1024"].reshape(T, D).T,
        "mask": _np.broadcast_to(I["mask_BxS2_bk0"].reshape(1, T), (HEADS, T)).copy()
        .view(_np.int32),
        "gates": _np.broadcast_to(
            _np.stack([I["g_xattn"], I["g_ffn"]], axis=1).reshape(1, 8), (P, 8)),
        "mats0": _np.concatenate([
            dim_major(I["L0_xattn_Wk"]), dim_major(I["L0_xattn_Wq"]), I["L0_xattn_Wv"],
            *head_slots(I["L0_xattn_Wo"]), padded(I["L0_ffn_router_weight"].T)], axis=1),
        "mats1": _np.concatenate([
            I["L1_xattn_Wq"], I["L1_xattn_Wk"], I["L1_xattn_Wv"], I["L1_xattn_Wg"], I["L1_xattn_Wo"],
            I["L1_ffn_W_fc"].T, row_chunks(I["L1_ffn_W_proj"].T)], axis=1),
        "lora": _np.concatenate([
            I["L1_ffn_A_fc"], I["L1_ffn_B_fc"].T, I["L1_ffn_A_proj"], I["L1_ffn_B_proj"].T], axis=1),
        "mats2": _np.concatenate([
            I["L2_xattn_Wq"], I["L2_xattn_Wkv"], row_chunks(I["L2_xattn_Wout"]),
            padded(I["L2_ffn_gate_w"].T), I["L2_ffn_sw1"].T, I["L2_ffn_sw2"].T,
            row_chunks(I["L2_ffn_sw3"].T)], axis=1),
        "mats3": _np.concatenate([
            dim_major(kw.T), dim_major(qw.T), vw.T, *head_slots(I["L3_xattn_out_w"].T),
            padded(I["L3_ffn_gate_w"].T)], axis=1),
        "cols": columns(
            dim_major(I["L0_xattn_bk"]), dim_major(I["L0_xattn_bq"]),
            *head_slots(I["L0_xattn_bv"]), I["L0_xattn_bo"],
            dim_major(kb), dim_major(qb), *head_slots(vb), I["L3_xattn_out_b"],
            I["L1_xattn_bq"], I["L1_xattn_bk"], I["L1_xattn_bv"], I["L1_xattn_bg"], I["L1_xattn_bo"],
            *I["L1_ffn_b_fc"].reshape(4, P), I["L1_ffn_b_proj"],
            I["L2_xattn_ln_m_w"], I["L2_xattn_ln_m_b"], I["L2_xattn_ln_l_w"], I["L2_xattn_ln_l_b"],
            *I["L2_ffn_b1"], *I["L2_ffn_b2"], *I["L2_ffn_b3"]),
        "route_bias": _np.broadcast_to(_np.concatenate(
            [I["L0_ffn_e_bias"], I["L3_ffn_gate_bias"]]).reshape(1, -1), (P, 80)),
        "experts0": expert_pairs(*(I["L0_ffn_" + n] for n in (
            "gate_w", "up_w", "down_w", "sh_gate_w", "sh_up_w", "sh_down_w"))),
        "experts3": expert_pairs(*(I["L3_ffn_" + n] for n in (
            "eg_w", "eu_w", "ed_w", "sg_w", "su_w", "sd_w"))),
        "experts2": _np.concatenate([I["L2_ffn_" + n].transpose(0, 2, 1) for n in ("w1", "w3", "w2")], axis=2),
    }
    arrays.update(_constants(_np, _ml))
    arrays = {name: _np.ascontiguousarray(a) for name, a in arrays.items()}
    nc = _bacc.Bacc("TRN2", target_bir_lowering=False, num_devices=1)
    aps = {name: nc.dram_tensor("in_" + name, a.shape, _mybir.dt.from_np(a.dtype), kind="ExternalInput").ap()
           for name, a in arrays.items()}
    out = nc.dram_tensor("out_t", (D, T), _mybir.dt.float32, kind="ExternalOutput").ap()
    flamingo_kernel(nc, aps, out)
    r = _run(nc, [{"in_" + name: a for name, a in arrays.items()}], core_ids=[0])
    return _np.ascontiguousarray(r.results[0]["out_t"].T).reshape(8, 128, D)


def _constants(np, ml):
    P = 128
    bf16 = ml.bfloat16
    lane = np.arange(P)

    def expert_select(experts, ktiles):
        rows = np.arange(ktiles * P)
        pairs = np.zeros((1 + experts // 2, ktiles, P, P), bf16)
        for pair in range(experts // 2):
            mine = (rows[:, None] < 3 * experts) & (rows[:, None] % experts == 2 * pair + lane[None] // 64)
            pairs[1 + pair] = mine.reshape(ktiles, P, P)
        return pairs.transpose(0, 2, 1, 3)

    sel2 = np.zeros((8, 2, P, P), bf16)
    for e in range(8):
        for piece in range(3):
            sel2[e, 0, 8 * piece + e] = 1
        sel2[e, 1, 24 + e] = 1

    def earlier(n):
        return np.broadcast_to(np.tril(np.ones((n, n), np.float32), -1).reshape(1, n * n), (P, n * n))

    return {
        "ident": np.eye(P, dtype=np.float32),
        "ident_bf": np.eye(P, dtype=bf16),
        "spread_sum": (lane[:, None] == lane[None] // 16 * 16 + 8).astype(np.float32),
        "earlier4": earlier(4), "earlier8": earlier(8),
        "select0": expert_select(16, 1), "select3": expert_select(64, 2),
        "select2": sel2.transpose(2, 0, 1, 3),
    }
```

```python
import concourse.bass as bass
from concourse import mybir
from contextlib import ExitStack



def flamingo_kernel(nc, a, out, stages=8):
    f32, bf16 = mybir.dt.float32, mybir.dt.bfloat16
    ACT, ALU, X = mybir.ActivationFunctionType, mybir.AluOpType, mybir.AxisListType.X
    ds = bass.ds

    P, T, B = 128, 1024, 8
    HALF = T // 2
    BH = B // 2
    HEADS, HD = 16, 8
    QUADS = HEADS // 4
    SPLIT = 3
    PAIRS = SPLIT * SPLIT
    MASK_ROW = 96
    EPS = 1e-5
    GELU = ACT.Gelu
    REDUCE_MAX = bass.bass_isa.ReduceOp.max

    ctx = ExitStack()
    with ctx:
        def sb(name, shape, dt=f32):
            return ctx.enter_context(nc.sbuf_tensor(name, shape, dt))

        def signal(name):
            return ctx.enter_context(nc.semaphore(name))

        x = sb("x", [P, 2, HALF])
        context = sb("context", [P, 2, HALF])
        xn = sb("xn", [P, 2, HALF])
        latents = sb("latents", [P, B, 2, P])
        ident = sb("ident", [P, P])
        ident_bf = sb("ident_bf", [P, P], bf16)
        ones = sb("ones", [P, P])
        mean_w = sb("mean_w", [P, P])
        zeros_bf = sb("zeros_bf", [P, HALF], bf16)
        earlier4 = sb("earlier4", [P, 4, 4])
        earlier8 = sb("earlier8", [P, 8, 8])
        N0, N1, N2, N3 = (a[f"mats{n}"].shape[1] for n in range(4))
        mats0, mats1, mats2, mats3 = (sb(f"mats{n}", [P, w]) for n, w in enumerate((N0, N1, N2, N3)))
        lora = sb("lora", [16, 1280])
        cols = sb("cols", [P, a["cols"].shape[1]])
        gates = sb("gates", [P, 8])
        tg = sb("tg", [P, 8])
        tgb = sb("tgb", [P, 8])
        route_bias = sb("route_bias", [P, 80])
        mask_words = sb("mask_words", [HEADS, T // 4], mybir.dt.int32)
        mask_u8 = mask_words[:, :].bitcast(mybir.dt.uint8)
        latent_rows = latents[0:HEADS, :, :, :].rearrange("p b s t -> p (b s t)")
        mask_neg = latent_rows[:, 0:512].bitcast(bf16)
        ones16 = latent_rows[:, 512:1024].bitcast(bf16)
        arena = sb("arena", [P, 20480])
        stack_q = arena[:, 0:8192].bitcast(bf16).rearrange("p (h t) -> p h t", h=HEADS)
        stack_k = arena[:, 8192:16384].bitcast(bf16).rearrange("p (h t) -> p h t", h=HEADS)
        q1 = arena[:, 0:1024].rearrange("p (c t) -> p c t", c=2)
        k1 = arena[:, 1024:2048].rearrange("p (c t) -> p c t", c=2)
        gate1 = arena[:, 2048:3072].rearrange("p (c t) -> p c t", c=2)
        v1 = arena[:, 3072:4096].rearrange("p (b d) -> p b d", b=B)
        k2 = arena[:, 0:8192].rearrange("p (m b k) -> p m b k", m=4, b=B)
        q2 = arena[:, 8192:11264].rearrange("p (m t) -> p m t", m=3)
        v2 = arena[:, 11264:20480].rearrange("p (t s d) -> p t s d", t=2 * B, d=64)
        rt = arena[:, 16384:16384 + 14 * 288].rearrange("p (n v) -> p n v", n=14)
        v_tok = sb("v_tok", [P, B, P])
        head_v = sb("head_v", [P, 2304])
        v_slots = head_v[:, :].rearrange("p (g c) -> p g c", g=2)
        q2_last = head_v[:, 0:1024]
        q_slot = [sb("q_slot", [P, 4, 2, P])[:, :, :, :],
                  head_v[:, 1024:2048].rearrange("p (m j t) -> p m j t", m=4, j=2)]
        cen = sb("cen", [P, 2, HALF])
        sq = sb("sq", [P, 2, HALF])
        diag = sb("diag", [P, 2, HALF])
        rstd = sb("rstd", [P, 2, BH])
        wa, wb, wc = (sb(n, [P, 2, HALF]) for n in ("wa", "wb", "wc"))
        pieces = sb("pieces", [P, 2, SPLIT, HALF], bf16)
        row_max = sb("row_max", [P, 2, 4])
        o_sb = sb("o_sb", [P, 4, P])
        o_tok = sb("o_tok", [P, P])
        o_fm = sb("o_fm", [P, 4, P])
        o_inv = sb("o_inv", [P, 16])
        upd = sb("upd", [P, HALF])
        ring = sb("ring", [P, 4, 384])
        ring_sel = sb("ring_sel", [P, 4, 2, P], bf16)
        select2 = sb("select2", [P, 8, 2, P], bf16)
        comb_pieces = sb("comb_pieces", [P, 8, 256], bf16)
        comb_t = sb("comb_t", [P, 2, T], bf16)
        bank = [ctx.enter_context(nc.psum_tensor(f"bank{n}", [P, 512], f32)) for n in range(8)]

        in_ctx, in_x, in_consts, in_mats1, in_mats2, in_mats3 = (
            signal(n) for n in ("in_ctx", "in_x", "in_consts", "in_mats1", "in_mats2", "in_mats3"))
        prepared = signal("prepared")
        pool_ready = signal("pool_ready")
        tg_ready, tgb_ready = signal("tg_ready"), signal("tgb_ready")
        x_updated = signal("x_updated")
        update_ready = signal("update_ready")
        out_stored = signal("out_stored")
        ln_mean, ln_cen, ln_sq, ln_var, ln_std, ln_inv, ln_diag, ln_spread, ln_out = (
            signal(n) for n in ("ln_mean", "ln_cen", "ln_sq", "ln_var", "ln_std", "ln_inv",
                                "ln_diag", "ln_spread", "ln_out"))
        dve_chain = signal("dve_chain")
        act_chain = signal("act_chain")

        K0B, Q0B, V0B, O0B, K3B, Q3B, V3B, O3B = range(8)
        Q1B, K1B, V1B, G1B, O1B, FCB, PROJB = 8, 9, 10, 11, 12, 13, 17
        LNMW, LNMB, LNLW, LNLB, B1, B2, B3 = 18, 19, 20, 21, 22, 30, 38

        def col(n):
            return cols[:, n:n + 1]

        PER_STAGE = [8, 2, 2, 2, 8, 2, 8, 2]

        def x_count(s, c):
            return sum(PER_STAGE[:s]) + PER_STAGE[s] * (c + 1) // 2

        def whole(t):
            return lambda c: t[:, c, :]

        def latent_half(which):
            return lambda c: latents[:, BH * c:BH * c + BH, which, :]

        NORMS = []
        NORM_OF = {}
        for s in range(8):
            NORM_OF[s] = [len(NORMS)]
            NORMS.append((whole(x), whole(xn), None, ("x", s)))
            if s == 4:
                NORM_OF[s] += [len(NORMS), len(NORMS) + 1]
                NORMS.append((whole(context), latent_half(0), (LNMW, LNMB), ("ctx", s)))
                NORMS.append((whole(xn), latent_half(1), (LNLW, LNLB), ("xn", s)))

        def norm_bank(c):
            return bank[c]

        A_STAGE = [0, 6]
        A_MATS = [mats0, mats3]
        A_BIAS = [(K0B, Q0B, V0B, O0B), (K3B, Q3B, V3B, O3B)]
        a_proj, a_full, a_first, a_rest, a_piece2, a_split = (
            signal(n) for n in ("a_proj", "a_full", "a_first", "a_rest", "a_piece2", "a_split"))
        a_stacked = [signal("a_stacked0"), signal("a_stacked1")]
        a_mask = signal("a_mask")
        a_vproj, a_vtok = signal("a_vproj"), signal("a_vtok")
        a_s, a_max, a_sub, a_exp, a_tr, a_ev, a_pv = (
            signal(n) for n in ("a_scores", "a_max", "a_shifted", "a_exp", "a_transposed",
                                "a_evacuated", "a_pv"))
        a_slots, a_ocopy, a_turned, a_inv, a_norm, a_back, a_ofm, a_y = (
            signal(n) for n in ("a_slots", "a_ocopy", "a_turned", "a_inverse", "a_normed", "a_back",
                                "a_ofm", "a_y"))
        UNITS = B * QUADS
        SCALE_A = HD ** -0.5

        c_proj, c_slot, c_rec, c_norm = (signal(n) for n in ("c_proj", "c_qslot", "c_rec", "c_norm"))
        c_kq = [signal("c_evac0"), signal("c_evac1")]
        o_bias = signal("o_bias")

        w_in = [signal(f"w_in{s}") for s in range(4)]
        m_logit, m_score, m_comb, m_combT, m_combE = (
            signal(n) for n in ("m_logit", "m_score", "m_comb", "m_comb_t", "m_comb_evac"))
        m_shift = signal("m_shift")
        m_g, m_u, m_cb, m_silu, m_t, m_h, m_down, m_zero = (
            signal(n) for n in ("m_gate", "m_up", "m_weight", "m_silu", "m_prod", "m_hidden", "m_down",
                                "m_zero"))
        MOE = [
            dict(stage=1, E=16, G=4, TG=2, K=4, KT=1, mats=mats0, at=4 * P, bias=0, tri=earlier4),
            dict(stage=7, E=64, G=8, TG=4, K=6, KT=2, mats=mats3, at=4 * P, bias=16, tri=earlier8),
        ]
        for n, m in enumerate(MOE):
            m["n"] = n
            m["pairs"] = m["E"] // 2
            m["units"] = 2 * (m["pairs"] + 1)
            m["u0"] = MOE[0]["units"] if n else 0

        def fills2(e):
            before = sum(1 for q in range(MOE[0]["pairs"] + 1) if (q + 3) % 4 == e % 4)
            return 32 * before + 16 * (e // 4 + 1)

        def moe_units_until(n):
            return sum(m["units"] for m in MOE[:n])

        b_proj, b_evac, b_v, b_vev, b_s, b_p, b_tr, b_pt, b_pv, b_ctx, b_y = (
            signal(n) for n in ("b_proj", "b_evac", "b_v", "b_vev", "b_scores", "b_probs", "b_tr",
                                "b_pt", "b_pv", "b_ctx", "b_y"))
        d_lora, d_up, d_act, d_down, d_rowmax, d_max, d_w = (
            signal(n) for n in ("d_lora", "d_up", "d_act", "d_down", "d_rowmax", "d_max", "d_w"))
        w_max = sb("w_max", [P, 4])
        e_wb, e_xs, e_h1, e_x3, e_mk, e_h, e_x3b, e_u, e_x2, e_v, e_y, e_z, e_sg, e_sh, e_zd = (
            signal(n) for n in ("e_wb", "e_xs", "e_h1", "e_x3", "e_mk", "e_h", "e_x3b", "e_u", "e_x2",
                                "e_v", "e_y", "e_z", "e_sg", "e_sh", "e_zdown"))
        b_e, b_n = signal("b_exp"), signal("b_probs_normed")
        eps_col = sb("eps_col", [P, 1])
        w_stat = sb("w_stat", [P, 6])
        ROUND = 1.5 * 2.0 ** 23

        def bank2(n):
            return bank[2 + n % 6][:, :]

        def product2(n):
            c, k = n // 20, n % 20
            if k < 8:
                m, g = k // 2, k % 2
                return k2[:, m, BH * c + 2 * g:BH * c + 2 * g + 2, :], 1.0
            if k < 11:
                return q2[:, k - 8, c * HALF:c * HALF + HALF], 64 ** -0.5
            if k == 11:
                return q2_last[:, c * HALF:c * HALF + HALF], 64 ** -0.5
            return v2[:, 8 * c + k - 12, 0:8, :], 1.0

        def over_batches(engine, batch):
            batch(0, 0)
            batch(1, 1)
            with engine.Fori(1, B // 2 - 1) as pair:
                batch(2 * pair, 0)
                batch(2 * pair + 1, 1)
            batch(B - 2, 0)
            batch(B - 1, 1)

        def beyond(b, k):
            return not isinstance(b, int) or b >= k

        def hidden1(n):
            return (wa if n % 4 < 2 else wb)[:, n % 2, :]

        block = ctx.enter_context(nc.Block())

        @block.sync
        def _(sp):
            def load(dst, src, done):
                sp.dma_start(dst, src).then_inc(done, 16)

            halves = "p (c t) -> p c t"
            load(mats0[:, :], a["mats0"], in_ctx)
            load(context[:, :, :], a["ctx_t"].rearrange(halves, c=2), in_ctx)
            load(cols[:, :], a["cols"], in_ctx)
            load(ident[:, :], a["ident"], in_ctx)
            load(x[:, :, :], a["x_t"].rearrange(halves, c=2), in_x)
            load(mask_words[:, :], a["mask"], in_x)
            load(gates[:, :], a["gates"], in_x)
            load(ident_bf[:, :], a["ident_bf"], in_consts)
            load(earlier4[:, :, :], a["earlier4"].rearrange("p (i j) -> p i j", i=4), in_consts)
            load(earlier8[:, :, :], a["earlier8"].rearrange("p (i j) -> p i j", i=8), in_consts)
            load(route_bias[:, :], a["route_bias"], in_consts)

            def stack(inst, k):
                n = 4 * inst + k
                sp.wait_ge(a_split, n + 1)
                half = k % 2
                dst = stack_k if k < 2 else stack_q
                for block_ in range(PAIRS):
                    piece = block_ % SPLIT if k < 2 else block_ // SPLIT
                    sp.dma_start(dst[HD * block_:HD * block_ + HD, :, half * HALF:half * HALF + HALF],
                                 pieces[:, n % 2, piece, :]).then_inc(a_stacked[n % 2], 16)

            def fill(m, q, slot):
                w = a["experts0" if m["n"] == 0 else "experts3"]
                s = a["select0" if m["n"] == 0 else "select3"]
                kt = m["KT"]
                sp.dma_start(ring[:, slot, :], w[q]).then_inc(w_in[slot], 16)
                sp.dma_start(ring_sel[:, slot, 0:kt, :], s[q]).then_inc(w_in[slot], 16)

            def fill_dyn(m, q0, j, slot):
                w = a["experts0" if m["n"] == 0 else "experts3"]
                s = a["select0" if m["n"] == 0 else "select3"]
                kt = m["KT"]
                q = q0 + j
                sp.dma_start(ring[:, slot, :], w[ds(q, 1), :, :].squeeze(0)).then_inc(w_in[slot], 16)
                sp.dma_start(ring_sel[:, slot, 0:kt, :],
                             s[ds(q, 1), :, :, :].squeeze(0)).then_inc(w_in[slot], 16)

            def moe_first(n):
                for q in range(4):
                    fill(MOE[n], q, (q + 3) % 4)

            def moe_rest(n):
                m, u0 = MOE[n], moe_units_until(n)
                groups = m["pairs"] // 4
                with sp.Fori(1, groups) as it:
                    for j in range(4):
                        sp.wait_ge(m_down, u0 + 8 * it + 2 * j - 6)
                        fill_dyn(m, 4 * it, j, (j + 3) % 4)
                q = m["pairs"]
                sp.wait_ge(m_down, u0 + 2 * (q - 4) + 2)
                fill(m, q, (q + 3) % 4)

            sp.wait_ge(a_mask, 2)
            sp.wait_ge(pool_ready, 1)
            sp.wait_ge(prepared, 3)
            sp.dma_start(stack_k[MASK_ROW:MASK_ROW + 1, :, :], mask_neg).then_inc(in_x, 16)
            sp.dma_start(stack_q[MASK_ROW:MASK_ROW + 1, :, :], ones16).then_inc(in_x, 16)
            for k in range(4):
                stack(0, k)
            moe_first(0)
            load(mats1[:, :], a["mats1"], in_mats1)
            load(lora[:, :], a["lora"], in_mats1)
            load(mats2[:, :], a["mats2"], in_mats2)
            load(select2[:, :, :, :], a["select2"], in_mats2)
            load(mats3[:, :], a["mats3"], in_mats3)
            if stages > 1:
                moe_rest(0)
            if stages > 5:
                sp.wait_ge(m_down, MOE[0]["units"])
                for e in range(4):
                    sp.dma_start(ring[:, e, :], a["experts2"][e]).then_inc(w_in[e], 16)
                for e in range(4, 8):
                    sp.wait_ge(e_x2, 2 * (e - 4) + 2)
                    sp.dma_start(ring[:, e - 4, :], a["experts2"][e]).then_inc(w_in[e - 4], 16)
            if stages > 6:
                sp.wait_ge(pool_ready, 7)
                sp.wait_ge(prepared, 6)
                for k in range(4):
                    stack(1, k)
            if stages > 7:
                sp.wait_ge(e_x2, 16)
                moe_first(1)
                moe_rest(1)
            for c in range(2):
                sp.wait_ge(x_updated, x_count(stages - 1, c))
                sp.dma_start(out[:, c * HALF:c * HALF + HALF], x[:, c, :]).then_inc(out_stored, 16)
            sp.wait_ge(out_stored, 32)

        @block.gpsimd
        def _(pool):
            def zero_stack():
                nc.gpsimd.memset(arena[64:128, 8192:16384], 0.0).then_inc(pool_ready, 1)

            def ones_around_v(inst):
                nc.gpsimd.memset(head_v[:, :], 0.0).then_inc(pool_ready, 1)
                pool.wait_ge(pool_ready, 2)
                spread = v_slots[:, :, 0:1152].rearrange("p g (h r) -> p g h r", r=144)
                nc.gpsimd.memset(spread[:, :, :, HD:16], 1.0).then_inc(pool_ready, 1)

            zero_stack()
            pool.wait_ge(pool_ready, 1)
            ones_around_v(0)

            def add_update(s, k, c, lo, width, n):
                pool.wait_ge(update_ready, n + 1)
                dst = x[:, c, lo:lo + width] if isinstance(lo, int) else x[:, c, ds(lo, width)]
                nc.gpsimd.tensor_tensor(dst, dst, upd[:, 0:width], ALU.add).then_inc(x_updated, 1)

            def attn_slots(inst, b):
                u0 = UNITS * (inst if inst < 2 else 0)
                spread = v_slots[:, :, 0:1152].rearrange("p g (h r) -> p g h r", r=144)
                src = v_tok[:, b, :] if isinstance(b, int) else v_tok[:, ds(b, 1), :].squeeze(1)
                nc.gpsimd.tensor_copy(spread[:, :, :, 0:HD],
                                      src.rearrange("p (g h d) -> p g h d", g=2, d=HD)).then_inc(a_slots, 1)

            def attn(inst, base_pv, base_slots, before):
                pool.wait_ge(a_vtok, 2 * inst + 2)
                attn_slots(inst, 0)

                def batch(b, last):
                    if not last:
                        pool.wait_ge(a_pv, base_pv + 4 * b + 4)
                        attn_slots(inst, b + 1)
                    pool.wait_ge(update_ready, before + b + 1)
                    xs = x[:, :, :].rearrange("p c t -> p (c t)")
                    dst = xs[:, ds(b * P, P)]
                    nc.gpsimd.tensor_tensor(dst, dst, upd[:, 0:P], ALU.add).then_inc(x_updated, 1)
                with pool.Fori(0, B - 1) as b:
                    batch(b, False)
                batch(B - 1, True)

            pool.wait_ge(in_x, 48)
            pool.wait_ge(pool_ready, 3)
            attn(0, 0, 0, 0)
            n = 8
            if stages > 1:
                for c in range(2):
                    add_update(1, 0, c, 0, HALF, n)
                    n += 1
            if stages > 2:
                for c in range(2):
                    add_update(2, 0, c, 0, HALF, n)
                    n += 1
            if stages > 3:
                pool.wait_ge(d_rowmax, 2)
                nc.gpsimd.partition_all_reduce(w_max[:, 2:4], w_max[:, 0:2], P, REDUCE_MAX).then_inc(d_max, 1)
                for c in range(2):
                    add_update(3, 0, c, 0, HALF, n)
                    n += 1
            if stages > 4:
                nc.gpsimd.memset(q_slot[0], 0.0).then_inc(pool_ready, 1)
                pool.wait_ge(a_pv, UNITS)
                nc.gpsimd.memset(q_slot[1], 0.0).then_inc(pool_ready, 1)
                pool.wait_ge(m_comb, 2)
                nc.gpsimd.memset(v2[:, :, 8, :], 1.0).then_inc(pool_ready, 1)
                with pool.Fori(0, B) as b:
                    pool.wait_ge(update_ready, 14 + b + 1)
                    xs = x[:, :, :].rearrange("p c t -> p (c t)")
                    dst = xs[:, ds(b * P, P)]
                    nc.gpsimd.tensor_tensor(dst, dst, upd[:, 0:P], ALU.add).then_inc(x_updated, 1)
                n += 8
            if stages > 5:
                pool.wait_ge(a_pv, 2 * UNITS)
                pool.wait_ge(x_updated, n)
                zero_stack()
                pool.wait_ge(pool_ready, 7)
                for e in range(8):
                    for c in range(2):
                        pool.wait_ge(e_v, 2 * e + c + 1)
                        if e == 0:
                            pool.wait_ge(e_z, 2)
                        if e > 0:
                            pool.wait_ge(e_y, 2 * (e - 1) + c + 1)
                        nc.gpsimd.tensor_tensor(cen[:, c, :], cen[:, c, :], wc[:, c, :], ALU.add)\
                            .then_inc(e_y, 1)
                for c in range(2):
                    add_update(5, 0, c, 0, HALF, n)
                    n += 1
            if stages > 6:
                nc.gpsimd.memset(head_v[:, :], 0.0).then_inc(pool_ready, 1)
                pool.wait_ge(pool_ready, 8)
                spread = v_slots[:, :, 0:1152].rearrange("p g (h r) -> p g h r", r=144)
                nc.gpsimd.memset(spread[:, :, :, HD:16], 1.0).then_inc(pool_ready, 1)
                pool.wait_ge(pool_ready, 9)
                attn(1, 2 * UNITS, 0, n)
                n += 8
            if stages > 7:
                for c in range(2):
                    add_update(7, 0, c, 0, HALF, n)
                    n += 1

        @block.tensor
        def _(pe):
            mm = nc.tensor.matmul

            def norm_stats(i, c, last_wait=None):
                src, dst, affine, (kind, s) = NORMS[i]
                if kind == "x" and s > 0:
                    pe.wait_ge(x_updated, x_count(s - 1, c))
                if kind == "x" and s == 0:
                    pe.wait_ge(in_x, 48)
                if kind == "xn":
                    pe.wait_ge(ln_out, 2 * NORM_OF[4][0] + c + 1)
                if i > 0:
                    pe.wait_ge(ln_out, 2 * (i - 1) + c + 1)
                mm(bank[c][:, :], mean_w[:, :], src(c), start=True, stop=True).then_inc(ln_mean, 1)

            def norm_var(i, c):
                pe.wait_ge(ln_sq, 2 * i + c + 1)
                for j in range(BH):
                    last = mm(bank[c][:, j * P:j * P + P], sq[:, c, j * P:j * P + P], mean_w[:, :],
                              start=True, stop=True)
                last.then_inc(ln_var, 1)

            def norm_spread(i, c):
                pe.wait_ge(ln_diag, 2 * i + c + 1)
                mm(bank[c][:, :], ones[:, :], diag[:, c, :], start=True, stop=True).then_inc(ln_spread, 1)

            def norm(i):
                for c in range(2):
                    norm_stats(i, c)
                for c in range(2):
                    norm_var(i, c)
                for c in range(2):
                    norm_spread(i, c)

            def prep(inst, k):
                n = 4 * inst + k
                w = A_MATS[inst][:, (0 if k < 2 else P):(P if k < 2 else 2 * P)]
                src = context if k < 2 else xn
                if k >= 2:
                    pe.wait_ge(ln_out, 2 * NORM_OF[A_STAGE[inst]][0] + k - 1)
                if n >= 2:
                    pe.wait_ge(a_first, n - 1)
                mm(bank[6 + k % 2][:, :], w, src[:, k % 2, :], start=True, stop=True).then_inc(a_proj, 1)

            def attn_v(inst):
                for c in range(2):
                    for j in range(BH):
                        last = mm(bank[4 + c][:, j * P:j * P + P], context[:, c, j * P:j * P + P],
                                  A_MATS[inst][:, 2 * P:3 * P], start=True, stop=True)
                    last.then_inc(a_vproj, 1)

            def units(base, bb, scores, probs_v, tail):
                def transposes(b, u):
                    pe.wait_ge(a_exp, base + 4 * b + u + 1)
                    if not (base == 0 and isinstance(b, int) and b == 0 and u < 2):
                        pe.wait_ge(a_ev, base + 4 * b + u - 1)
                    for j in range(4):
                        last = nc.tensor.transpose(bank[2 + u % 2][:, j * P:j * P + P],
                                                   wb[:, u % 2, j * P:j * P + P], ident[:, :])
                    last.then_inc(a_tr, 1)

                def batch(b, odd):
                    for u in range(4):
                        if u < 2:
                            scores(b, u + 2, odd)
                        elif not (isinstance(b, int) and b == B - 1):
                            scores(b + 1, u - 2, 1 - odd)
                        transposes(b, u)
                        if u > 0:
                            probs_v(b, u - 1)
                        elif beyond(b, 1):
                            probs_v(b - 1, 3)
                        if beyond(b, 1):
                            tail(b - 1, u)
                scores(0, 0, 0)
                scores(0, 1, 0)
                over_batches(pe, batch)
                probs_v(B - 1, 3)
                for u in range(4):
                    tail(B - 1, u)

            def attn(inst):
                base, bb = (0, 0) if inst == 0 else (2 * UNITS, B)
                tb, yb = B * inst, 2 * B * inst
                w = A_MATS[inst]
                pe.wait_ge(a_stacked[0], 288 * (inst + 1))
                pe.wait_ge(a_stacked[1], 288 * (inst + 1))
                if inst == 0:
                    pe.wait_ge(in_x, 80)
                    pe.wait_ge(in_consts, 64)

                def scores(b, u, half):
                    if not (base == 0 and isinstance(b, int) and b == 0 and u < 2):
                        pe.wait_ge(a_sub, base + 4 * b + u - 1)
                    for j in range(4):
                        tok = ds(b * P, P)
                        last = mm(bank[u % 2][:, j * P:j * P + P], stack_q[:, 4 * u + j, tok],
                                  stack_k[:, 4 * u + j, tok], start=True, stop=True)
                    last.then_inc(a_s, 1)

                def probs_v(b, u):
                    pe.wait_ge(a_ev, base + 4 * b + u + 1)
                    if u == 0:
                        pe.wait_ge(a_slots, bb + b + 1)
                        if not (tb == 0 and isinstance(b, int) and b == 0):
                            pe.wait_ge(a_ocopy, tb + b)
                    g = u // 2
                    for j in range(4):
                        h = 4 * (u % 2) + j
                        last = mm(bank[4][:, g * P:g * P + P], v_slots[:, g, h * P:h * P + P],
                                  wc[:, u % 2, j * P:j * P + P], start=(h == 0), stop=(h == 7))
                    last.then_inc(a_pv, 1)

                def tail(b, u):
                    if u == 1:
                        pe.wait_ge(a_ocopy, tb + b + 1)
                        if beyond(b, 1) or tb > 0:
                            pe.wait_ge(a_norm, tb + b)
                        for g in range(2):
                            last = nc.tensor.transpose(bank[5][:, g * P:g * P + P], o_sb[:, g, :], ident[:, :])
                        last.then_inc(a_turned, 1)
                    if u == 2:
                        pe.wait_ge(a_norm, tb + b + 1)
                        if beyond(b, 1) or yb > 0:
                            pe.wait_ge(a_ofm, yb + b)
                        nc.tensor.transpose(bank[6][:, 0:P], o_tok[:, :], ident[:, :]).then_inc(a_back, 1)
                    if u == 3:
                        pe.wait_ge(a_ofm, yb + b + 1)
                        if beyond(b, 1) or yb > 0:
                            pe.wait_ge(update_ready, (0 if inst == 0 else x_count(5, 1)) + b)
                        mm(bank[7][:, 0:P], w[:, 3 * P:4 * P], o_fm[:, 0, :], start=True, stop=True)\
                            .then_inc(a_y, 1)
                units(base, bb, scores, probs_v, tail)

            def bias_through_o(inst):
                vb = A_BIAS[inst][2]
                mm(bank[7][:, 0:1], A_MATS[inst][:, 3 * P:4 * P], col(vb), start=True, stop=True)\
                    .then_inc(o_bias, 1)

            def moe(n):
                m = MOE[n]
                u0, kt = moe_units_until(n), m["KT"]
                for c in range(2):
                    pe.wait_ge(ln_out, 2 * NORM_OF[m["stage"]][0] + c + 1)
                    for j in range(BH):
                        last = mm(bank[4 + c][:, j * P:j * P + P], xn[:, c, j * P:j * P + P],
                                  m["mats"][:, m["at"]:m["at"] + P], start=True, stop=True)
                    last.then_inc(m_logit, 1)
                for c in range(2):
                    mm(bank[6 + c][:, :], zeros_bf[:, 0:P], zeros_bf[:, :], start=True, stop=False)

                def front(slot, c, weighed, fill_count):
                    pe.wait_ge(w_in[slot], fill_count)
                    mm(bank[c][:, :], ring[:, slot, 0:P], xn[:, c, :], start=True, stop=True)\
                        .then_inc(m_g, 1)
                    mm(bank[2 + c][:, :], ring[:, slot, P:2 * P], xn[:, c, :], start=True, stop=True)\
                        .then_inc(m_u, 1)
                    if weighed:
                        for k in range(kt):
                            last = mm(bank[4 + c][:, :], ring_sel[:, slot, k, :],
                                      comb_t[:, k, c * HALF:c * HALF + HALF],
                                      start=(k == 0), stop=(k == kt - 1))
                        last.then_inc(m_cb, 1)

                def down(slot, c, unit, stop=False):
                    pe.wait_ge(m_h, unit + 1)
                    mm(bank[6 + c][:, :], ring[:, slot, 2 * P:3 * P], wc[:, c, :],
                       start=False, stop=stop).then_inc(m_down, 1)

                def filled(slot, more):
                    before = 32 * sum(
                        1 for mm_ in MOE[:n] for q in range(mm_["pairs"] + 1) if (q + 3) % 4 == slot)
                    return before + (32 if n else 0) + 32 * more

                front(3, 0, False, filled(3, 1))
                front(3, 1, False, filled(3, 1))
                down(3, 0, u0)
                for c in range(2):
                    pe.wait_ge(m_comb, 4 * n + c + 1)
                    for k in range(kt):
                        for j in range(BH):
                            last = nc.tensor.transpose(
                                bank[4 + c][:, :].bitcast(bf16)[:, (k * BH + j) * P:(k * BH + j) * P + P],
                                comb_pieces[:, BH * c + j, k * P:k * P + P], ident_bf[:, :])
                    last.then_inc(m_combT, 1)
                pe.wait_ge(m_combE, 4 * n + 2)
                with pe.Fori(0, m["pairs"] // 4) as it:
                    for k in range(8):
                        slot, c = k // 2, k % 2
                        front(slot, c, True, filled(slot, 0) + 32 * it + (64 if slot == 3 else 32))
                        down((slot + 3) % 4 if c == 0 else slot, 1 - c, u0 + 8 * it + k + 1)
                mm(bank[6][:, :], zeros_bf[:, 0:P], zeros_bf[:, :], start=False, stop=True)\
                    .then_inc(m_zero, 1)
                down(3, 1, u0 + m["units"] - 1, stop=True)

            pe.wait_ge(in_ctx, 64)
            pe.wait_ge(prepared, 5)
            prep(0, 0)
            prep(0, 1)
            norm(0)
            attn_v(0)
            prep(0, 2)
            prep(0, 3)
            pe.wait_ge(a_vtok, 2)
            pe.wait_ge(a_first, 4)
            bias_through_o(0)
            attn(0)
            if stages > 1:
                norm(NORM_OF[1][0])
                moe(0)
            if stages > 2:
                w = mats1
                pe.wait_ge(in_mats1, 32)
                norm(NORM_OF[2][0])
                pe.wait_ge(x_updated, x_count(1, 1))
                for c in range(2):
                    mm(bank[2 + c][:, :], w[:, P:2 * P], context[:, c, :], start=True, stop=True)\
                        .then_inc(b_proj, 1)
                for c in range(2):
                    for j in range(BH):
                        last = mm(bank[4 + c][:, j * P:j * P + P], context[:, c, j * P:j * P + P],
                                  w[:, 2 * P:3 * P], start=True, stop=True)
                    last.then_inc(b_v, 1)
                for c in range(2):
                    pe.wait_ge(ln_out, 2 * NORM_OF[2][0] + c + 1)
                    mm(bank[6 + c][:, :], w[:, 0:P], xn[:, c, :], start=True, stop=True).then_inc(b_proj, 1)
                for c in range(2):
                    pe.wait_ge(b_evac, c + 1)
                    mm(bank[2 + c][:, :], w[:, 3 * P:4 * P], xn[:, c, :], start=True, stop=True)\
                        .then_inc(b_proj, 1)
                for c in range(2):
                    pe.wait_ge(b_evac, 3 + c)
                    for j in range(BH):
                        last = mm(bank[c][:, j * P:j * P + P], q1[:, c, j * P:j * P + P],
                                  k1[:, c, j * P:j * P + P], start=True, stop=True)
                    last.then_inc(b_s, 1)
                pe.wait_ge(b_vev, 2)
                for c in range(2):
                    pe.wait_ge(b_n, c + 1)
                    for j in range(BH):
                        last = nc.tensor.transpose(bank[4 + c][:, j * P:j * P + P],
                                                   wb[:, c, j * P:j * P + P], ident[:, :])
                    last.then_inc(b_tr, 1)
                for c in range(2):
                    pe.wait_ge(b_pt, c + 1)
                    for j in range(BH):
                        last = mm(bank[6 + c][:, j * P:j * P + P], v1[:, BH * c + j, :],
                                  wc[:, c, j * P:j * P + P], start=True, stop=True)
                    last.then_inc(b_pv, 1)
                for c in range(2):
                    pe.wait_ge(b_ctx, c + 1)
                    mm(bank[c][:, :], w[:, 4 * P:5 * P], wa[:, c, :], start=True, stop=True)\
                        .then_inc(b_y, 1)
            if stages > 3:
                for c in range(2):
                    pe.wait_ge(update_ready, 12)
                mm(bank[2][:, :], lora[:, 0:P], lora[:, P:5 * P], start=True, stop=True).then_inc(d_lora, 1)
                for j in range(4):
                    last = mm(bank[3][:, j * P:j * P + P], lora[:, 5 * P + j * P:5 * P + j * P + P],
                              lora[:, 9 * P:10 * P], start=True, stop=True)
                last.then_inc(d_lora, 1)
                norm(NORM_OF[3][0])
                pe.wait_ge(d_w, 2)
                for c in range(2):
                    pe.wait_ge(ln_out, 2 * NORM_OF[3][0] + c + 1)

                def up(m_):
                    f, c = m_ // 2, m_ % 2
                    if m_ >= 4:
                        pe.wait_ge(d_act, m_ - 3)
                    mm(bank[2 + m_ % 4][:, :], mats1[:, (5 + f) * P:(6 + f) * P], xn[:, c, :],
                       start=True, stop=True).then_inc(d_up, 1)

                up(0)
                up(1)
                for m_ in range(8):
                    f, c = m_ // 2, m_ % 2
                    if m_ + 2 < 8:
                        up(m_ + 2)
                    pe.wait_ge(d_act, m_ + 1)
                    mm(bank[6 + c][:, :], mats1[:, (9 + f) * P:(10 + f) * P], hidden1(m_),
                       start=(f == 0), stop=(f == 3)).then_inc(d_down, 1)
            if stages > 4:
                w = mats2
                pe.wait_ge(in_mats2, 32)
                i0, i1, i2 = NORM_OF[4]
                norm(i0)
                norm(i1)
                norm(i2)
                pe.wait_ge(update_ready, 14)
                n = 0

                def put(n):
                    if n >= 6:
                        pe.wait_ge(c_kq[n % 2], (n - 6) // 2 + 1)
                    return bank[2 + n % 6]
                flat = latents[:, :, :, :].rearrange("p b s t -> p (b s t)")
                for c in range(2):
                    pe.wait_ge(ln_out, 2 * i2 + c + 1)
                    for m_ in range(4):
                        for g in range(2):
                            gg = 2 * c + g
                            mm(put(n)[:, :], w[:, (4 + m_) * P:(5 + m_) * P],
                               flat[:, gg * 512:gg * 512 + 512], start=True, stop=True).then_inc(c_proj, 1)
                            n += 1
                    for m_ in range(4):
                        mm(put(n)[:, :], w[:, m_ * P:(m_ + 1) * P],
                           latents[:, BH * c:BH * c + BH, 1, :], start=True, stop=True)\
                            .then_inc(c_proj, 1)
                        n += 1
                    for t in range(8):
                        tile = 8 * c + t
                        mm(put(n)[:, :], flat[:, tile * P:tile * P + P], w[:, 8 * P:12 * P],
                           start=True, stop=True).then_inc(c_proj, 1)
                        n += 1
                for k in range(2):
                    pe.wait_ge(c_kq[k], 20)
                pe.wait_ge(pool_ready, 6)
                base, bb = UNITS, B

                def scores2(b, u, half):
                    if u == 0:
                        pe.wait_ge(c_slot, 4 * b + 4)
                    pe.wait_ge(a_sub, base + 4 * b + u - 1)
                    for j in range(2):
                        last = mm(bank[u % 2][:, j * 256:j * 256 + 256], q_slot[half][:, u, j, :],
                                  k2[:, u, ds(b, 1), :].squeeze(1), start=True, stop=True)
                    last.then_inc(a_s, 1)

                def probs_v2(b, u):
                    pe.wait_ge(a_ev, base + 4 * b + u + 1)
                    if u % 2 == 0 and beyond(b, 1):
                        pe.wait_ge(c_norm, 2 * b + u // 2 - 1)
                    for j in range(2):
                        h = 2 * u + j
                        for t in range(2):
                            v = v2[:, ds(2 * b + t, 1), h:9:8 - h, :].squeeze(1)
                            last = mm(bank[4 + u // 2][:, (2 * (u % 2) + j) * P:(2 * (u % 2) + j) * P + P],
                                      wc[:, u % 2, (2 * j + t) * P:(2 * j + t) * P + P], v,
                                      start=(t == 0), stop=(t == 1))
                    last.then_inc(a_pv, 1)

                def tail2(b, u):
                    if u == 2:
                        pe.wait_ge(c_norm, 2 * b + 2)
                        pe.wait_ge(a_ofm, B + b)
                        for g in range(4):
                            last = nc.tensor.transpose(bank[6][:, g * P:g * P + P], o_sb[:, g, :], ident[:, :])
                        last.then_inc(a_back, 1)
                    if u == 3:
                        pe.wait_ge(a_ofm, B + b + 1)
                        pe.wait_ge(update_ready, 14 + b)
                        for g in range(4):
                            last = mm(bank[7][:, 0:P], w[:, (12 + g) * P:(13 + g) * P], o_fm[:, g, :],
                                      start=(g == 0), stop=(g == 3))
                        last.then_inc(a_y, 1)
                units(base, bb, scores2, probs_v2, tail2)
            if stages > 5:
                w = mats2
                norm(NORM_OF[5][0])
                for c in range(2):
                    pe.wait_ge(ln_out, 2 * NORM_OF[5][0] + c + 1)
                    for j in range(BH):
                        last = mm(bank[4 + c][:, j * P:j * P + P], xn[:, c, j * P:j * P + P],
                                  w[:, 16 * P:17 * P], start=True, stop=True)
                    last.then_inc(m_logit, 1)
                def shared_down(k):
                    f, c = k // 2, k % 2
                    pe.wait_ge(e_sh, k + 1)
                    mm(bank[6 + c][:, :], w[:, (21 + f) * P:(22 + f) * P], wc[:, c, :],
                       start=(f == 0), stop=(f == 1)).then_inc(e_zd, 1)
                for f in range(2):
                    for c in range(2):
                        k = 2 * f + c
                        if k >= 2:
                            pe.wait_ge(e_sh, k - 1)
                        mm(bank[c][:, :], w[:, (17 + f) * P:(18 + f) * P], xn[:, c, :],
                           start=True, stop=True).then_inc(e_h1, 1)
                        mm(bank[2 + c][:, :], w[:, (19 + f) * P:(20 + f) * P], xn[:, c, :],
                           start=True, stop=True).then_inc(e_x3, 1)
                        if k >= 1:
                            shared_down(k - 1)
                shared_down(3)
                for c in range(2):
                    pe.wait_ge(m_comb, 2 + c + 1)
                    for j in range(BH):
                        last = nc.tensor.transpose(
                            bank[4 + c][:, :].bitcast(bf16)[:, j * P:j * P + P],
                            comb_pieces[:, BH * c + j, 0:P], ident_bf[:, :])
                    last.then_inc(m_combT, 1)
                pe.wait_ge(m_combE, 4)
                pe.wait_ge(e_z, 2)

                def late(e, c):
                    pe.wait_ge(e_h, 2 * e + c + 1)
                    if (e, c) != (0, 0):
                        pe.wait_ge(e_v, 2 * e + c)
                    mm(bank[6][:, :], ring[:, e % 4, 2 * P:3 * P], wb[:, c, :], start=True, stop=True)\
                        .then_inc(e_x2, 1)

                for e in range(8):
                    for c in range(2):
                        k = 2 * e + c
                        sel = comb_t[:, 0, c * HALF:c * HALF + HALF]
                        if k >= 1:
                            pe.wait_ge(e_xs, k)
                        mm(bank[4][:, :], select2[:, e, 0, :], sel, start=True, stop=True).then_inc(e_wb, 1)
                        if k >= 1:
                            late((k - 1) // 2, (k - 1) % 2)
                        pe.wait_ge(w_in[e % 4], fills2(e))
                        pe.wait_ge(e_xs, k + 1)
                        mm(bank[c][:, :], ring[:, e % 4, 0:P], wa[:, c, :], start=True, stop=True)\
                            .then_inc(e_h1, 1)
                        mm(bank[2 + c][:, :], ring[:, e % 4, P:2 * P], wa[:, c, :], start=True, stop=True)\
                            .then_inc(e_x3, 1)
                        if k >= 1:
                            pe.wait_ge(e_u, k)
                        mm(bank[5][:, :], select2[:, e, 1, :], sel, start=True, stop=True).then_inc(e_mk, 1)
                late(7, 1)
            if stages > 6:
                pe.wait_ge(in_mats3, 16)
                pe.wait_ge(e_v, 16)
                prep(1, 0)
                prep(1, 1)
                attn_v(1)
                norm(NORM_OF[6][0])
                prep(1, 2)
                prep(1, 3)
                pe.wait_ge(a_first, 8)
                pe.wait_ge(a_vtok, 4)
                bias_through_o(1)
                attn(1)
            if stages > 7:
                norm(NORM_OF[7][0])
                moe(1)

        @block.scalar
        def _(act):
            fn = nc.scalar.activation

            def norm(i):
                for c in range(2):
                    act.wait_ge(ln_cen, 2 * i + c + 1)
                    fn(sq[:, c, :], cen[:, c, :], ACT.Square).then_inc(ln_sq, 1)
                for c in range(2):
                    act.wait_ge(ln_var, 2 * i + c + 1)
                    fn(rstd[:, c, :], bank[c][:, :].rearrange("p (j m) -> p j m", j=BH)[:, :, 0],
                       ACT.Sqrt, bias=eps_col[:, :]).then_inc(ln_std, 1)

            def prep(inst, k):
                n = 4 * inst + k
                bias = col(A_BIAS[inst][0] if k < 2 else A_BIAS[inst][1])
                act.wait_ge(a_proj, n + 1)
                if n >= 2:
                    act.wait_ge(a_rest, n - 1)
                    act.wait_ge(a_stacked[n % 2], 144 * (n // 2))
                fn(wa[:, k % 2, :], bank[6 + k % 2][:, :], ACT.Identity, bias=bias).then_inc(a_full, 1)
                fn(pieces[:, n % 2, 0, :], bank[6 + k % 2][:, :], ACT.Identity, bias=bias)\
                    .then_inc(a_first, 1)

            def v_token_major(inst):
                for c in range(2):
                    act.wait_ge(a_vproj, 2 * inst + c + 1)
                    fn(v_tok[:, BH * c:BH * c + BH, :], bank[4 + c][:, :], ACT.Copy).then_inc(a_vtok, 1)

            def update(s, src, n, width):
                if n is not None:
                    act.wait_ge(x_updated, n)
                if s in (0, 2, 3, 6):
                    fn(upd[:, 0:width], src, ACT.Identity, bias=tgb[:, s:s + 1], scale=tg[:, s:s + 1])\
                        .then_inc(update_ready, 1)
                else:
                    fn(upd[:, 0:width], src, ACT.Copy, scale=tg[:, s:s + 1]).then_inc(update_ready, 1)

            def units(base, s, before, scale, y_before, turned):
                width = P if turned is not None else 4 * P

                def exp(b, u):
                    act.wait_ge(a_sub, base + 4 * b + u + 1)
                    if base > 0 or beyond(b, 1) or u > 1:
                        act.wait_ge(a_tr, base + 4 * b + u - 1)
                    fn(wb[:, u % 2, :], wa[:, u % 2, :], ACT.Exp, scale=scale).then_inc(a_exp, 1)

                def evac(b, u):
                    act.wait_ge(a_tr, base + 4 * b + u + 1)
                    if base > 0 or beyond(b, 1) or u > 1:
                        act.wait_ge(a_pv, base + 4 * b + u - 1)
                    fn(wc[:, u % 2, :], bank[2 + u % 2][:, :], ACT.Copy).then_inc(a_ev, 1)

                def copy_o(b):
                    act.wait_ge(a_pv, base + 4 * b + 4)
                    if turned > 0 or beyond(b, 1):
                        act.wait_ge(a_turned, turned + b)
                    fn(o_sb[:, 0:2, :], bank[4][:, 0:2 * P], ACT.Copy).then_inc(a_ocopy, 1)

                def copy_back(b):
                    act.wait_ge(a_back, y_before + b + 1)
                    if y_before > 0 or beyond(b, 1):
                        act.wait_ge(a_y, y_before + b)
                    fn(o_fm[:, 0:width // P, :], bank[6][:, 0:width], ACT.Copy).then_inc(a_ofm, 1)

                def batch_update(b):
                    act.wait_ge(a_y, y_before + b + 1)
                    update(s, bank[7][:, 0:P], before + b if before > 0 or beyond(b, 1) else None, P)

                def batch(b, odd):
                    for u in range(4):
                        if u < 3:
                            exp(b, u + 1)
                        elif not (isinstance(b, int) and b == B - 1):
                            exp(b + 1, 0)
                        if u == 0 and beyond(b, 2):
                            batch_update(b - 2)
                        if u == 3 and beyond(b, 1):
                            copy_back(b - 1)
                        evac(b, u)
                        if u == 0 and turned is not None and beyond(b, 1):
                            copy_o(b - 1)
                exp(0, 0)
                over_batches(act, batch)
                batch_update(B - 2)
                if turned is not None:
                    copy_o(B - 1)
                copy_back(B - 1)
                batch_update(B - 1)

            def moe(n):
                m = MOE[n]
                u0, s = moe_units_until(n), m["stage"]
                for c in range(2):
                    act.wait_ge(m_logit, 4 * n + c + 1)
                    fn(rt[:, c, 0:4 * m["E"]].rearrange("p (t e) -> p t e", t=4),
                       bank[4 + c][:, :].rearrange("p (t e) -> p t e", t=4)[:, :, 0:m["E"]],
                       ACT.Sigmoid).then_inc(m_score, 1)
                nc.scalar.preload_act_table(ACT.Silu)

                def silu(c, unit, first):
                    act.wait_ge(m_g, unit + 1)
                    if not first:
                        act.wait_ge(m_t, unit - 1)
                    fn(wa[:, c, :], bank[c][:, :], ACT.Silu).then_inc(m_silu, 1)
                silu(0, u0, n == 0)
                silu(1, u0 + 1, n == 0)
                with act.Fori(0, m["pairs"] // 4) as it:
                    for k in range(8):
                        silu(k % 2, u0 + 2 + 8 * it + k, False)
                before = x_count(s - 1, 1)
                for c in range(2):
                    if c == 0:
                        act.wait_ge(m_zero, n + 1)
                    else:
                        act.wait_ge(m_down, u0 + m["units"])
                    update(s, bank[6 + c][:, :], before + c, HALF)

            act.wait_ge(in_x, 48)
            fn(tg[:, :], gates[:, :], ACT.Tanh).then_inc(tg_ready, 1)
            act.wait_ge(in_ctx, 64)
            act.wait_ge(prepared, 4)
            prep(0, 0)
            prep(0, 1)
            norm(0)
            v_token_major(0)
            prep(0, 2)
            prep(0, 3)
            act.wait_ge(tgb_ready, 3)
            act.wait_ge(tg_ready, 1)
            nc.scalar.preload_act_table(ACT.Exp)
            units(0, 0, 0, SCALE_A, 0, 0)
            if stages > 1:
                norm(NORM_OF[1][0])
                moe(0)
            if stages > 2:
                norm(NORM_OF[2][0])
                for c in range(2):
                    act.wait_ge(b_proj, c + 1)
                    fn(k1[:, c, :], bank[2 + c][:, :], ACT.Identity, bias=col(K1B)).then_inc(b_evac, 1)
                for c in range(2):
                    act.wait_ge(b_proj, 3 + c)
                    fn(q1[:, c, :], bank[6 + c][:, :], ACT.Identity, bias=col(Q1B)).then_inc(b_evac, 1)
                for c in range(2):
                    act.wait_ge(b_proj, 5 + c)
                    fn(gate1[:, c, :], bank[2 + c][:, :], ACT.Sigmoid, bias=col(G1B)).then_inc(b_evac, 1)
                for c in range(2):
                    act.wait_ge(b_p, c + 1)
                    fn(wb[:, c, :], wa[:, c, :], ACT.Exp).then_inc(b_e, 1)
                for c in range(2):
                    act.wait_ge(b_tr, c + 1)
                    fn(wc[:, c, :], bank[4 + c][:, :], ACT.Copy).then_inc(b_pt, 1)
                for c in range(2):
                    act.wait_ge(b_y, c + 1)
                    update(2, bank[c][:, :], 10 + c, HALF)
            if stages > 3:
                norm(NORM_OF[3][0])
                for n in range(8):
                    act.wait_ge(d_up, n + 1)
                    if n >= 4:
                        act.wait_ge(d_down, n - 3)
                    fn(hidden1(n), bank[2 + n % 4][:, :], GELU, bias=col(FCB + n // 2)).then_inc(d_act, 1)
                for c in range(2):
                    act.wait_ge(d_down, 7 + c)
                    update(3, bank[6 + c][:, :], 12 + c, HALF)
            if stages > 4:
                for i in NORM_OF[4]:
                    norm(i)
                for n in range(0, 40, 2):
                    act.wait_ge(c_proj, n + 1)
                    dst, scale = product2(n)
                    fn(dst, bank2(n), ACT.Copy, scale=scale).then_inc(c_kq[0], 1)
                nc.scalar.preload_act_table(ACT.Exp)
                units(UNITS, 4, 14, 1.0, B, None)
            if stages > 5:
                norm(NORM_OF[5][0])
                for c in range(2):
                    act.wait_ge(m_shift, c + 1)
                    fn(rt[:, c, 0:32], rt[:, c, 0:32], ACT.Exp).then_inc(m_score, 1)
                for k in range(4):
                    act.wait_ge(e_h1, k + 1)
                    if k >= 2:
                        act.wait_ge(e_sh, k - 1)
                    fn(wb[:, k % 2, :], bank[k % 2][:, :], ACT.Silu).then_inc(e_sg, 1)
                act.wait_ge(e_sh, 4)
                for k in range(16):
                    e, c = k // 2, k % 2
                    act.wait_ge(e_h1, 4 + k + 1)
                    if k >= 2:
                        act.wait_ge(e_x2, k - 1)
                    fn(wb[:, c, :], bank[c][:, :], ACT.Silu, bias=col(B1 + e)).then_inc(e_h, 1)
                    act.wait_ge(e_x3, 4 + k + 1)
                    if k >= 2:
                        act.wait_ge(e_u, k - 1)
                    fn(sq[:, c, :], bank[2 + c][:, :], ACT.Identity, bias=col(B3 + e)).then_inc(e_x3b, 1)
                for c in range(2):
                    act.wait_ge(e_y, 15 + c)
                    update(5, cen[:, c, :], 22 + c, HALF)
            if stages > 6:
                prep(1, 0)
                prep(1, 1)
                v_token_major(1)
                norm(NORM_OF[6][0])
                prep(1, 2)
                prep(1, 3)
                act.wait_ge(tgb_ready, 4)
                nc.scalar.preload_act_table(ACT.Exp)
                units(2 * UNITS, 6, 24, SCALE_A, 2 * B, B)
            if stages > 7:
                norm(NORM_OF[7][0])
                moe(1)

        @block.vector
        def _(dve):
            v = nc.vector
            chain = [0]

            def link(ins):
                chain[0] += 1
                ins.then_inc(dve_chain, 1)
                dve.wait_ge(dve_chain, chain[0])

            def norm(i):
                src, dst, affine, _ = NORMS[i]
                for c in range(2):
                    dve.wait_ge(ln_mean, 2 * i + c + 1)
                    if i > 0:
                        dve.wait_ge(ln_out, 2 * (i - 1) + c + 1)
                    v.tensor_tensor(cen[:, c, :], src(c), bank[c][:, :], ALU.subtract).then_inc(ln_cen, 1)
                for c in range(2):
                    n = 2 * i + c + 1
                    dve.wait_ge(ln_std, n)
                    v.reciprocal(rstd[:, c, :], rstd[:, c, :]).then_inc(ln_inv, 1)
                    dve.wait_ge(ln_inv, n)
                    wide = [P, BH, P]
                    v.tensor_tensor(diag[:, c, :].rearrange("p (j m) -> p j m", j=BH),
                                    ident[:, :].unsqueeze(1).to_broadcast(wide),
                                    rstd[:, c, :].unsqueeze(2).to_broadcast(wide), ALU.mult)\
                        .then_inc(ln_diag, 1)
                for c in range(2):
                    dve.wait_ge(ln_spread, 2 * i + c + 1)
                    if affine is None:
                        v.tensor_tensor(dst(c), cen[:, c, :], bank[c][:, :], ALU.mult).then_inc(ln_out, 1)
                    else:
                        link(v.tensor_tensor(cen[:, c, :], cen[:, c, :], bank[c][:, :], ALU.mult))
                        v.tensor_scalar(dst(c), cen[:, c, :].rearrange("p (b t) -> p b t", b=BH),
                                        col(affine[0]), col(affine[1]), ALU.mult, ALU.add)\
                            .then_inc(ln_out, 1)

            def prep(inst, k):
                n = 4 * inst + k
                dve.wait_ge(a_full, n + 1)
                dve.wait_ge(a_first, n + 1)
                v.tensor_tensor(wb[:, k % 2, :], wa[:, k % 2, :], pieces[:, n % 2, 0, :], ALU.subtract)\
                    .then_inc(a_rest, 1)
                dve.wait_ge(a_rest, n + 1)
                v.tensor_copy(pieces[:, n % 2, 1, :], wb[:, k % 2, :]).then_inc(a_piece2, 1)
                dve.wait_ge(a_piece2, n + 1)
                v.tensor_tensor(pieces[:, n % 2, 2, :], wb[:, k % 2, :], pieces[:, n % 2, 1, :],
                                ALU.subtract).then_inc(a_split, 1)

            def units(base, heads, extra):
                def unit(b, u):
                    n = base + 4 * b + u
                    s = bank[u % 2][:, :].rearrange("p (h k) -> p h k", h=heads)
                    dve.wait_ge(a_s, n + 1)
                    v.tensor_reduce(row_max[:, u % 2, 0:heads], s, X, ALU.max).then_inc(a_max, 1)
                    dve.wait_ge(a_max, n + 1)
                    if base > 0 or beyond(b, 1) or u > 1:
                        dve.wait_ge(a_exp, n - 1)
                    v.tensor_tensor(wa[:, u % 2, :].rearrange("p (h k) -> p h k", h=heads), s,
                                    row_max[:, u % 2, 0:heads].unsqueeze(2)
                                    .to_broadcast([P, heads, 512 // heads]), ALU.subtract)\
                        .then_inc(a_sub, 1)

                def batch(b, odd):
                    for u in range(4):
                        unit(b, u)
                        extra(b, u, odd)
                over_batches(dve, batch)

            def attn(inst):
                base, tb = (0 if inst == 0 else 2 * UNITS), B * inst
                yb = 2 * B * inst

                def divide(b):
                    o = bank[5][:, 0:2 * P].rearrange("p (h s d) -> p h s d", h=HEADS, s=2)
                    dve.wait_ge(a_turned, tb + b + 1)
                    if tb > 0 or beyond(b, 1):
                        dve.wait_ge(a_norm, tb + b)
                    v.reciprocal(o_inv[:, :], o[:, :, 1, 0]).then_inc(a_inv, 1)
                    dve.wait_ge(a_inv, tb + b + 1)
                    if tb > 0 or beyond(b, 1):
                        dve.wait_ge(a_back, yb + b)
                    v.tensor_tensor(o_tok[:, :].rearrange("p (h d) -> p h d", h=HEADS), o[:, :, 0, :],
                                    o_inv[:, :].unsqueeze(2).to_broadcast([P, HEADS, HD]), ALU.mult)\
                        .then_inc(a_norm, 1)

                def extra(b, u, odd):
                    if u == 3 and beyond(b, 1):
                        divide(b - 1)
                units(base, 4, extra)
                divide(B - 1)

            def attn2():
                base = UNITS

                def q_fill(b, half):
                    tok = ds(b * P, P)
                    for j, rows in enumerate((slice(0, 64), slice(64, P))):
                        v.tensor_copy(q_slot[half][rows, 0:3, j, :], q2[rows, :, tok]).then_inc(c_slot, 1)
                        v.tensor_copy(q_slot[half][rows, 3, j, :], q2_last[rows, tok]).then_inc(c_slot, 1)

                def finish(b, p):
                    o = bank[4 + p][:, :].rearrange("p (h s d) -> p h s d", h=4, s=2)
                    dve.wait_ge(a_pv, base + 4 * b + 2 * p + 2)
                    if p > 0 or beyond(b, 1):
                        dve.wait_ge(c_norm, 2 * b + p)
                    v.reciprocal(o_inv[:, 0:4], o[:, :, 1, 0]).then_inc(c_rec, 1)
                    dve.wait_ge(c_rec, 2 * b + p + 1)
                    if p == 0:
                        dve.wait_ge(a_back, B + b)
                    v.tensor_tensor(o_sb[:, 2 * p:2 * p + 2, :].rearrange("p g (h d) -> p (g h) d", d=64),
                                    o[:, :, 0, :], o_inv[:, 0:4].unsqueeze(2).to_broadcast([P, 4, 64]),
                                    ALU.mult).then_inc(c_norm, 1)

                def extra(b, u, odd):
                    if u == 0 and beyond(b, 1):
                        finish(b - 1, 0)
                    if u == 1 and not (isinstance(b, int) and b == B - 1):
                        if beyond(b, 1):
                            dve.wait_ge(a_s, base + 4 * b)
                        q_fill(b + 1, 1 - odd)
                    if u == 2 and beyond(b, 1):
                        finish(b - 1, 1)
                dve.wait_ge(pool_ready, 5)
                for k in range(2):
                    dve.wait_ge(c_kq[k], 20)
                q_fill(0, 0)
                units(base, 2, extra)
                finish(B - 1, 0)
                finish(B - 1, 1)

            def ranks(vals, g, tri, s0):
                shape = [P, 4, g, g]
                def square(n):
                    return rt[:, n, 0:4 * g * g].rearrange("p (t i j) -> p t i j", t=4, i=g)
                mine = vals.unsqueeze(3).to_broadcast(shape)
                other = vals.unsqueeze(2).to_broadcast(shape)
                more, same = square(s0), square(s0 + 1)
                v.tensor_tensor(more, other, mine, ALU.is_gt)
                link(v.tensor_tensor(same, other, mine, ALU.is_equal))
                link(v.tensor_tensor(same, same, tri[:, :, :].unsqueeze(1).to_broadcast(shape), ALU.mult))
                link(v.tensor_tensor(more, more, same, ALU.add))
                rank = rt[:, s0 + 2, 0:4 * g].rearrange("p (t i) -> p t i", t=4)
                link(v.tensor_reduce(rank, more, X, ALU.add))
                return rank

            def grid(n, e):
                return rt[:, n, 0:4 * e].rearrange("p (t e) -> p t e", t=4)

            def split_weights(comb, e, c, tmp):
                rest = grid(tmp, e)
                dst = comb_pieces[:, BH * c:BH * c + BH, :]
                link(v.tensor_copy(dst[:, :, 0:e], comb))
                link(v.tensor_tensor(rest, comb, dst[:, :, 0:e], ALU.subtract))
                link(v.tensor_copy(dst[:, :, e:2 * e], rest))
                return v.tensor_tensor(dst[:, :, 2 * e:3 * e], rest, dst[:, :, e:2 * e], ALU.subtract)

            def route(n, c):
                m = MOE[n]
                E, G, K = m["E"], m["G"], m["K"]
                size = E // G
                dve.wait_ge(m_score, 4 * n + c + 1)
                score = grid(c, E)
                bias = route_bias[:, m["bias"]:m["bias"] + E].unsqueeze(1).to_broadcast([P, 4, E])
                biased = grid(2, E)
                link(v.tensor_tensor(biased, score, bias, ALU.add))
                groups = biased.rearrange("p t (g s) -> p t g s", g=G)
                best = grid(3, G)
                if n == 0:
                    pair = groups.rearrange("p t g (a b) -> p t g a b", a=2)
                    pair = biased.rearrange("p t (g a b) -> p (t g) a b", g=G, a=2)
                    hi = rt[:, 4, 0:32].rearrange("p (x a) -> p x a", a=2)
                    lo = rt[:, 5, 0:32].rearrange("p (x a) -> p x a", a=2)
                    v.tensor_tensor(hi, pair[:, :, :, 0], pair[:, :, :, 1], ALU.max)
                    link(v.tensor_tensor(lo, pair[:, :, :, 0], pair[:, :, :, 1], ALU.min))
                    t1, t2, t3 = (rt[:, k, 0:16] for k in (6, 7, 8))
                    v.tensor_tensor(t1, hi[:, :, 0], hi[:, :, 1], ALU.max)
                    v.tensor_tensor(t2, hi[:, :, 0], hi[:, :, 1], ALU.min)
                    link(v.tensor_tensor(t3, lo[:, :, 0], lo[:, :, 1], ALU.max))
                    link(v.tensor_tensor(t2, t2, t3, ALU.max))
                    link(v.tensor_tensor(rt[:, 3, 0:16], t1, t2, ALU.add))
                else:
                    link(v.tensor_reduce(best, groups, X, ALU.max))
                rank = ranks(best, G, m["tri"], 4)
                keep = grid(7, G)
                link(v.tensor_scalar(keep, rank, float(m["TG"]) - 0.5, None, ALU.is_lt))
                width = E + 8 - K
                ext = rt[:, 8, 0:4 * width].rearrange("p (t e) -> p t e", t=4)
                cut = rt[:, 9, 0:4 * width].rearrange("p (t e) -> p t e", t=4)
                v.memset(ext[:, :, E:width], 3e38)
                for t in range(4):
                    ins = v.tensor_tensor(ext[:, t, 0:E].rearrange("p (g s) -> p g s", g=G),
                                          groups[:, t, :, :],
                                          keep[:, t, :].unsqueeze(2).to_broadcast([P, G, size]), ALU.mult)
                link(ins)
                top = rt[:, 10, 0:32].rearrange("p (t k) -> p t k", t=4)
                for t in range(4):
                    ins = v.max(top[:, t, :], ext[:, t, :])
                link(ins)
                for t in range(4):
                    ins = v.match_replace(cut[:, t, :], top[:, t, :], ext[:, t, :], -3e38)
                link(ins)
                chosen = grid(11, E)
                link(v.tensor_scalar(chosen, cut[:, :, 0:E], -1e38, None, ALU.is_lt))
                weight = score if n == 0 else ext[:, :, 0:E]
                picked = grid(12, E)
                link(v.tensor_tensor(picked, weight, chosen, ALU.mult))
                total = rt[:, 13, 0:4]
                link(v.tensor_reduce(total, picked, X, ALU.add))
                link(v.tensor_scalar(total, total, 1e-20 if n == 0 else 1e-8, None, ALU.add))
                link(v.reciprocal(total, total))
                link(v.tensor_tensor(picked, picked, total.unsqueeze(2).to_broadcast([P, 4, E]), ALU.mult))
                if n == 0:
                    link(v.tensor_scalar(picked, picked, 2.5, None, ALU.mult))
                split_weights(picked, E, c, 11).then_inc(m_comb, 1)

            def weights_out(n, c, kt):
                dve.wait_ge(m_combT, 2 * n + c + 1)
                v.tensor_copy(comb_t[:, 0:kt, c * HALF:c * HALF + HALF],
                              bank[4 + c][:, :].bitcast(bf16)[:, 0:kt * HALF]
                              .rearrange("p (k t) -> p k t", k=kt)).then_inc(m_combE, 1)

            def moe(n):
                m = MOE[n]
                u0, kt = moe_units_until(n), m["KT"]

                def products(c, unit, weighed, first):
                    dve.wait_ge(m_silu, unit + 1)
                    dve.wait_ge(m_u, unit + 1)
                    v.tensor_tensor(wb[:, c, :], wa[:, c, :], bank[2 + c][:, :], ALU.mult).then_inc(m_t, 1)
                    dve.wait_ge(m_t, unit + 1)
                    if not first:
                        dve.wait_ge(m_down, unit - 1)
                    if weighed:
                        dve.wait_ge(m_cb, unit - 2 * n - 1)
                        v.tensor_tensor(wc[:, c, :], wb[:, c, :], bank[4 + c][:, :], ALU.mult)\
                            .then_inc(m_h, 1)
                    else:
                        v.tensor_copy(wc[:, c, :], wb[:, c, :]).then_inc(m_h, 1)
                for c in range(2):
                    route(n, c)
                for c in range(2):
                    products(c, u0 + c, False, n == 0)
                for c in range(2):
                    weights_out(2 * n, c, kt)
                with dve.Fori(0, m["pairs"] // 4) as it:
                    for k in range(8):
                        products(k % 2, u0 + 2 + 8 * it + k, True, False)

            v.memset(mean_w[:, :], 1.0 / P).then_inc(prepared, 1)
            v.memset(zeros_bf[:, :], 0.0).then_inc(prepared, 1)
            v.memset(arena[64:128, 0:8192], 0.0).then_inc(prepared, 1)
            v.memset(eps_col[:, :], EPS).then_inc(prepared, 1)
            v.memset(ones[:, :], 1.0).then_inc(prepared, 1)
            v.memset(ones16, 1.0).then_inc(a_mask, 1)
            dve.wait_ge(in_x, 48)
            v.tensor_scalar(mask_neg, mask_u8, -1e30, None, ALU.mult).then_inc(a_mask, 1)
            prep(0, 0)
            prep(0, 1)
            dve.wait_ge(in_ctx, 64)
            norm(0)
            prep(0, 2)
            prep(0, 3)
            v.memset(comb_pieces[:, :, :], 0.0)
            dve.wait_ge(tg_ready, 1)
            v.tensor_tensor(tgb[:, 2:3], tg[:, 2:3], col(O1B), ALU.mult).then_inc(tgb_ready, 1)
            v.tensor_tensor(tgb[:, 3:4], tg[:, 3:4], col(PROJB), ALU.mult).then_inc(tgb_ready, 1)
            dve.wait_ge(o_bias, 1)
            v.tensor_scalar(tgb[:, 0:1], bank[7][:, 0:1], col(O0B), tg[:, 0:1], ALU.add, ALU.mult)\
                .then_inc(tgb_ready, 1)
            attn(0)
            if stages > 1:
                norm(NORM_OF[1][0])
                moe(0)
            if stages > 2:
                norm(NORM_OF[2][0])
                for c in range(2):
                    dve.wait_ge(b_v, c + 1)
                    v.tensor_copy(v1[:, BH * c:BH * c + BH, :], bank[4 + c][:, :]).then_inc(b_vev, 1)
                for c in range(2):
                    s = bank[c][:, :].rearrange("p (b k) -> p b k", b=BH)
                    wide = [P, BH, P]
                    dve.wait_ge(b_s, c + 1)
                    link(v.tensor_reduce(row_max[:, c, :], s, X, ALU.max))
                    v.tensor_tensor(wa[:, c, :].rearrange("p (b k) -> p b k", b=BH), s,
                                    row_max[:, c, :].unsqueeze(2).to_broadcast(wide),
                                    ALU.subtract).then_inc(b_p, 1)
                for c in range(2):
                    e = wb[:, c, :].rearrange("p (b k) -> p b k", b=BH)
                    dve.wait_ge(b_e, c + 1)
                    link(v.tensor_reduce(row_max[:, c, :], e, X, ALU.add))
                    link(v.reciprocal(row_max[:, c, :], row_max[:, c, :]))
                    v.tensor_tensor(e, e, row_max[:, c, :].unsqueeze(2).to_broadcast(wide), ALU.mult)\
                        .then_inc(b_n, 1)
                for c in range(2):
                    dve.wait_ge(b_pv, c + 1)
                    dve.wait_ge(b_evac, 5 + c)
                    v.scalar_tensor_tensor(wa[:, c, :], bank[6 + c][:, :], col(V1B), gate1[:, c, :],
                                           ALU.add, ALU.mult).then_inc(b_ctx, 1)
            if stages > 3:
                for n in range(2):
                    w = mats1[:, (5 + 4 * n) * P:(9 + 4 * n) * P]
                    v.tensor_reduce(w_max[:, n:n + 1], w, X, ALU.max, apply_absolute_value=True)\
                        .then_inc(d_rowmax, 1)
                dve.wait_ge(d_max, 1)
                scale, inv, neg = w_stat[:, 0:2], w_stat[:, 2:4], w_stat[:, 4:6]
                link(v.tensor_scalar(scale, w_max[:, 2:4], 1.0 / 127.0, None, ALU.mult))
                v.reciprocal(inv, scale)
                link(v.tensor_scalar(neg, scale, -1.0, None, ALU.mult))
                for n in range(2):
                    w = mats1[:, (5 + 4 * n) * P:(9 + 4 * n) * P]
                    s1, i1_, n1 = scale[:, n:n + 1], inv[:, n:n + 1], neg[:, n:n + 1]
                    q, e = sq[:, 0, :], sq[:, 1, :]
                    link(v.tensor_scalar(q, w, i1_, None, ALU.mult))
                    link(v.scalar_tensor_tensor(e, q, n1, w, ALU.mult, ALU.add))
                    link(v.scalar_tensor_tensor(q, e, i1_, q, ALU.mult, ALU.add))
                    link(v.tensor_scalar(q, q, ROUND, ROUND, ALU.add, ALU.subtract))
                    link(v.tensor_scalar(q, q, 127.0, -128.0, ALU.min, ALU.max))
                    link(v.scalar_tensor_tensor(e, q, s1, w, ALU.mult, ALU.subtract))
                    link(v.tensor_tensor(w, w, e, ALU.add))
                    dve.wait_ge(d_lora, n + 1)
                    v.scalar_tensor_tensor(w, bank[2 + n][:, :], 2.0, w, ALU.mult, ALU.add)\
                        .then_inc(d_w, 1)
                norm(NORM_OF[3][0])
            if stages > 4:
                for i in NORM_OF[4]:
                    norm(i)
                for n in range(1, 40, 2):
                    dve.wait_ge(c_proj, n + 1)
                    dst, scale = product2(n)
                    v.tensor_scalar(dst, bank2(n), scale, None, ALU.mult).then_inc(c_kq[1], 1)
                attn2()
            if stages > 5:
                v.memset(arena[64:128, 0:8192], 0.0).then_inc(prepared, 1)
                norm(NORM_OF[5][0])

                def softmax_route(c):
                    logits = bank[4 + c][:, :].rearrange("p (t e) -> p t e", t=4)[:, :, 0:8]
                    top = rt[:, 2 + c, 0:4]
                    dve.wait_ge(m_logit, 2 + c + 1)
                    link(v.tensor_reduce(top, logits, X, ALU.max))
                    v.tensor_tensor(grid(c, 8), logits, top.unsqueeze(2).to_broadcast([P, 4, 8]),
                                    ALU.subtract).then_inc(m_shift, 1)

                def pick(c):
                    dve.wait_ge(m_score, 2 + c + 1)
                    score, total = grid(c, 8), rt[:, 2 + c, 0:4]
                    link(v.tensor_reduce(total, score, X, ALU.add))
                    link(v.reciprocal(total, total))
                    link(v.tensor_tensor(score, score, total.unsqueeze(2).to_broadcast([P, 4, 8]), ALU.mult))
                    rank = ranks(score, 8, earlier8, 4)
                    v.tensor_scalar(comb_pieces[:, BH * c:BH * c + BH, 24:32], rank, 1.5, None, ALU.is_lt)
                    split_weights(score, 8, c, 8).then_inc(m_comb, 1)

                def shared(k):
                    dve.wait_ge(e_sg, k + 1)
                    dve.wait_ge(e_x3, k + 1)
                    if k >= 2:
                        dve.wait_ge(e_zd, k - 1)
                    v.tensor_tensor(wc[:, k % 2, :], wb[:, k % 2, :], bank[2 + k % 2][:, :], ALU.mult)\
                        .then_inc(e_sh, 1)
                for c in range(2):
                    softmax_route(c)
                for c in range(2):
                    pick(c)
                for k in range(4):
                    shared(k)
                for c in range(2):
                    dve.wait_ge(e_zd, 3 + c)
                    v.tensor_copy(cen[:, c, :], bank[6 + c][:, :]).then_inc(e_z, 1)
                for c in range(2):
                    weights_out(1, c, 1)

                def late(k):
                    e, c = k // 2, k % 2
                    dve.wait_ge(e_x2, k + 1)
                    dve.wait_ge(e_u, k + 1)
                    if k >= 2:
                        dve.wait_ge(e_y, k - 1)
                    v.scalar_tensor_tensor(wc[:, c, :], bank[6][:, :], col(B2 + e), diag[:, c, :],
                                           ALU.add, ALU.mult).then_inc(e_v, 1)
                for k in range(16):
                    e, c = k // 2, k % 2
                    dve.wait_ge(e_wb, k + 1)
                    if k >= 2:
                        dve.wait_ge(e_x3, 4 + k - 1)
                    v.tensor_tensor(wa[:, c, :], xn[:, c, :], bank[4][:, :], ALU.mult).then_inc(e_xs, 1)
                    if k >= 1:
                        late(k - 1)
                    dve.wait_ge(e_x3b, k + 1)
                    dve.wait_ge(e_mk, k + 1)
                    v.tensor_tensor(diag[:, c, :], sq[:, c, :], bank[5][:, :], ALU.mult).then_inc(e_u, 1)
                late(15)
            if stages > 6:
                prep(1, 0)
                prep(1, 1)
                norm(NORM_OF[6][0])
                prep(1, 2)
                prep(1, 3)
                dve.wait_ge(o_bias, 2)
                v.tensor_scalar(tgb[:, 6:7], bank[7][:, 0:1], col(O3B), tg[:, 6:7], ALU.add, ALU.mult)\
                    .then_inc(tgb_ready, 1)
                attn(1)
            if stages > 7:
                norm(NORM_OF[7][0])
                moe(1)




def kernel(**inputs):
    import numpy as _np
    import ml_dtypes as _ml
    import concourse.bacc as _bacc
    from concourse import mybir as _mybir
    from concourse.bass_utils import run_bass_kernel_spmd as _run

    I = {name: _np.asarray(value) for name, value in inputs.items()}
    P, T, D, HEADS, HD = 128, 1024, 128, 16, 8

    def columns(*vectors):
        return _np.stack(vectors, axis=1)

    def dim_major(w):
        return w.reshape(*w.shape[:-1], HEADS, HD).swapaxes(-1, -2).reshape(w.shape)

    def row_chunks(w):
        return w.reshape(-1, P, w.shape[1]).transpose(1, 0, 2).reshape(P, -1)

    def padded(w, width=P):
        return _np.pad(w, ((0, 0), (0, width - w.shape[1])))

    def expert_pairs(gate, up, down, shared_gate, shared_up, shared_down):
        e, i, h = gate.shape
        def in_major(w, shared):
            pairs = w.reshape(e // 2, 2 * i, h).transpose(0, 2, 1)
            return _np.concatenate([shared.T[None], pairs])
        downs = down.transpose(0, 2, 1).reshape(e // 2, 2 * i, h)
        downs = _np.concatenate([shared_down.T[None], downs])
        return _np.concatenate([in_major(gate, shared_gate), in_major(up, shared_up), downs], axis=2)

    qw, kw, vw = _np.split(I["L3_xattn_in_proj_weight"], 3, axis=0)
    qb, kb, vb = _np.split(I["L3_xattn_in_proj_bias"], 3)
    arrays = {
        "x_t": I["x"].reshape(T, D).T,
        "ctx_t": I["ctx_1024"].reshape(T, D).T,
        "mask": _np.broadcast_to(I["mask_BxS2_bk0"].reshape(1, T), (HEADS, T)).copy()
        .view(_np.int32),
        "gates": _np.broadcast_to(
            _np.stack([I["g_xattn"], I["g_ffn"]], axis=1).reshape(1, 8), (P, 8)),
        "mats0": _np.concatenate([
            dim_major(I["L0_xattn_Wk"]), dim_major(I["L0_xattn_Wq"]), I["L0_xattn_Wv"],
            I["L0_xattn_Wo"], padded(I["L0_ffn_router_weight"].T)], axis=1),
        "mats1": _np.concatenate([
            I["L1_xattn_Wq"], I["L1_xattn_Wk"], I["L1_xattn_Wv"], I["L1_xattn_Wg"], I["L1_xattn_Wo"],
            I["L1_ffn_W_fc"].T, row_chunks(I["L1_ffn_W_proj"].T)], axis=1),
        "lora": _np.concatenate([
            I["L1_ffn_A_fc"], I["L1_ffn_B_fc"].T, I["L1_ffn_A_proj"], I["L1_ffn_B_proj"].T], axis=1),
        "mats2": _np.concatenate([
            I["L2_xattn_Wq"], I["L2_xattn_Wkv"], row_chunks(I["L2_xattn_Wout"]),
            padded(I["L2_ffn_gate_w"].T), I["L2_ffn_sw1"].T, I["L2_ffn_sw2"].T,
            row_chunks(I["L2_ffn_sw3"].T)], axis=1),
        "mats3": _np.concatenate([
            dim_major(kw.T), dim_major(qw.T), vw.T, I["L3_xattn_out_w"].T,
            padded(I["L3_ffn_gate_w"].T)], axis=1),
        "cols": columns(
            dim_major(I["L0_xattn_bk"]), dim_major(I["L0_xattn_bq"]),
            I["L0_xattn_bv"], I["L0_xattn_bo"],
            dim_major(kb), dim_major(qb), vb, I["L3_xattn_out_b"],
            I["L1_xattn_bq"], I["L1_xattn_bk"], I["L1_xattn_bv"], I["L1_xattn_bg"], I["L1_xattn_bo"],
            *I["L1_ffn_b_fc"].reshape(4, P), I["L1_ffn_b_proj"],
            I["L2_xattn_ln_m_w"], I["L2_xattn_ln_m_b"], I["L2_xattn_ln_l_w"], I["L2_xattn_ln_l_b"],
            *I["L2_ffn_b1"], *I["L2_ffn_b2"], *I["L2_ffn_b3"]),
        "route_bias": _np.broadcast_to(_np.concatenate(
            [I["L0_ffn_e_bias"], I["L3_ffn_gate_bias"]]).reshape(1, -1), (P, 80)),
        "experts0": expert_pairs(*(I["L0_ffn_" + n] for n in (
            "gate_w", "up_w", "down_w", "sh_gate_w", "sh_up_w", "sh_down_w"))),
        "experts3": expert_pairs(*(I["L3_ffn_" + n] for n in (
            "eg_w", "eu_w", "ed_w", "sg_w", "su_w", "sd_w"))),
        "experts2": _np.concatenate([I["L2_ffn_" + n].transpose(0, 2, 1) for n in ("w1", "w3", "w2")], axis=2),
    }
    arrays.update(_constants(_np, _ml))
    arrays = {name: _np.ascontiguousarray(a) for name, a in arrays.items()}
    nc = _bacc.Bacc("TRN2", target_bir_lowering=False, num_devices=1)
    aps = {name: nc.dram_tensor("in_" + name, a.shape, _mybir.dt.from_np(a.dtype), kind="ExternalInput").ap()
           for name, a in arrays.items()}
    out = nc.dram_tensor("out_t", (D, T), _mybir.dt.float32, kind="ExternalOutput").ap()
    flamingo_kernel(nc, aps, out)
    r = _run(nc, [{"in_" + name: a for name, a in arrays.items()}], core_ids=[0])
    return _np.ascontiguousarray(r.results[0]["out_t"].T).reshape(8, 128, D)


def _constants(np, ml):
    P = 128
    bf16 = ml.bfloat16
    lane = np.arange(P)

    def expert_select(experts, ktiles):
        rows = np.arange(ktiles * P)
        pairs = np.zeros((1 + experts // 2, ktiles, P, P), bf16)
        for pair in range(experts // 2):
            mine = (rows[:, None] < 3 * experts) & (rows[:, None] % experts == 2 * pair + lane[None] // 64)
            pairs[1 + pair] = mine.reshape(ktiles, P, P)
        return pairs.transpose(0, 2, 1, 3)

    sel2 = np.zeros((8, 2, P, P), bf16)
    for e in range(8):
        for piece in range(3):
            sel2[e, 0, 8 * piece + e] = 1
        sel2[e, 1, 24 + e] = 1

    def earlier(n):
        return np.broadcast_to(np.tril(np.ones((n, n), np.float32), -1).reshape(1, n * n), (P, n * n))

    return {
        "ident": np.eye(P, dtype=np.float32),
        "ident_bf": np.eye(P, dtype=bf16),
        "earlier4": earlier(4), "earlier8": earlier(8),
        "select0": expert_select(16, 1), "select3": expert_select(64, 2),
        "select2": sel2.transpose(2, 0, 1, 3),
    }
```

```python
import concourse.bass as bass
from concourse import mybir
from contextlib import ExitStack



def flamingo_kernel(nc, a, out):
    f32, f32r, bf16 = mybir.dt.float32, mybir.dt.float32r, mybir.dt.bfloat16
    ACT, ALU, X = mybir.ActivationFunctionType, mybir.AluOpType, mybir.AxisListType.X
    ds = bass.ds

    P, T, B = 128, 1024, 8
    HALF = T // 2
    BH = B // 2
    HEADS, HD = 16, 8
    QUADS = HEADS // 4
    SPLIT = 3
    MASK_ROW = 96
    EPS = 1e-5
    GELU = ACT.Gelu
    REDUCE_MAX = bass.bass_isa.ReduceOp.max

    ctx = ExitStack()
    with ctx:
        def sb(name, shape, dt=f32):
            return ctx.enter_context(nc.sbuf_tensor(name, shape, dt))

        def signal(name):
            return ctx.enter_context(nc.semaphore(name))

        x = sb("x", [P, 2, HALF])
        context = sb("context", [P, 2, HALF])
        xn = sb("xn", [P, 2, HALF])
        latents = sb("latents", [P, B, 2, P])
        ident = sb("ident", [P, P])
        ident_bf = sb("ident_bf", [P, P], bf16)
        ones = sb("ones", [P, P])
        mean_w = sb("mean_w", [P, P])
        earlier4 = sb("earlier4", [P, 4, 4])
        earlier8 = sb("earlier8", [P, 8, 8])
        N0, N1, N2, N3 = (a[f"mats{n}"].shape[1] for n in range(4))
        mats0, mats1, mats2, mats3 = (sb(f"mats{n}", [P, w]) for n, w in enumerate((N0, N1, N2, N3)))
        lora = sb("lora", [16, 1280])
        cols = sb("cols", [P, a["cols"].shape[1]])
        gates = sb("gates", [P, 8])
        tg = sb("tg", [P, 8])
        tgb = sb("tgb", [P, 8])
        route_bias = sb("route_bias", [P, 80])
        mask_words = sb("mask_words", [HEADS, T // 4], mybir.dt.int32)
        mask_u8 = mask_words[:, :].bitcast(mybir.dt.uint8)
        latent_rows = latents[0:HEADS, :, :, :].rearrange("p b s t -> p (b s t)")
        mask_neg = latent_rows[:, 0:512].bitcast(bf16)
        ones16 = latent_rows[:, 512:1024].bitcast(bf16)
        arena = sb("arena", [P, 20480])
        arena_at = nc.sbuf_base - 4 * 20480
        stack_q = arena[:, 0:8192].bitcast(bf16).rearrange("p (h t) -> p h t", h=HEADS)
        stack_k = arena[:, 8192:16384].bitcast(bf16).rearrange("p (h t) -> p h t", h=HEADS)
        q1 = arena[:, 0:1024].rearrange("p (c t) -> p c t", c=2)
        k1 = arena[:, 1024:2048].rearrange("p (c t) -> p c t", c=2)
        gate1 = arena[:, 2048:3072].rearrange("p (c t) -> p c t", c=2)
        v1 = arena[:, 3072:4096].rearrange("p (b d) -> p b d", b=B)
        k2 = arena[:, 0:8192].rearrange("p (m b k) -> p m b k", m=4, b=B)
        q2 = arena[:, 8192:11264].rearrange("p (m t) -> p m t", m=3)
        v2 = arena[:, 11264:20480].rearrange("p (t s d) -> p t s d", t=2 * B, d=64)
        rt = arena[:, 16384:16384 + 14 * 288].rearrange("p (n v) -> p n v", n=14)
        v_tok = sb("v_tok", [P, B, P])
        head_v = sb("head_v", [P, 2304])
        v_slots = head_v[:, :].rearrange("p (g c) -> p g c", g=2)
        q2_last = head_v[:, 0:1024]
        q_slot = [sb("q_slot", [P, 4, 2, P])[:, :, :, :],
                  head_v[:, 1024:2048].rearrange("p (m j t) -> p m j t", m=4, j=2)]
        cen = sb("cen", [P, 2, HALF])
        sq = sb("sq", [P, 2, HALF])
        diag = sb("diag", [P, 2, HALF])
        rstd = sb("rstd", [P, 2, BH])
        wa, wb, wc = (sb(n, [P, 2, HALF]) for n in ("wa", "wb", "wc"))
        pieces = sb("pieces", [P, 2, SPLIT, HALF], bf16)
        row_max = sb("row_max", [P, 2, 4])
        o_sb = sb("o_sb", [P, 4, P])
        o_tok = sb("o_tok", [P, P])
        o_fm = sb("o_fm", [P, 4, P])
        o_inv = sb("o_inv", [P, 16])
        upd = sb("upd", [P, HALF])
        ring = sb("ring", [P, 4, 512])
        w_hi, w_lo = (nc.alloc_sbuf_tensor_at(name, [P, 4, 512], f32r, offset=arena_at + k * 8192)
                      for k, name in enumerate(("w_hi", "w_lo")))
        xn_hi, xn_lo, h_hi, h_lo = (
            nc.alloc_sbuf_tensor_at(name, [P, 2, HALF], f32r, offset=arena_at + 16384 + k * 4096)
            for k, name in enumerate(("xn_hi", "xn_lo", "h_hi", "h_lo")))
        select2 = sb("select2", [P, 8, 2, P], bf16)
        comb_pieces = sb("comb_pieces", [P, 8, P])
        comb_t = sb("comb_t", [P, T], f32r)
        comb_t2 = nc.alloc_sbuf_tensor_at("comb_t2", [P, T], bf16, offset=nc.sbuf_base - 4 * T)
        comb_pieces2 = comb_pieces[:, :, 0:64].bitcast(bf16)
        bank = [ctx.enter_context(nc.psum_tensor(f"bank{n}", [P, 512], f32)) for n in range(8)]

        in_ctx, in_x, in_consts, in_mats1, in_mats2, in_mats3 = (
            signal(n) for n in ("in_ctx", "in_x", "in_consts", "in_mats1", "in_mats2", "in_mats3"))
        prepared = signal("prepared")
        pool_ready = signal("pool_ready")
        tg_ready, tgb_ready = signal("tg_ready"), signal("tgb_ready")
        x_updated = signal("x_updated")
        update_ready = signal("update_ready")
        out_stored = signal("out_stored")
        ln_mean, ln_cen, ln_sq, ln_var, ln_std, ln_inv, ln_diag, ln_spread, ln_out = (
            signal(n) for n in ("ln_mean", "ln_cen", "ln_sq", "ln_var", "ln_std", "ln_inv",
                                "ln_diag", "ln_spread", "ln_out"))
        dve_chain = signal("dve_chain")

        K0B, Q0B, V0B, O0B, K3B, Q3B, V3B, O3B = range(8)
        Q1B, K1B, V1B, G1B, O1B, FCB, PROJB = 8, 9, 10, 11, 12, 13, 17
        LNMW, LNMB, LNLW, LNLB, B1, B2, B3 = 18, 19, 20, 21, 22, 30, 38

        def col(n):
            return cols[:, n:n + 1]

        PER_STAGE = [8, 2, 2, 2, 8, 2, 8, 2]

        def x_count(s, c):
            return sum(PER_STAGE[:s]) + PER_STAGE[s] * (c + 1) // 2

        def u_count(s):
            return sum(0 if k in (1, 5, 7) else PER_STAGE[k] for k in range(s))

        def whole(t):
            return lambda c: t[:, c, :]

        def latent_half(which):
            return lambda c: latents[:, BH * c:BH * c + BH, which, :]

        NORMS = []
        NORM_OF = {}
        for s in range(8):
            NORM_OF[s] = [len(NORMS)]
            NORMS.append((whole(x), whole(xn), None, ("x", s)))
            if s == 0:
                CTX_NORM = len(NORMS)
                NORMS.append((whole(context), latent_half(0), (LNMW, LNMB), ("ctx", s)))
            if s == 4:
                NORM_OF[s].append(len(NORMS))
                NORMS.append((whole(xn), latent_half(1), (LNLW, LNLB), ("xn", s)))

        A_STAGE = [0, 6]
        A_MATS = [mats0, mats3]
        A_BIAS = [(K0B, Q0B, V0B, O0B), (K3B, Q3B, V3B, O3B)]
        a_proj, a_full, a_first, a_rest, a_piece2, a_split = (
            signal(n) for n in ("a_proj", "a_full", "a_first", "a_rest", "a_piece2", "a_split"))
        a_stacked = [signal("a_stacked0"), signal("a_stacked1")]
        a_mask = signal("a_mask")
        a_vproj, a_vtok = signal("a_vproj"), signal("a_vtok")
        a_s, a_max, a_sub, a_exp, a_tr, a_ev, a_pv = (
            signal(n) for n in ("a_scores", "a_max", "a_shifted", "a_exp", "a_transposed",
                                "a_evacuated", "a_pv"))
        a_slots, a_ocopy, a_turned, a_inv, a_norm, a_back, a_ofm, a_y = (
            signal(n) for n in ("a_slots", "a_ocopy", "a_turned", "a_inverse", "a_normed", "a_back",
                                "a_ofm", "a_y"))
        UNITS = B * QUADS
        SCALE_A = HD ** -0.5

        c_proj, c_slot, c_rec, c_norm = (signal(n) for n in ("c_proj", "c_qslot", "c_rec", "c_norm"))
        c_kq = [signal("c_evac0"), signal("c_evac1")]
        o_bias = signal("o_bias")

        w_in = [signal(f"w_in{s}") for s in range(4)]
        m_logit, m_score, m_comb, m_combT, m_combE = (
            signal(n) for n in ("m_logit", "m_score", "m_comb", "m_comb_t", "m_comb_evac"))
        m_shift = signal("m_shift")
        m_g, m_u, m_cb, m_silu, m_t, m_h, m_h_hi, m_h_lo, m_down = (
            signal(n) for n in ("m_gate", "m_up", "m_weight", "m_silu", "m_prod", "m_hidden", "m_hidden_hi",
                                "m_hidden_lo", "m_down"))
        m_w_hi, m_w_lo, m_x_hi = (signal(n) for n in ("m_w_hi", "m_w_lo", "m_x_hi"))
        m_x_lo = [signal("m_x_lo0"), signal("m_x_lo1")]
        ORDER = [(0, 0), (1, 0), (0, 1), (1, 1), (2, 0), (3, 0), (2, 1), (3, 1)]
        LAST_USE = [2, 3, 6, 7]
        FIRST_ORDER = [(0, 0), (1, 0), (2, 0), (3, 0), (0, 1), (1, 1), (2, 1), (3, 1)]
        FIRST_LAST_USE = [4, 5, 6, 7]
        MOE = [
            dict(stage=1, E=16, G=4, TG=2, K=4, mats=mats0, at=4 * P, bias=0, tri=earlier4),
            dict(stage=7, E=64, G=8, TG=4, K=6, mats=mats3, at=4 * P, bias=16, tri=earlier8),
        ]
        for n, m in enumerate(MOE):
            m["n"] = n
            m["pairs"] = m["E"] // 2
            m["rounds"] = m["pairs"] // 4
            m["units"] = 2 * (m["pairs"] + 1)
            m["u0"] = MOE[0]["units"] if n else 0
            m["q0"] = MOE[0]["pairs"] + 1 if n else 0
            m["weights"], m["fill0"] = a["experts0" if n == 0 else "experts3"], []
        for slot in range(4):
            MOE[0]["fill0"].append(0)
            MOE[1]["fill0"].append(2 + sum(1 for q in range(MOE[0]["pairs"] + 1) if (q + 3) % 4 == slot))

        def over_rounds(engine, m, round_):
            round_(0, True, False)
            if m["rounds"] > 2:
                with engine.Fori(1, m["rounds"] - 1) as i:
                    round_(i, False, False)
            round_(m["rounds"] - 1, False, True)

        def fills2(e):
            before = sum(1 for q in range(MOE[0]["pairs"] + 1) if (q + 3) % 4 == e % 4)
            return 16 * (before + e // 4 + 1)

        b_proj, b_evac, b_v, b_vev, b_s, b_p, b_tr, b_pt, b_pv, b_ctx, b_y = (
            signal(n) for n in ("b_proj", "b_evac", "b_v", "b_vev", "b_scores", "b_probs", "b_tr",
                                "b_pt", "b_pv", "b_ctx", "b_y"))
        d_lora, d_up, d_act, d_down, d_rowmax, d_max, d_w = (
            signal(n) for n in ("d_lora", "d_up", "d_act", "d_down", "d_rowmax", "d_max", "d_w"))
        w_max = sb("w_max", [P, 4])
        e_wb, e_xs, e_h1, e_x3, e_mk, e_h, e_x3b, e_u, e_x2, e_v, e_y, e_z, e_sg, e_sh, e_zd = (
            signal(n) for n in ("e_wb", "e_xs", "e_h1", "e_x3", "e_mk", "e_h", "e_x3b", "e_u", "e_x2",
                                "e_v", "e_y", "e_z", "e_sg", "e_sh", "e_zdown"))
        b_e, b_n = signal("b_exp"), signal("b_probs_normed")
        eps_col = sb("eps_col", [P, 1])
        w_stat = sb("w_stat", [P, 6])
        ROUND = 1.5 * 2.0 ** 23

        def bank2(n):
            return bank[2 + n % 6][:, :]

        def product2(n):
            c, k = n // 20, n % 20
            if k < 8:
                m, g = k // 2, k % 2
                return k2[:, m, BH * c + 2 * g:BH * c + 2 * g + 2, :], 1.0
            if k < 11:
                return q2[:, k - 8, c * HALF:c * HALF + HALF], 64 ** -0.5
            if k == 11:
                return q2_last[:, c * HALF:c * HALF + HALF], 64 ** -0.5
            return v2[:, 8 * c + k - 12, 0:8, :], 1.0

        def over_batches(engine, batch):
            batch(0, 0)
            batch(1, 1)
            with engine.Fori(1, B // 2 - 1) as pair:
                batch(2 * pair, 0)
                batch(2 * pair + 1, 1)
            batch(B - 2, 0)
            batch(B - 1, 1)

        def beyond(b, k):
            return not isinstance(b, int) or b >= k

        def hidden1(n):
            return (wa if n % 4 < 2 else wb)[:, n % 2, :]

        def stack(engine, inst, k):
            n = 4 * inst + k
            half = k % 2
            dst = stack_k if k < 2 else stack_q
            for piece, written in enumerate((a_first, a_piece2, a_split)):
                engine.wait_ge(written, n + 1)
                for other in range(SPLIT):
                    row = HD * (SPLIT * other + piece if k < 2 else SPLIT * piece + other)
                    engine.dma_start(dst[row:row + HD, :, half * HALF:half * HALF + HALF],
                                     pieces[:, n % 2, piece, :]).then_inc(a_stacked[n % 2], 16)

        block = ctx.enter_context(nc.Block())

        @block.sync
        def _(sp):
            def load(dst, src, done):
                sp.dma_start(dst, src).then_inc(done, 16)

            halves = "p (c t) -> p c t"
            load(x[:, :, :], a["x_t"].rearrange(halves, c=2), in_x)
            load(context[:, :, :], a["ctx_t"].rearrange(halves, c=2), in_ctx)
            load(mats0[:, :], a["mats0"], in_ctx)
            load(gates[:, :], a["gates"], in_x)
            load(mask_words[:, :], a["mask"], in_x)
            load(cols[:, :], a["cols"], in_ctx)
            load(ident[:, :], a["ident"], in_ctx)
            load(ident_bf[:, :], a["ident_bf"], in_consts)
            load(earlier4[:, :, :], a["earlier4"].rearrange("p (i j) -> p i j", i=4), in_consts)
            load(earlier8[:, :, :], a["earlier8"].rearrange("p (i j) -> p i j", i=8), in_consts)
            load(route_bias[:, :], a["route_bias"], in_consts)

            def fill(m, q):
                sp.dma_start(ring[:, (q + 3) % 4, :], m["weights"][q]).then_inc(w_in[(q + 3) % 4], 16)

            def moe_first(m):
                for q in range(4):
                    fill(m, q)

            def moe_rest(m):
                with sp.Fori(1, m["rounds"]) as i:
                    for j in range(4):
                        slot = (j + 3) % 4
                        sp.wait_ge(m_w_lo, m["q0"] + 4 * i + j - 3)
                        sp.dma_start(ring[:, slot, :], m["weights"][ds(4 * i + j, 1), :, :].squeeze(0))\
                            .then_inc(w_in[slot], 16)
                sp.wait_ge(m_w_lo, m["q0"] + m["pairs"] - 3)
                fill(m, m["pairs"])

            sp.wait_ge(a_mask, 2)
            sp.wait_ge(pool_ready, 1)
            sp.dma_start(stack_k[MASK_ROW:MASK_ROW + 1, :, :], mask_neg).then_inc(in_x, 16)
            stack(sp, 0, 0)
            sp.wait_ge(pool_ready, 2)
            sp.dma_start(stack_q[MASK_ROW:MASK_ROW + 1, :, :], ones16).then_inc(in_x, 16)
            stack(sp, 0, 2)
            moe_first(MOE[0])
            load(mats1[:, :], a["mats1"], in_mats1)
            load(lora[:, :], a["lora"], in_mats1)
            load(mats2[:, :], a["mats2"], in_mats2)
            load(select2[:, :, :, :], a["select2"], in_mats2)
            load(mats3[:, :], a["mats3"], in_mats3)
            moe_rest(MOE[0])
            sp.wait_ge(m_w_lo, MOE[1]["q0"])
            for e in range(4):
                sp.dma_start(ring[:, e, 0:384], a["experts2"][e]).then_inc(w_in[e], 16)
            sp.wait_ge(pool_ready, 9)
            stack(sp, 1, 0)
            for e in range(4, 8):
                sp.wait_ge(e_x2, 2 * (e - 4) + 2)
                sp.dma_start(ring[:, e - 4, 0:384], a["experts2"][e]).then_inc(w_in[e - 4], 16)
            stack(sp, 1, 2)
            sp.wait_ge(e_x2, 16)
            moe_first(MOE[1])
            moe_rest(MOE[1])
            for c in range(2):
                sp.wait_ge(x_updated, x_count(7, c))
                sp.dma_start(out[:, c * HALF:c * HALF + HALF], x[:, c, :]).then_inc(out_stored, 16)
            sp.wait_ge(out_stored, 32)

        @block.gpsimd
        def _(pool):
            def zero_stacks():
                nc.gpsimd.memset(arena[64:128, 8192:16384], 0.0).then_inc(pool_ready, 1)
                nc.gpsimd.memset(arena[64:128, 0:8192], 0.0).then_inc(pool_ready, 1)

            def ones_around_v(inst):
                nc.gpsimd.memset(head_v[:, :], 0.0).then_inc(pool_ready, 1)
                pool.wait_ge(pool_ready, 3)
                spread = v_slots[:, :, 0:1152].rearrange("p g (h r) -> p g h r", r=144)
                nc.gpsimd.memset(spread[:, :, :, HD:16], 1.0).then_inc(pool_ready, 1)

            zero_stacks()
            pool.wait_ge(pool_ready, 2)
            ones_around_v(0)

            def moe(m):
                n, q0, u0 = m["n"], m["q0"], m["u0"]

                def rest(slot, q):
                    pool.wait_ge(m_w_hi, q + 1)
                    nc.gpsimd.tensor_tensor(w_lo[:, slot, 0:384], ring[:, slot, 0:384],
                                            w_hi[:, slot, 0:384].bitcast(f32), ALU.subtract).then_inc(m_w_lo, 1)

                def hidden_rest(k, v, older):
                    pool.wait_ge(m_h_hi, v + 1)
                    if older:
                        pool.wait_ge(m_down, v - 1)
                    nc.gpsimd.tensor_tensor(h_lo[:, k % 2, :], wc[:, k % 2, :], h_hi[:, k % 2, :].bitcast(f32),
                                            ALU.subtract).then_inc(m_h_lo, 1)

                rest(3, q0)
                rest(0, q0 + 1)
                pool.wait_ge(m_x_hi, 2 * n + 2)
                nc.gpsimd.tensor_tensor(xn_lo[:, 1, :], xn[:, 1, :], xn_hi[:, 1, :].bitcast(f32),
                                        ALU.subtract).then_inc(m_x_lo[1], 1)
                hidden_rest(0, u0, n > 0)
                rest(1, q0 + 2)
                hidden_rest(1, u0 + 1, n > 0)
                rest(2, q0 + 3)
                rest(3, q0 + 4)

                def round_(i, first, last):
                    v, q = u0 + 2 + 8 * i, q0 + 1 + 4 * i
                    for k in range(8):
                        if first and k in (6, 7):
                            rest(k - 6, q + k - 2)
                        if not (last and k == 7):
                            hidden_rest(k, v + k, True)
                        if k in (1, 2) and not first:
                            rest(k + 1, q + k + 1)
                        if k in (5, 6) and not (first or last):
                            rest(k - 5, q + k - 1)
                over_rounds(pool, m, round_)

            def attn_slots(inst, b):
                u0 = UNITS * (inst if inst < 2 else 0)
                spread = v_slots[:, :, 0:1152].rearrange("p g (h r) -> p g h r", r=144)
                src = v_tok[:, b, :] if isinstance(b, int) else v_tok[:, ds(b, 1), :].squeeze(1)
                nc.gpsimd.tensor_copy(spread[:, :, :, 0:HD],
                                      src.rearrange("p (g h d) -> p g h d", g=2, d=HD)).then_inc(a_slots, 1)

            def first_slots(inst):
                pool.wait_ge(a_vtok, 2 * inst + 2)
                attn_slots(inst, 0)

            def attn(inst, base_pv, before):
                stack(pool, inst, 3)

                def batch(b, last):
                    if not last:
                        pool.wait_ge(a_pv, base_pv + 4 * b + 4)
                        attn_slots(inst, b + 1)
                    pool.wait_ge(update_ready, before + b + 1)
                    xs = x[:, :, :].rearrange("p c t -> p (c t)")
                    dst = xs[:, ds(b * P, P)]
                    nc.gpsimd.tensor_tensor(dst, dst, upd[:, 0:P], ALU.add).then_inc(x_updated, 1)
                with pool.Fori(0, B - 1) as b:
                    batch(b, False)
                batch(B - 1, True)

            pool.wait_ge(in_x, 48)
            pool.wait_ge(pool_ready, 4)
            stack(pool, 0, 1)
            first_slots(0)
            attn(0, 0, 0)
            moe(MOE[0])
            pool.wait_ge(d_rowmax, 2)
            nc.gpsimd.partition_all_reduce(w_max[:, 2:4], w_max[:, 0:2], P, REDUCE_MAX).then_inc(d_max, 1)
            nc.gpsimd.memset(q_slot[0], 0.0).then_inc(pool_ready, 1)
            pool.wait_ge(a_pv, UNITS)
            nc.gpsimd.memset(q_slot[1], 0.0).then_inc(pool_ready, 1)
            pool.wait_ge(m_comb, 2)
            nc.gpsimd.memset(v2[:, :, 8, :], 1.0).then_inc(pool_ready, 1)
            with pool.Fori(0, B) as b:
                pool.wait_ge(update_ready, u_count(4) + b + 1)
                xs = x[:, :, :].rearrange("p c t -> p (c t)")
                dst = xs[:, ds(b * P, P)]
                nc.gpsimd.tensor_tensor(dst, dst, upd[:, 0:P], ALU.add).then_inc(x_updated, 1)
            pool.wait_ge(a_pv, 2 * UNITS)
            pool.wait_ge(x_updated, x_count(4, 1))
            zero_stacks()
            pool.wait_ge(pool_ready, 9)
            stack(pool, 1, 1)
            for e in range(8):
                for c in range(2):
                    pool.wait_ge(e_v, 2 * e + c + 1)
                    if e == 0:
                        pool.wait_ge(e_z, 2)
                    if e > 0:
                        pool.wait_ge(e_y, 2 * (e - 1) + c + 1)
                    nc.gpsimd.tensor_tensor(cen[:, c, :], cen[:, c, :], wc[:, c, :], ALU.add)\
                        .then_inc(e_y, 1)
            nc.gpsimd.memset(head_v[:, :], 0.0).then_inc(pool_ready, 1)
            pool.wait_ge(pool_ready, 10)
            spread = v_slots[:, :, 0:1152].rearrange("p g (h r) -> p g h r", r=144)
            nc.gpsimd.memset(spread[:, :, :, HD:16], 1.0).then_inc(pool_ready, 1)
            pool.wait_ge(pool_ready, 11)
            first_slots(1)
            attn(1, 2 * UNITS, u_count(6))
            moe(MOE[1])

        @block.tensor
        def _(pe):
            mm = nc.tensor.matmul

            def norm_stats(i, c):
                src, dst, affine, (kind, s) = NORMS[i]
                if kind == "x" and s > 0:
                    pe.wait_ge(x_updated, x_count(s - 1, c))
                if kind == "x" and s == 0:
                    pe.wait_ge(in_x, 48)
                if kind == "xn":
                    pe.wait_ge(ln_out, 2 * NORM_OF[4][0] + c + 1)
                if i > 0:
                    pe.wait_ge(ln_out, 2 * (i - 1) + c + 1)
                mm(bank[c][:, :], mean_w[:, :], src(c), start=True, stop=True).then_inc(ln_mean, 1)

            def norm_var(i, c):
                pe.wait_ge(ln_sq, 2 * i + c + 1)
                for j in range(BH):
                    last = mm(bank[c][:, j * P:j * P + P], sq[:, c, j * P:j * P + P], mean_w[:, :],
                              start=True, stop=True)
                last.then_inc(ln_var, 1)

            def norm_spread(i, c):
                pe.wait_ge(ln_diag, 2 * i + c + 1)
                mm(bank[c][:, :], ones[:, :], diag[:, c, :], start=True, stop=True).then_inc(ln_spread, 1)

            def norm_means(i):
                for c in range(2):
                    norm_stats(i, c)

            def norm_rest(i):
                for c in range(2):
                    norm_var(i, c)
                for c in range(2):
                    norm_spread(i, c)

            def norm(i):
                norm_means(i)
                norm_rest(i)

            def prep(inst, k):
                n = 4 * inst + k
                w = A_MATS[inst][:, (0 if k < 2 else P):(P if k < 2 else 2 * P)]
                src = context if k < 2 else xn
                if k >= 2:
                    pe.wait_ge(ln_out, 2 * NORM_OF[A_STAGE[inst]][0] + k - 1)
                if n >= 2:
                    pe.wait_ge(a_first, n - 1)
                mm(bank[6 + k % 2][:, :], w, src[:, k % 2, :], start=True, stop=True).then_inc(a_proj, 1)

            def attn_v(inst):
                for c in range(2):
                    for j in range(BH):
                        last = mm(bank[4 + c][:, j * P:j * P + P], context[:, c, j * P:j * P + P],
                                  A_MATS[inst][:, 2 * P:3 * P], start=True, stop=True)
                    last.then_inc(a_vproj, 1)

            def units(base, bb, scores, probs_v, tail):
                def transposes(b, u):
                    pe.wait_ge(a_exp, base + 4 * b + u + 1)
                    if not (base == 0 and isinstance(b, int) and b == 0 and u < 2):
                        pe.wait_ge(a_ev, base + 4 * b + u - 1)
                    for j in range(4):
                        last = nc.tensor.transpose(bank[2 + u % 2][:, j * P:j * P + P],
                                                   wb[:, u % 2, j * P:j * P + P], ident[:, :])
                    last.then_inc(a_tr, 1)

                def batch(b, odd):
                    for u in range(4):
                        if u < 2:
                            scores(b, u + 2, odd)
                        elif not (isinstance(b, int) and b == B - 1):
                            scores(b + 1, u - 2, 1 - odd)
                        transposes(b, u)
                        if u > 0:
                            probs_v(b, u - 1)
                        elif beyond(b, 1):
                            probs_v(b - 1, 3)
                        if beyond(b, 1):
                            tail(b - 1, u)
                scores(0, 0, 0)
                scores(0, 1, 0)
                over_batches(pe, batch)
                probs_v(B - 1, 3)
                for u in range(4):
                    tail(B - 1, u)

            def attn(inst):
                base, bb = (0, 0) if inst == 0 else (2 * UNITS, B)
                tb, yb = B * inst, 2 * B * inst
                w = A_MATS[inst]
                pe.wait_ge(a_stacked[0], 288 * (inst + 1))
                if inst == 0:
                    pe.wait_ge(ln_out, 2 * CTX_NORM + 2)
                if inst == 0:
                    pe.wait_ge(in_x, 80)
                    pe.wait_ge(in_consts, 64)

                def scores(b, u, half):
                    if isinstance(b, int) and (b, u) == (2, 0):
                        pe.wait_ge(a_stacked[1], 288 * (inst + 1))
                    if not (base == 0 and isinstance(b, int) and b == 0 and u < 2):
                        pe.wait_ge(a_sub, base + 4 * b + u - 1)
                    for j in range(4):
                        tok = ds(b * P, P)
                        last = mm(bank[u % 2][:, j * P:j * P + P], stack_q[:, 4 * u + j, tok],
                                  stack_k[:, 4 * u + j, tok], start=True, stop=True)
                    last.then_inc(a_s, 1)

                def probs_v(b, u):
                    pe.wait_ge(a_ev, base + 4 * b + u + 1)
                    if u == 0:
                        pe.wait_ge(a_slots, bb + b + 1)
                        if not (tb == 0 and isinstance(b, int) and b == 0):
                            pe.wait_ge(a_ocopy, tb + b)
                    g = u // 2
                    for j in range(4):
                        h = 4 * (u % 2) + j
                        last = mm(bank[4][:, g * P:g * P + P], v_slots[:, g, h * P:h * P + P],
                                  wc[:, u % 2, j * P:j * P + P], start=(h == 0), stop=(h == 7))
                    last.then_inc(a_pv, 1)

                def tail(b, u):
                    if u == 1:
                        pe.wait_ge(a_ocopy, tb + b + 1)
                        if beyond(b, 1) or tb > 0:
                            pe.wait_ge(a_norm, tb + b)
                        for g in range(2):
                            last = nc.tensor.transpose(bank[5][:, g * P:g * P + P], o_sb[:, g, :], ident[:, :])
                        last.then_inc(a_turned, 1)
                    if u == 2:
                        pe.wait_ge(a_norm, tb + b + 1)
                        if beyond(b, 1) or yb > 0:
                            pe.wait_ge(a_ofm, yb + b)
                        nc.tensor.transpose(bank[6][:, 0:P], o_tok[:, :], ident[:, :]).then_inc(a_back, 1)
                    if u == 3:
                        pe.wait_ge(a_ofm, yb + b + 1)
                        if beyond(b, 1) or yb > 0:
                            pe.wait_ge(update_ready, u_count(A_STAGE[inst]) + b)
                        mm(bank[7][:, 0:P], w[:, 3 * P:4 * P], o_fm[:, 0, :], start=True, stop=True)\
                            .then_inc(a_y, 1)
                units(base, bb, scores, probs_v, tail)

            def bias_through_o(inst):
                vb = A_BIAS[inst][2]
                mm(bank[7][:, 0:1], A_MATS[inst][:, 3 * P:4 * P], col(vb), start=True, stop=True)\
                    .then_inc(o_bias, 1)

            def moe(m):
                n, u0, q0 = m["n"], m["u0"], m["q0"]
                for c in range(2):
                    pe.wait_ge(ln_out, 2 * NORM_OF[m["stage"]][0] + c + 1)
                    for j in range(BH):
                        last = mm(bank[4 + c][:, j * P:j * P + P], xn[:, c, j * P:j * P + P],
                                  m["mats"][:, m["at"]:m["at"] + P], start=True, stop=True)
                    last.then_inc(m_logit, 1)

                def product(out, w, w_rest, x_, x_rest, start=True, stop=True):
                    mm(out, w, x_, start=start, stop=False)
                    mm(out, w, x_rest, start=False, stop=False)
                    return mm(out, w_rest, x_, start=False, stop=stop)

                def gate_up(slot, c, k, unit, pair, older):
                    pe.wait_ge(m_w_lo, pair + 1)
                    if older:
                        pe.wait_ge(m_h, unit - 1)
                    for col_, bank_, done in ((0, bank[k % 2], m_g), (P, bank[2 + k % 2], m_u)):
                        product(bank_[:, :], w_hi[:, slot, col_:col_ + P], w_lo[:, slot, col_:col_ + P],
                                xn_hi[:, c, :], xn_lo[:, c, :]).then_inc(done, 1)

                def weight(slot, c, k):
                    mm(bank[4 + k % 2][:, :], w_hi[:, slot, 384:512], comb_t[:, c * HALF:c * HALF + HALF],
                       start=True, stop=True).then_inc(m_cb, 1)

                def down(slot, c, k, unit, start=False, stop=False):
                    pe.wait_ge(m_h_lo, unit + 1)
                    product(bank[6 + c][:, :], w_hi[:, slot, 256:384], w_lo[:, slot, 256:384],
                            h_hi[:, k % 2, :], h_lo[:, k % 2, :], start, stop).then_inc(m_down, 1)

                def combine_t(c):
                    pe.wait_ge(m_comb, 4 * n + c + 1)
                    if c == 1:
                        pe.wait_ge(m_h, u0 + 4)
                    for j in range(BH):
                        last = nc.tensor.transpose(bank[4 + c][:, j * P:j * P + P],
                                                   comb_pieces[:, BH * c + j, :], ident[:, :])
                    last.then_inc(m_combT, 1)

                def round_(i, first, last):
                    v = u0 + 2 + 8 * i
                    order = FIRST_ORDER if first else ORDER
                    for k, (slot, c) in enumerate(order):
                        if first and k < 2:
                            continue
                        gate_up(slot, c, k, v + k, q0 + 1 + 4 * i + slot, True)
                        if first and k == 3:
                            combine_t(1)
                            pe.wait_ge(m_combE, 4 * n + 2)
                        weight(slot, c, k)
                        if k >= 2:
                            down(*order[k - 2], k, v + k - 2, stop=last and k == 7)
                        elif not first:
                            down(*ORDER[k + 6], k, v + k - 2)

                for c in range(2):
                    pe.wait_ge(m_x_lo[c], n + 1)
                    gate_up(3, c, c, u0 + c, q0, False)
                gate_up(*FIRST_ORDER[0], 0, u0 + 2, q0 + 1 + FIRST_ORDER[0][0], True)
                for c in range(2):
                    down(3, c, c, u0 + c, start=True)
                combine_t(0)
                gate_up(*FIRST_ORDER[1], 1, u0 + 3, q0 + 1 + FIRST_ORDER[1][0], True)
                pe.wait_ge(m_combE, 4 * n + 1)
                for k in range(2):
                    weight(*FIRST_ORDER[k], k)
                over_rounds(pe, m, round_)
                for k in (6, 7):
                    down(*ORDER[k], k, u0 + m["units"] - 8 + k, stop=(k == 7))

            pe.wait_ge(in_ctx, 64)
            pe.wait_ge(prepared, 3)
            norm_means(0)
            prep(0, 0)
            prep(0, 1)
            norm_rest(0)
            prep(0, 2)
            prep(0, 3)
            norm_means(CTX_NORM)
            attn_v(0)
            norm_rest(CTX_NORM)
            pe.wait_ge(a_vtok, 2)
            pe.wait_ge(a_first, 4)
            bias_through_o(0)
            attn(0)
            norm(NORM_OF[1][0])
            moe(MOE[0])
            w = mats1
            pe.wait_ge(in_mats1, 32)
            norm(NORM_OF[2][0])
            pe.wait_ge(x_updated, x_count(1, 1))
            for c in range(2):
                mm(bank[2 + c][:, :], w[:, P:2 * P], context[:, c, :], start=True, stop=True)\
                    .then_inc(b_proj, 1)
            for c in range(2):
                for j in range(BH):
                    last = mm(bank[4 + c][:, j * P:j * P + P], context[:, c, j * P:j * P + P],
                              w[:, 2 * P:3 * P], start=True, stop=True)
                last.then_inc(b_v, 1)
            for c in range(2):
                pe.wait_ge(ln_out, 2 * NORM_OF[2][0] + c + 1)
                mm(bank[6 + c][:, :], w[:, 0:P], xn[:, c, :], start=True, stop=True).then_inc(b_proj, 1)
            for c in range(2):
                pe.wait_ge(b_evac, c + 1)
                mm(bank[2 + c][:, :], w[:, 3 * P:4 * P], xn[:, c, :], start=True, stop=True)\
                    .then_inc(b_proj, 1)
            for c in range(2):
                pe.wait_ge(b_evac, 3 + c)
                for j in range(BH):
                    last = mm(bank[c][:, j * P:j * P + P], q1[:, c, j * P:j * P + P],
                              k1[:, c, j * P:j * P + P], start=True, stop=True)
                last.then_inc(b_s, 1)
            pe.wait_ge(b_vev, 2)
            for c in range(2):
                pe.wait_ge(b_n, c + 1)
                for j in range(BH):
                    last = nc.tensor.transpose(bank[4 + c][:, j * P:j * P + P],
                                               wb[:, c, j * P:j * P + P], ident[:, :])
                last.then_inc(b_tr, 1)
            for c in range(2):
                pe.wait_ge(b_pt, c + 1)
                for j in range(BH):
                    last = mm(bank[6 + c][:, j * P:j * P + P], v1[:, BH * c + j, :],
                              wc[:, c, j * P:j * P + P], start=True, stop=True)
                last.then_inc(b_pv, 1)
            pe.wait_ge(b_evac, 6)
            mm(bank[2][:, :], lora[:, 0:P], lora[:, P:5 * P], start=True, stop=True).then_inc(d_lora, 1)
            for j in range(4):
                last = mm(bank[3][:, j * P:j * P + P], lora[:, 5 * P + j * P:5 * P + j * P + P],
                          lora[:, 9 * P:10 * P], start=True, stop=True)
            last.then_inc(d_lora, 1)
            for c in range(2):
                pe.wait_ge(b_ctx, c + 1)
                mm(bank[c][:, :], w[:, 4 * P:5 * P], wa[:, c, :], start=True, stop=True)\
                    .then_inc(b_y, 1)
            norm(NORM_OF[3][0])
            pe.wait_ge(d_w, 2)
            for c in range(2):
                pe.wait_ge(ln_out, 2 * NORM_OF[3][0] + c + 1)

            def up(m_):
                f, c = m_ // 2, m_ % 2
                if m_ >= 4:
                    pe.wait_ge(d_act, m_ - 3)
                mm(bank[2 + m_ % 4][:, :], mats1[:, (5 + f) * P:(6 + f) * P], xn[:, c, :],
                   start=True, stop=True).then_inc(d_up, 1)

            up(0)
            up(1)
            for m_ in range(8):
                f, c = m_ // 2, m_ % 2
                if m_ + 2 < 8:
                    up(m_ + 2)
                pe.wait_ge(d_act, m_ + 1)
                mm(bank[6 + c][:, :], mats1[:, (9 + f) * P:(10 + f) * P], hidden1(m_),
                   start=(f == 0), stop=(f == 3)).then_inc(d_down, 1)
            w = mats2
            pe.wait_ge(in_mats2, 32)
            i0, i2 = NORM_OF[4]
            norm(i0)
            norm(i2)
            pe.wait_ge(update_ready, u_count(4))
            n = 0

            def put(n):
                if n >= 6:
                    pe.wait_ge(c_kq[n % 2], (n - 6) // 2 + 1)
                return bank[2 + n % 6]
            flat = latents[:, :, :, :].rearrange("p b s t -> p (b s t)")
            for c in range(2):
                pe.wait_ge(ln_out, 2 * i2 + c + 1)
                for m_ in range(4):
                    for g in range(2):
                        gg = 2 * c + g
                        mm(put(n)[:, :], w[:, (4 + m_) * P:(5 + m_) * P],
                           flat[:, gg * 512:gg * 512 + 512], start=True, stop=True).then_inc(c_proj, 1)
                        n += 1
                for m_ in range(4):
                    mm(put(n)[:, :], w[:, m_ * P:(m_ + 1) * P],
                       latents[:, BH * c:BH * c + BH, 1, :], start=True, stop=True)\
                        .then_inc(c_proj, 1)
                    n += 1
                for t in range(8):
                    tile = 8 * c + t
                    mm(put(n)[:, :], flat[:, tile * P:tile * P + P], w[:, 8 * P:12 * P],
                       start=True, stop=True).then_inc(c_proj, 1)
                    n += 1
            for k in range(2):
                pe.wait_ge(c_kq[k], 20)
            pe.wait_ge(pool_ready, 7)
            base, bb = UNITS, B

            def scores2(b, u, half):
                if u == 0:
                    pe.wait_ge(c_slot, 4 * b + 4)
                pe.wait_ge(a_sub, base + 4 * b + u - 1)
                for j in range(2):
                    last = mm(bank[u % 2][:, j * 256:j * 256 + 256], q_slot[half][:, u, j, :],
                              k2[:, u, ds(b, 1), :].squeeze(1), start=True, stop=True)
                last.then_inc(a_s, 1)

            def probs_v2(b, u):
                pe.wait_ge(a_ev, base + 4 * b + u + 1)
                if u % 2 == 0 and beyond(b, 1):
                    pe.wait_ge(c_norm, 2 * b + u // 2 - 1)
                for j in range(2):
                    h = 2 * u + j
                    for t in range(2):
                        v = v2[:, ds(2 * b + t, 1), h:9:8 - h, :].squeeze(1)
                        last = mm(bank[4 + u // 2][:, (2 * (u % 2) + j) * P:(2 * (u % 2) + j) * P + P],
                                  wc[:, u % 2, (2 * j + t) * P:(2 * j + t) * P + P], v,
                                  start=(t == 0), stop=(t == 1))
                last.then_inc(a_pv, 1)

            def tail2(b, u):
                if u == 2:
                    pe.wait_ge(c_norm, 2 * b + 2)
                    pe.wait_ge(a_ofm, B + b)
                    for g in range(4):
                        last = nc.tensor.transpose(bank[6][:, g * P:g * P + P], o_sb[:, g, :], ident[:, :])
                    last.then_inc(a_back, 1)
                if u == 3:
                    pe.wait_ge(a_ofm, B + b + 1)
                    pe.wait_ge(update_ready, u_count(4) + b)
                    for g in range(4):
                        last = mm(bank[7][:, 0:P], w[:, (12 + g) * P:(13 + g) * P], o_fm[:, g, :],
                                  start=(g == 0), stop=(g == 3))
                    last.then_inc(a_y, 1)
            units(base, bb, scores2, probs_v2, tail2)
            w = mats2
            pe.wait_ge(in_mats3, 16)
            pe.wait_ge(a_ofm, 2 * B)
            prep(1, 0)
            pe.wait_ge(update_ready, u_count(5))
            prep(1, 1)
            norm(NORM_OF[5][0])
            for c in range(2):
                pe.wait_ge(ln_out, 2 * NORM_OF[5][0] + c + 1)
                for j in range(BH):
                    last = mm(bank[4 + c][:, j * P:j * P + P], xn[:, c, j * P:j * P + P],
                              w[:, 16 * P:17 * P], start=True, stop=True)
                last.then_inc(m_logit, 1)
            def shared_down(k):
                f, c = k // 2, k % 2
                pe.wait_ge(e_sh, k + 1)
                if k == 0:
                    pe.wait_ge(a_first, 6)
                mm(bank[6 + c][:, :], w[:, (21 + f) * P:(22 + f) * P], wc[:, c, :],
                   start=(f == 0), stop=(f == 1)).then_inc(e_zd, 1)
            def combine_t2(c):
                pe.wait_ge(m_comb, 2 + c + 1)
                for j in range(BH):
                    last = nc.tensor.transpose(
                        bank[4 + c][:, :].bitcast(bf16)[:, j * P:j * P + P],
                        comb_pieces2[:, BH * c + j, :], ident_bf[:, :])
                last.then_inc(m_combT, 1)

            for f in range(2):
                for c in range(2):
                    k = 2 * f + c
                    if k >= 2:
                        pe.wait_ge(e_sh, k - 1)
                    mm(bank[c][:, :], w[:, (17 + f) * P:(18 + f) * P], xn[:, c, :],
                       start=True, stop=True).then_inc(e_h1, 1)
                    mm(bank[2 + c][:, :], w[:, (19 + f) * P:(20 + f) * P], xn[:, c, :],
                       start=True, stop=True).then_inc(e_x3, 1)
                    if k == 3:
                        combine_t2(0)
                    if k >= 1:
                        shared_down(k - 1)
            shared_down(3)

            def late(e, c):
                pe.wait_ge(e_h, 2 * e + c + 1)
                if (e, c) != (0, 0):
                    pe.wait_ge(e_v, 2 * e + c)
                mm(bank[6][:, :], ring[:, e % 4, 2 * P:3 * P], wb[:, c, :], start=True, stop=True)\
                    .then_inc(e_x2, 1)

            def weight(k):
                e, c = k // 2, k % 2
                if k < 2:
                    pe.wait_ge(m_combE, 3 + k)
                if k >= 1:
                    pe.wait_ge(e_xs, k)
                mm(bank[4][:, :], select2[:, e, 0, :], comb_t2[:, c * HALF:c * HALF + HALF],
                   start=True, stop=True).then_inc(e_wb, 1)

            weight(0)
            for k in range(16):
                e, c = k // 2, k % 2
                if 1 <= k < 15:
                    weight(k + 1)
                pe.wait_ge(w_in[e % 4], fills2(e))
                pe.wait_ge(e_xs, k + 1)
                if k >= 2:
                    pe.wait_ge(e_h, k - 1)
                    pe.wait_ge(e_x3b, k - 1)
                mm(bank[c][:, :], ring[:, e % 4, 0:P], wa[:, c, :], start=True, stop=True)\
                    .then_inc(e_h1, 1)
                mm(bank[2 + c][:, :], ring[:, e % 4, P:2 * P], wa[:, c, :], start=True, stop=True)\
                    .then_inc(e_x3, 1)
                if k == 0:
                    combine_t2(1)
                    weight(1)
                if k >= 1:
                    late((k - 1) // 2, (k - 1) % 2)
                    pe.wait_ge(e_u, k)
                mm(bank[5][:, :], select2[:, e, 1, :], comb_t2[:, c * HALF:c * HALF + HALF],
                   start=True, stop=True).then_inc(e_mk, 1)
            late(7, 1)
            norm(NORM_OF[6][0])
            pe.wait_ge(e_v, 16)
            prep(1, 2)
            prep(1, 3)
            attn_v(1)
            pe.wait_ge(a_first, 8)
            pe.wait_ge(a_vtok, 4)
            bias_through_o(1)
            attn(1)
            norm(NORM_OF[7][0])
            moe(MOE[1])

        @block.scalar
        def _(act):
            fn = nc.scalar.activation

            def norm_means(i):
                nc.scalar.preload_act_table(ACT.Sqrt)
                for c in range(2):
                    act.wait_ge(ln_cen, 2 * i + c + 1)
                    fn(sq[:, c, :], cen[:, c, :], ACT.Square).then_inc(ln_sq, 1)

            def norm_rest(i):
                for c in range(2):
                    act.wait_ge(ln_var, 2 * i + c + 1)
                    fn(rstd[:, c, :], bank[c][:, :].rearrange("p (j m) -> p j m", j=BH)[:, :, 0],
                       ACT.Sqrt, bias=eps_col[:, :]).then_inc(ln_std, 1)

            def norm(i):
                norm_means(i)
                norm_rest(i)

            def prep(inst, k):
                n = 4 * inst + k
                bias = col(A_BIAS[inst][0] if k < 2 else A_BIAS[inst][1])
                act.wait_ge(a_proj, n + 1)
                if n >= 2:
                    act.wait_ge(a_rest, n - 1)
                    act.wait_ge(a_stacked[n % 2], 144 * (n // 2))
                fn(wa[:, k % 2, :], bank[6 + k % 2][:, :], ACT.Identity, bias=bias).then_inc(a_full, 1)
                fn(pieces[:, n % 2, 0, :], bank[6 + k % 2][:, :], ACT.Identity, bias=bias)\
                    .then_inc(a_first, 1)

            def v_token_major(inst):
                for c in range(2):
                    act.wait_ge(a_vproj, 2 * inst + c + 1)
                    fn(v_tok[:, BH * c:BH * c + BH, :], bank[4 + c][:, :], ACT.Copy).then_inc(a_vtok, 1)

            def update(s, src, n, width):
                if n is not None:
                    act.wait_ge(x_updated, n)
                if s in (0, 2, 3, 6):
                    fn(upd[:, 0:width], src, ACT.Identity, bias=tgb[:, s:s + 1], scale=tg[:, s:s + 1])\
                        .then_inc(update_ready, 1)
                else:
                    fn(upd[:, 0:width], src, ACT.Copy, scale=tg[:, s:s + 1]).then_inc(update_ready, 1)

            def units(base, s, before, scale, y_before, turned):
                width = P if turned is not None else 4 * P

                def exp(b, u):
                    act.wait_ge(a_sub, base + 4 * b + u + 1)
                    if base > 0 or beyond(b, 1) or u > 1:
                        act.wait_ge(a_tr, base + 4 * b + u - 1)
                    fn(wb[:, u % 2, :], wa[:, u % 2, :], ACT.Exp, scale=scale).then_inc(a_exp, 1)

                def evac(b, u):
                    act.wait_ge(a_tr, base + 4 * b + u + 1)
                    if base > 0 or beyond(b, 1) or u > 1:
                        act.wait_ge(a_pv, base + 4 * b + u - 1)
                    fn(wc[:, u % 2, :], bank[2 + u % 2][:, :], ACT.Copy).then_inc(a_ev, 1)

                def copy_o(b):
                    act.wait_ge(a_pv, base + 4 * b + 4)
                    if turned > 0 or beyond(b, 1):
                        act.wait_ge(a_turned, turned + b)
                    fn(o_sb[:, 0:2, :], bank[4][:, 0:2 * P], ACT.Copy).then_inc(a_ocopy, 1)

                def copy_back(b):
                    act.wait_ge(a_back, y_before + b + 1)
                    if y_before > 0 or beyond(b, 1):
                        act.wait_ge(a_y, y_before + b)
                    fn(o_fm[:, 0:width // P, :], bank[6][:, 0:width], ACT.Copy).then_inc(a_ofm, 1)

                def batch_update(b):
                    act.wait_ge(a_y, y_before + b + 1)
                    update(s, bank[7][:, 0:P], before + b if before > 0 or beyond(b, 1) else None, P)

                def batch(b, odd):
                    for u in range(4):
                        if u < 3:
                            exp(b, u + 1)
                        elif not (isinstance(b, int) and b == B - 1):
                            exp(b + 1, 0)
                        if u == 0 and beyond(b, 2):
                            batch_update(b - 2)
                        if u == 3 and beyond(b, 1):
                            copy_back(b - 1)
                        evac(b, u)
                        if u == 0 and turned is not None and beyond(b, 1):
                            copy_o(b - 1)
                exp(0, 0)
                over_batches(act, batch)
                batch_update(B - 2)
                if turned is not None:
                    copy_o(B - 1)
                copy_back(B - 1)
                batch_update(B - 1)

            def moe(m):
                n, u0, q0, s = m["n"], m["u0"], m["q0"], m["stage"]

                def split(slot, pair, fills, used):
                    act.wait_ge(w_in[slot], 16 * (m["fill0"][slot] + fills))
                    if used is not None:
                        act.wait_ge(m_down, used)
                    fn(w_hi[:, slot, :], ring[:, slot, :], ACT.Copy).then_inc(m_w_hi, 1)

                def scores(c):
                    act.wait_ge(m_logit, 4 * n + c + 1)
                    fn(rt[:, c, 0:4 * m["E"]].rearrange("p (t e) -> p t e", t=4),
                       bank[4 + c][:, :].rearrange("p (t e) -> p t e", t=4)[:, :, 0:m["E"]],
                       ACT.Sigmoid).then_inc(m_score, 1)

                def silu(k, v, older):
                    act.wait_ge(m_g, v + 1)
                    if older:
                        act.wait_ge(m_h, v - 1)
                    fn(wa[:, k % 2, :], bank[k % 2][:, :], ACT.Silu).then_inc(m_silu, 1)

                def hidden(k, v, older):
                    act.wait_ge(m_h, v + 1)
                    if older:
                        act.wait_ge(m_down, v - 1)
                        act.wait_ge(m_h_lo, v - 1)
                    fn(h_hi[:, k % 2, :], wc[:, k % 2, :], ACT.Copy).then_inc(m_h_hi, 1)

                def weights_out(c):
                    act.wait_ge(m_combT, 4 * n + c + 1)
                    fn(comb_t[:, c * HALF:c * HALF + HALF], bank[4 + c][:, :], ACT.Copy)\
                        .then_inc(m_combE, 1)

                nc.scalar.preload_act_table(ACT.Sigmoid)
                split(3, q0, 1, None if n == 0 else u0)
                split(0, q0 + 1, 1, None)
                for c in range(2):
                    act.wait_ge(ln_out, 2 * NORM_OF[s][0] + c + 1)
                    fn(xn_hi[:, c, :], xn[:, c, :], ACT.Copy).then_inc(m_x_hi, 1)
                    scores(c)
                nc.scalar.preload_act_table(ACT.Silu)
                silu(0, u0, n > 0)
                silu(1, u0 + 1, n > 0)
                hidden(0, u0, n > 0)
                split(1, q0 + 2, 1, None)
                silu(0, u0 + 2, True)
                hidden(1, u0 + 1, n > 0)
                split(2, q0 + 3, 1, None)
                weights_out(0)
                split(3, None, 2, u0 + 2)

                def round_(i, first, last):
                    v = u0 + 2 + 8 * i
                    for k in range(8):
                        if first and k == 7:
                            split(1, None, 2, v + FIRST_LAST_USE[1] + 1)
                        if not (last and k == 7):
                            silu(k + 1, v + k + 1, True)
                        if first and k == 2:
                            weights_out(1)
                        if first and k == 6:
                            split(0, None, 2, v + FIRST_LAST_USE[0] + 1)
                        hidden(k, v + k, True)
                        if k in (1, 2) and not first:
                            split(k + 1, None, i + (1 if k == 1 else 2), v - 8 + LAST_USE[k + 1] + 1)
                        if k in (5, 6) and not (first or last):
                            split(k - 5, None, i + 2, v + LAST_USE[k - 5] + 1)
                over_rounds(act, m, round_)

            act.wait_ge(in_x, 48)
            fn(tg[:, :], gates[:, :], ACT.Tanh).then_inc(tg_ready, 1)
            act.wait_ge(in_ctx, 64)
            act.wait_ge(prepared, 3)
            norm_means(0)
            prep(0, 0)
            prep(0, 1)
            norm_rest(0)
            prep(0, 2)
            norm_means(CTX_NORM)
            v_token_major(0)
            norm_rest(CTX_NORM)
            nc.scalar.preload_act_table(ACT.Exp)
            prep(0, 3)
            act.wait_ge(tgb_ready, 3)
            act.wait_ge(tg_ready, 1)
            units(0, 0, 0, SCALE_A, 0, 0)
            norm(NORM_OF[1][0])
            moe(MOE[0])
            norm(NORM_OF[2][0])
            nc.scalar.preload_act_table(ACT.Sigmoid)
            for c in range(2):
                act.wait_ge(b_proj, c + 1)
                fn(k1[:, c, :], bank[2 + c][:, :], ACT.Identity, bias=col(K1B)).then_inc(b_evac, 1)
            for c in range(2):
                act.wait_ge(b_proj, 3 + c)
                fn(q1[:, c, :], bank[6 + c][:, :], ACT.Identity, bias=col(Q1B)).then_inc(b_evac, 1)
            for c in range(2):
                act.wait_ge(b_proj, 5 + c)
                fn(gate1[:, c, :], bank[2 + c][:, :], ACT.Sigmoid, bias=col(G1B)).then_inc(b_evac, 1)
            for c in range(2):
                act.wait_ge(b_p, c + 1)
                fn(wb[:, c, :], wa[:, c, :], ACT.Exp).then_inc(b_e, 1)
            for c in range(2):
                act.wait_ge(b_tr, c + 1)
                fn(wc[:, c, :], bank[4 + c][:, :], ACT.Copy).then_inc(b_pt, 1)
            for c in range(2):
                act.wait_ge(b_y, c + 1)
                update(2, bank[c][:, :], x_count(1, 1) + c, HALF)
            norm(NORM_OF[3][0])
            nc.scalar.preload_act_table(GELU)
            for n in range(8):
                act.wait_ge(d_up, n + 1)
                if n >= 4:
                    act.wait_ge(d_down, n - 3)
                fn(hidden1(n), bank[2 + n % 4][:, :], GELU, bias=col(FCB + n // 2)).then_inc(d_act, 1)
            for c in range(2):
                act.wait_ge(d_down, 7 + c)
                update(3, bank[6 + c][:, :], x_count(2, 1) + c, HALF)
            for i in NORM_OF[4]:
                norm(i)
            for n in range(0, 40, 2):
                act.wait_ge(c_proj, n + 1)
                dst, scale = product2(n)
                fn(dst, bank2(n), ACT.Copy, scale=scale).then_inc(c_kq[0], 1)
            nc.scalar.preload_act_table(ACT.Exp)
            units(UNITS, 4, 14, 1.0, B, None)
            norm(NORM_OF[5][0])
            prep(1, 0)
            prep(1, 1)
            nc.scalar.preload_act_table(ACT.Exp)
            for c in range(2):
                act.wait_ge(m_shift, c + 1)
                fn(rt[:, c, 0:32], rt[:, c, 0:32], ACT.Exp).then_inc(m_score, 1)
            for k in range(4):
                act.wait_ge(e_h1, k + 1)
                if k >= 2:
                    act.wait_ge(e_sh, k - 1)
                fn(wb[:, k % 2, :], bank[k % 2][:, :], ACT.Silu).then_inc(e_sg, 1)
            def weights2_out(c):
                act.wait_ge(m_combT, 2 + c + 1)
                fn(comb_t2[:, c * HALF:c * HALF + HALF], bank[4 + c][:, :].bitcast(bf16)[:, 0:HALF],
                   ACT.Copy).then_inc(m_combE, 1)
            weights2_out(0)
            act.wait_ge(e_sh, 4)
            for c in range(2):
                act.wait_ge(e_zd, 3 + c)
                fn(cen[:, c, :], bank[6 + c][:, :], ACT.Copy).then_inc(e_z, 1)
            for k in range(16):
                e, c = k // 2, k % 2
                act.wait_ge(e_h1, 4 + k + 1)
                if k >= 2:
                    act.wait_ge(e_x2, k - 1)
                fn(wb[:, c, :], bank[c][:, :], ACT.Silu, bias=col(B1 + e)).then_inc(e_h, 1)
                if k == 0:
                    weights2_out(1)
                act.wait_ge(e_x3, 4 + k + 1)
                if k >= 2:
                    act.wait_ge(e_u, k - 1)
                fn(sq[:, c, :], bank[2 + c][:, :], ACT.Identity, bias=col(B3 + e)).then_inc(e_x3b, 1)
            norm(NORM_OF[6][0])
            nc.scalar.preload_act_table(ACT.Exp)
            prep(1, 2)
            prep(1, 3)
            v_token_major(1)
            act.wait_ge(tgb_ready, 4)
            units(2 * UNITS, 6, 24, SCALE_A, 2 * B, B)
            norm(NORM_OF[7][0])
            moe(MOE[1])

        @block.vector
        def _(dve):
            v = nc.vector
            chain = [0]

            def link(ins):
                chain[0] += 1
                ins.then_inc(dve_chain, 1)
                dve.wait_ge(dve_chain, chain[0])

            def add_gated(s, c, y):
                v.scalar_tensor_tensor(x[:, c, :], y, tg[:, s:s + 1], x[:, c, :], ALU.mult, ALU.add)\
                    .then_inc(x_updated, 1)

            def add_update(s, c):
                dve.wait_ge(update_ready, u_count(s) + c + 1)
                v.tensor_tensor(x[:, c, :], x[:, c, :], upd[:, :], ALU.add).then_inc(x_updated, 1)

            def norm_means(i):
                src = NORMS[i][0]
                for c in range(2):
                    dve.wait_ge(ln_mean, 2 * i + c + 1)
                    if i > 0:
                        dve.wait_ge(ln_out, 2 * (i - 1) + c + 1)
                    v.tensor_tensor(cen[:, c, :], src(c), bank[c][:, :], ALU.subtract).then_inc(ln_cen, 1)

            def norm_rest(i):
                _, dst, affine, _ = NORMS[i]
                for c in range(2):
                    n = 2 * i + c + 1
                    dve.wait_ge(ln_std, n)
                    v.reciprocal(rstd[:, c, :], rstd[:, c, :]).then_inc(ln_inv, 1)
                    dve.wait_ge(ln_inv, n)
                    wide = [P, BH, P]
                    v.tensor_tensor(diag[:, c, :].rearrange("p (j m) -> p j m", j=BH),
                                    ident[:, :].unsqueeze(1).to_broadcast(wide),
                                    rstd[:, c, :].unsqueeze(2).to_broadcast(wide), ALU.mult)\
                        .then_inc(ln_diag, 1)
                for c in range(2):
                    dve.wait_ge(ln_spread, 2 * i + c + 1)
                    if affine is None:
                        v.tensor_tensor(dst(c), cen[:, c, :], bank[c][:, :], ALU.mult).then_inc(ln_out, 1)
                    else:
                        link(v.tensor_tensor(cen[:, c, :], cen[:, c, :], bank[c][:, :], ALU.mult))
                        v.tensor_scalar(dst(c), cen[:, c, :].rearrange("p (b t) -> p b t", b=BH),
                                        col(affine[0]), col(affine[1]), ALU.mult, ALU.add)\
                            .then_inc(ln_out, 1)

            def norm(i):
                norm_means(i)
                norm_rest(i)

            def prep(inst, k):
                n = 4 * inst + k
                rest = (sq if n in (4, 5) else wb)[:, k % 2, :]
                dve.wait_ge(a_full, n + 1)
                dve.wait_ge(a_first, n + 1)
                v.tensor_tensor(rest, wa[:, k % 2, :], pieces[:, n % 2, 0, :], ALU.subtract)\
                    .then_inc(a_rest, 1)
                dve.wait_ge(a_rest, n + 1)
                v.tensor_copy(pieces[:, n % 2, 1, :], rest).then_inc(a_piece2, 1)
                dve.wait_ge(a_piece2, n + 1)
                v.tensor_tensor(pieces[:, n % 2, 2, :], rest, pieces[:, n % 2, 1, :],
                                ALU.subtract).then_inc(a_split, 1)

            def units(base, heads, extra):
                def unit(b, u):
                    n = base + 4 * b + u
                    s = bank[u % 2][:, :].rearrange("p (h k) -> p h k", h=heads)
                    dve.wait_ge(a_s, n + 1)
                    v.tensor_reduce(row_max[:, u % 2, 0:heads], s, X, ALU.max).then_inc(a_max, 1)
                    dve.wait_ge(a_max, n + 1)
                    if base > 0 or beyond(b, 1) or u > 1:
                        dve.wait_ge(a_exp, n - 1)
                    v.tensor_tensor(wa[:, u % 2, :].rearrange("p (h k) -> p h k", h=heads), s,
                                    row_max[:, u % 2, 0:heads].unsqueeze(2)
                                    .to_broadcast([P, heads, 512 // heads]), ALU.subtract)\
                        .then_inc(a_sub, 1)

                def batch(b, odd):
                    for u in range(4):
                        unit(b, u)
                        extra(b, u, odd)
                over_batches(dve, batch)

            def attn(inst):
                base, tb = (0 if inst == 0 else 2 * UNITS), B * inst
                yb = 2 * B * inst

                def divide(b):
                    o = bank[5][:, 0:2 * P].rearrange("p (h s d) -> p h s d", h=HEADS, s=2)
                    dve.wait_ge(a_turned, tb + b + 1)
                    if tb > 0 or beyond(b, 1):
                        dve.wait_ge(a_norm, tb + b)
                    v.reciprocal(o_inv[:, :], o[:, :, 1, 0]).then_inc(a_inv, 1)
                    dve.wait_ge(a_inv, tb + b + 1)
                    if tb > 0 or beyond(b, 1):
                        dve.wait_ge(a_back, yb + b)
                    v.tensor_tensor(o_tok[:, :].rearrange("p (h d) -> p h d", h=HEADS), o[:, :, 0, :],
                                    o_inv[:, :].unsqueeze(2).to_broadcast([P, HEADS, HD]), ALU.mult)\
                        .then_inc(a_norm, 1)

                def extra(b, u, odd):
                    if u == 3 and beyond(b, 1):
                        divide(b - 1)
                units(base, 4, extra)
                divide(B - 1)

            def attn2():
                base = UNITS

                def q_fill(b, half):
                    tok = ds(b * P, P)
                    for j, rows in enumerate((slice(0, 64), slice(64, P))):
                        v.tensor_copy(q_slot[half][rows, 0:3, j, :], q2[rows, :, tok]).then_inc(c_slot, 1)
                        v.tensor_copy(q_slot[half][rows, 3, j, :], q2_last[rows, tok]).then_inc(c_slot, 1)

                def finish(b, p):
                    o = bank[4 + p][:, :].rearrange("p (h s d) -> p h s d", h=4, s=2)
                    dve.wait_ge(a_pv, base + 4 * b + 2 * p + 2)
                    if p > 0 or beyond(b, 1):
                        dve.wait_ge(c_norm, 2 * b + p)
                    v.reciprocal(o_inv[:, 0:4], o[:, :, 1, 0]).then_inc(c_rec, 1)
                    dve.wait_ge(c_rec, 2 * b + p + 1)
                    if p == 0:
                        dve.wait_ge(a_back, B + b)
                    v.tensor_tensor(o_sb[:, 2 * p:2 * p + 2, :].rearrange("p g (h d) -> p (g h) d", d=64),
                                    o[:, :, 0, :], o_inv[:, 0:4].unsqueeze(2).to_broadcast([P, 4, 64]),
                                    ALU.mult).then_inc(c_norm, 1)

                def extra(b, u, odd):
                    if u == 0 and beyond(b, 1):
                        finish(b - 1, 0)
                    if u == 1 and not (isinstance(b, int) and b == B - 1):
                        if beyond(b, 1):
                            dve.wait_ge(a_s, base + 4 * b)
                        q_fill(b + 1, 1 - odd)
                    if u == 2 and beyond(b, 1):
                        finish(b - 1, 1)
                dve.wait_ge(pool_ready, 6)
                for k in range(2):
                    dve.wait_ge(c_kq[k], 20)
                q_fill(0, 0)
                units(base, 2, extra)
                finish(B - 1, 0)
                finish(B - 1, 1)

            def ranks(vals, g, tri, s0):
                shape = [P, 4, g, g]
                def square(n):
                    return rt[:, n, 0:4 * g * g].rearrange("p (t i j) -> p t i j", t=4, i=g)
                mine = vals.unsqueeze(3).to_broadcast(shape)
                other = vals.unsqueeze(2).to_broadcast(shape)
                more, same = square(s0), square(s0 + 1)
                v.tensor_tensor(more, other, mine, ALU.is_gt)
                link(v.tensor_tensor(same, other, mine, ALU.is_equal))
                link(v.tensor_tensor(same, same, tri[:, :, :].unsqueeze(1).to_broadcast(shape), ALU.mult))
                link(v.tensor_tensor(more, more, same, ALU.add))
                rank = rt[:, s0 + 2, 0:4 * g].rearrange("p (t i) -> p t i", t=4)
                link(v.tensor_reduce(rank, more, X, ALU.add))
                return rank

            def grid(n, e):
                return rt[:, n, 0:4 * e].rearrange("p (t e) -> p t e", t=4)

            def split_weights(comb, e, c):
                dst = comb_pieces[:, BH * c:BH * c + BH, :]
                link(v.tensor_copy(dst[:, :, 0:e].bitcast(f32r), comb))
                return v.tensor_tensor(dst[:, :, e:2 * e].bitcast(f32r), comb, dst[:, :, 0:e], ALU.subtract)

            def split_weights2(comb, e, c, tmp):
                rest = grid(tmp, e)
                dst = comb_pieces2[:, BH * c:BH * c + BH, :]
                link(v.tensor_copy(dst[:, :, 0:e], comb))
                link(v.tensor_tensor(rest, comb, dst[:, :, 0:e], ALU.subtract))
                link(v.tensor_copy(dst[:, :, e:2 * e], rest))
                return v.tensor_tensor(dst[:, :, 2 * e:3 * e], rest, dst[:, :, e:2 * e], ALU.subtract)

            def route_groups(m, c):
                n, E, G = m["n"], m["E"], m["G"]
                dve.wait_ge(m_score, 4 * n + c + 1)
                score = grid(c, E)
                bias = route_bias[:, m["bias"]:m["bias"] + E].unsqueeze(1).to_broadcast([P, 4, E])
                biased = grid(2, E)
                link(v.tensor_tensor(biased, score, bias, ALU.add))
                groups = biased.rearrange("p t (g s) -> p t g s", g=G)
                best = grid(3, G)
                if n == 0:
                    pair = groups.rearrange("p t g (a b) -> p t g a b", a=2)
                    pair = biased.rearrange("p t (g a b) -> p (t g) a b", g=G, a=2)
                    hi = rt[:, 4, 0:32].rearrange("p (x a) -> p x a", a=2)
                    lo = rt[:, 5, 0:32].rearrange("p (x a) -> p x a", a=2)
                    v.tensor_tensor(hi, pair[:, :, :, 0], pair[:, :, :, 1], ALU.max)
                    link(v.tensor_tensor(lo, pair[:, :, :, 0], pair[:, :, :, 1], ALU.min))
                    t1, t2, t3 = (rt[:, k, 0:16] for k in (6, 7, 8))
                    v.tensor_tensor(t1, hi[:, :, 0], hi[:, :, 1], ALU.max)
                    v.tensor_tensor(t2, hi[:, :, 0], hi[:, :, 1], ALU.min)
                    link(v.tensor_tensor(t3, lo[:, :, 0], lo[:, :, 1], ALU.max))
                    link(v.tensor_tensor(t2, t2, t3, ALU.max))
                    link(v.tensor_tensor(rt[:, 3, 0:16], t1, t2, ALU.add))
                else:
                    link(v.tensor_reduce(best, groups, X, ALU.max))
                rank = ranks(best, G, m["tri"], 4)
                keep = grid(7, G)
                link(v.tensor_scalar(keep, rank, float(m["TG"]) - 0.5, None, ALU.is_lt))

            def route_top(m, c):
                E, G, K = m["E"], m["G"], m["K"]
                size = E // G
                groups = grid(2, E).rearrange("p t (g s) -> p t g s", g=G)
                keep = grid(7, G)
                width = E + 8 - K
                ext = rt[:, 8, 0:4 * width].rearrange("p (t e) -> p t e", t=4)
                cut = rt[:, 9, 0:4 * width].rearrange("p (t e) -> p t e", t=4)
                v.memset(ext[:, :, E:width], 3e38)
                for t in range(4):
                    ins = v.tensor_tensor(ext[:, t, 0:E].rearrange("p (g s) -> p g s", g=G),
                                          groups[:, t, :, :],
                                          keep[:, t, :].unsqueeze(2).to_broadcast([P, G, size]), ALU.mult)
                link(ins)
                top = rt[:, 10, 0:32].rearrange("p (t k) -> p t k", t=4)
                for t in range(4):
                    ins = v.max(top[:, t, :], ext[:, t, :])
                link(ins)
                for t in range(4):
                    ins = v.match_replace(cut[:, t, :], top[:, t, :], ext[:, t, :], -3e38)
                link(ins)
                chosen = grid(11, E)
                link(v.tensor_scalar(chosen, cut[:, :, 0:E], -1e38, None, ALU.is_lt))

            def route_weights(m, c):
                n, E, K = m["n"], m["E"], m["K"]
                ext = rt[:, 8, 0:4 * (E + 8 - K)].rearrange("p (t e) -> p t e", t=4)
                chosen = grid(11, E)
                weight = grid(c, E) if n == 0 else ext[:, :, 0:E]
                picked = grid(12, E)
                link(v.tensor_tensor(picked, weight, chosen, ALU.mult))
                total = rt[:, 13, 0:4]
                link(v.tensor_reduce(total, picked, X, ALU.add))
                link(v.tensor_scalar(total, total, 1e-20 if n == 0 else 1e-8, None, ALU.add))
                link(v.reciprocal(total, total))
                link(v.tensor_tensor(picked, picked, total.unsqueeze(2).to_broadcast([P, 4, E]), ALU.mult))
                if n == 0:
                    link(v.tensor_scalar(picked, picked, 2.5, None, ALU.mult))
                split_weights(picked, E, c).then_inc(m_comb, 1)

            def moe(m):
                n, u0 = m["n"], m["u0"]

                def products(k, unit, weighed, older):
                    par = k % 2
                    dve.wait_ge(m_silu, unit + 1)
                    dve.wait_ge(m_u, unit + 1)
                    if older:
                        dve.wait_ge(m_h_lo, unit - 1)
                    if weighed:
                        v.tensor_tensor(wb[:, par, :], wa[:, par, :], bank[2 + par][:, :], ALU.mult)\
                            .then_inc(m_t, 1)
                        dve.wait_ge(m_t, unit - 2 * n - 1)
                        dve.wait_ge(m_cb, unit - 2 * n - 1)
                        v.tensor_tensor(wc[:, par, :], wb[:, par, :], bank[4 + par][:, :], ALU.mult)\
                            .then_inc(m_h, 1)
                    else:
                        v.tensor_tensor(wc[:, par, :], wa[:, par, :], bank[2 + par][:, :], ALU.mult)\
                            .then_inc(m_h, 1)

                dve.wait_ge(m_x_hi, 2 * n + 1)
                v.tensor_tensor(xn_lo[:, 0, :], xn[:, 0, :], xn_hi[:, 0, :].bitcast(f32), ALU.subtract)\
                    .then_inc(m_x_lo[0], 1)
                route_groups(m, 0)
                products(0, u0, False, n > 0)
                route_top(m, 0)
                products(1, u0 + 1, False, n > 0)
                route_weights(m, 0)
                route_groups(m, 1)
                products(0, u0 + 2, True, True)
                route_top(m, 1)
                products(1, u0 + 3, True, True)
                route_weights(m, 1)
                products(0, u0 + 4, True, True)
                products(1, u0 + 5, True, True)

                def round_(i, first, last):
                    for k in range(4 if first else 0, 8):
                        products(k, u0 + 2 + 8 * i + k, True, True)
                    if last:
                        unit = u0 + m["units"] - 1
                        dve.wait_ge(m_h_hi, unit + 1)
                        dve.wait_ge(m_down, unit - 1)
                        dve.wait_ge(m_h_lo, unit)
                        v.tensor_tensor(h_lo[:, 1, :], wc[:, 1, :], h_hi[:, 1, :].bitcast(f32),
                                        ALU.subtract).then_inc(m_h_lo, 1)
                over_rounds(dve, m, round_)
                for c in range(2):
                    dve.wait_ge(m_down, u0 + m["units"] - (2 if c == 0 else 0))
                    add_gated(m["stage"], c, bank[6 + c][:, :])

            v.memset(mean_w[:, :], 1.0 / P).then_inc(prepared, 1)
            v.memset(eps_col[:, :], EPS).then_inc(prepared, 1)
            v.memset(ones[:, :], 1.0).then_inc(prepared, 1)
            v.memset(ones16, 1.0).then_inc(a_mask, 1)
            dve.wait_ge(in_x, 48)
            v.tensor_scalar(mask_neg, mask_u8, -1e30, None, ALU.mult).then_inc(a_mask, 1)
            norm_means(0)
            prep(0, 0)
            prep(0, 1)
            dve.wait_ge(in_ctx, 64)
            norm_rest(0)
            prep(0, 2)
            norm_means(CTX_NORM)
            v.memset(comb_pieces[:, :, :], 0.0)
            dve.wait_ge(tg_ready, 1)
            v.tensor_tensor(tgb[:, 2:3], tg[:, 2:3], col(O1B), ALU.mult).then_inc(tgb_ready, 1)
            v.tensor_tensor(tgb[:, 3:4], tg[:, 3:4], col(PROJB), ALU.mult).then_inc(tgb_ready, 1)
            dve.wait_ge(in_x, 80)
            norm_rest(CTX_NORM)
            prep(0, 3)
            dve.wait_ge(o_bias, 1)
            v.tensor_scalar(tgb[:, 0:1], bank[7][:, 0:1], col(O0B), tg[:, 0:1], ALU.add, ALU.mult)\
                .then_inc(tgb_ready, 1)
            attn(0)
            norm(NORM_OF[1][0])
            moe(MOE[0])
            scale, inv, neg = w_stat[:, 0:2], w_stat[:, 2:4], w_stat[:, 4:6]

            def largest_weights():
                for n in range(2):
                    w = mats1[:, (5 + 4 * n) * P:(9 + 4 * n) * P]
                    v.tensor_reduce(w_max[:, n:n + 1], w, X, ALU.max, apply_absolute_value=True)\
                        .then_inc(d_rowmax, 1)

            def quantisation_steps():
                dve.wait_ge(d_max, 1)
                link(v.tensor_scalar(scale, w_max[:, 2:4], 1.0 / 127.0, None, ALU.mult))
                v.reciprocal(inv, scale)
                link(v.tensor_scalar(neg, scale, -1.0, None, ALU.mult))

            def fake_quantise(n):
                w = mats1[:, (5 + 4 * n) * P:(9 + 4 * n) * P]
                s1, i1_, n1 = scale[:, n:n + 1], inv[:, n:n + 1], neg[:, n:n + 1]
                q, e = sq[:, 0, :], sq[:, 1, :]
                link(v.tensor_scalar(q, w, i1_, None, ALU.mult))
                link(v.scalar_tensor_tensor(e, q, n1, w, ALU.mult, ALU.add))
                link(v.scalar_tensor_tensor(q, e, i1_, q, ALU.mult, ALU.add))
                link(v.tensor_scalar(q, q, ROUND, ROUND, ALU.add, ALU.subtract))
                link(v.tensor_scalar(q, q, 127.0, -128.0, ALU.min, ALU.max))
                link(v.scalar_tensor_tensor(e, q, s1, w, ALU.mult, ALU.subtract))
                link(v.tensor_tensor(w, w, e, ALU.add))

            dve.wait_ge(in_mats1, 32)
            largest_weights()
            norm(NORM_OF[2][0])
            quantisation_steps()
            for c in range(2):
                dve.wait_ge(b_v, c + 1)
                v.tensor_copy(v1[:, BH * c:BH * c + BH, :], bank[4 + c][:, :]).then_inc(b_vev, 1)
            fake_quantise(0)
            for c in range(2):
                s = bank[c][:, :].rearrange("p (b k) -> p b k", b=BH)
                wide = [P, BH, P]
                dve.wait_ge(b_s, c + 1)
                link(v.tensor_reduce(row_max[:, c, :], s, X, ALU.max))
                v.tensor_tensor(wa[:, c, :].rearrange("p (b k) -> p b k", b=BH), s,
                                row_max[:, c, :].unsqueeze(2).to_broadcast(wide),
                                ALU.subtract).then_inc(b_p, 1)
            for c in range(2):
                e = wb[:, c, :].rearrange("p (b k) -> p b k", b=BH)
                dve.wait_ge(b_e, c + 1)
                link(v.tensor_reduce(row_max[:, c, :], e, X, ALU.add))
                link(v.reciprocal(row_max[:, c, :], row_max[:, c, :]))
                v.tensor_tensor(e, e, row_max[:, c, :].unsqueeze(2).to_broadcast(wide), ALU.mult)\
                    .then_inc(b_n, 1)
            fake_quantise(1)
            for c in range(2):
                dve.wait_ge(b_pv, c + 1)
                dve.wait_ge(b_evac, 5 + c)
                v.scalar_tensor_tensor(wa[:, c, :], bank[6 + c][:, :], col(V1B), gate1[:, c, :],
                                       ALU.add, ALU.mult).then_inc(b_ctx, 1)
            for c in range(2):
                add_update(2, c)
            for n in range(2):
                w = mats1[:, (5 + 4 * n) * P:(9 + 4 * n) * P]
                dve.wait_ge(d_lora, n + 1)
                v.scalar_tensor_tensor(w, bank[2 + n][:, :], 2.0, w, ALU.mult, ALU.add)\
                    .then_inc(d_w, 1)
            norm(NORM_OF[3][0])
            for c in range(2):
                add_update(3, c)
            for i in NORM_OF[4]:
                norm(i)
            for n in range(1, 40, 2):
                dve.wait_ge(c_proj, n + 1)
                dst, scale = product2(n)
                v.tensor_scalar(dst, bank2(n), scale, None, ALU.mult).then_inc(c_kq[1], 1)
            attn2()
            v.memset(comb_pieces[:, :, 0:64], 0.0)
            norm(NORM_OF[5][0])

            def softmax_route(c):
                logits = bank[4 + c][:, :].rearrange("p (t e) -> p t e", t=4)[:, :, 0:8]
                top = rt[:, 2 + c, 0:4]
                dve.wait_ge(m_logit, 2 + c + 1)
                link(v.tensor_reduce(top, logits, X, ALU.max))
                v.tensor_tensor(grid(c, 8), logits, top.unsqueeze(2).to_broadcast([P, 4, 8]),
                                ALU.subtract).then_inc(m_shift, 1)

            def pick(c):
                dve.wait_ge(m_score, 2 + c + 1)
                score, total = grid(c, 8), rt[:, 2 + c, 0:4]
                link(v.tensor_reduce(total, score, X, ALU.add))
                link(v.reciprocal(total, total))
                link(v.tensor_tensor(score, score, total.unsqueeze(2).to_broadcast([P, 4, 8]), ALU.mult))
                rank = ranks(score, 8, earlier8, 4)
                v.tensor_scalar(comb_pieces2[:, BH * c:BH * c + BH, 24:32], rank, 1.5, None, ALU.is_lt)
                split_weights2(score, 8, c, 8).then_inc(m_comb, 1)

            def shared(k):
                dve.wait_ge(e_sg, k + 1)
                dve.wait_ge(e_x3, k + 1)
                if k >= 2:
                    dve.wait_ge(e_zd, k - 1)
                v.tensor_tensor(wc[:, k % 2, :], wb[:, k % 2, :], bank[2 + k % 2][:, :], ALU.mult)\
                    .then_inc(e_sh, 1)
            softmax_route(0)
            softmax_route(1)
            prep(1, 0)
            shared(0)
            shared(1)
            pick(0)
            shared(2)
            shared(3)
            def late(k):
                e, c = k // 2, k % 2
                dve.wait_ge(e_x2, k + 1)
                dve.wait_ge(e_u, k + 1)
                if k >= 2:
                    dve.wait_ge(e_y, k - 1)
                v.scalar_tensor_tensor(wc[:, c, :], bank[6][:, :], col(B2 + e), diag[:, c, :],
                                       ALU.add, ALU.mult).then_inc(e_v, 1)
            def weighed(k):
                c = k % 2
                dve.wait_ge(e_wb, k + 1)
                if k >= 2:
                    dve.wait_ge(e_x3, 4 + k - 1)
                v.tensor_tensor(wa[:, c, :], xn[:, c, :], bank[4][:, :], ALU.mult).then_inc(e_xs, 1)

            prep(1, 1)
            weighed(0)
            pick(1)
            for k in range(16):
                e, c = k // 2, k % 2
                if k + 1 < 16:
                    weighed(k + 1)
                if k >= 1:
                    late(k - 1)
                dve.wait_ge(e_x3b, k + 1)
                dve.wait_ge(e_mk, k + 1)
                v.tensor_tensor(diag[:, c, :], sq[:, c, :], bank[5][:, :], ALU.mult).then_inc(e_u, 1)
            late(15)
            for c in range(2):
                dve.wait_ge(e_y, 15 + c)
                add_gated(5, c, cen[:, c, :])
            norm(NORM_OF[6][0])
            prep(1, 2)
            prep(1, 3)
            dve.wait_ge(o_bias, 2)
            v.tensor_scalar(tgb[:, 6:7], bank[7][:, 0:1], col(O3B), tg[:, 6:7], ALU.add, ALU.mult)\
                .then_inc(tgb_ready, 1)
            attn(1)
            norm(NORM_OF[7][0])
            moe(MOE[1])




def kernel(**inputs):
    import numpy as _np
    import ml_dtypes as _ml
    import concourse.bacc as _bacc
    from concourse import mybir as _mybir
    from concourse.bass_utils import run_bass_kernel_spmd as _run

    I = {name: _np.asarray(value) for name, value in inputs.items()}
    P, T, D, HEADS, HD = 128, 1024, 128, 16, 8

    def columns(*vectors):
        return _np.stack(vectors, axis=1)

    def dim_major(w):
        return w.reshape(*w.shape[:-1], HEADS, HD).swapaxes(-1, -2).reshape(w.shape)

    def row_chunks(w):
        return w.reshape(-1, P, w.shape[1]).transpose(1, 0, 2).reshape(P, -1)

    def padded(w, width=P):
        return _np.pad(w, ((0, 0), (0, width - w.shape[1])))

    def expert_pairs(gate, up, down, shared_gate, shared_up, shared_down):
        e, i, h = gate.shape
        def in_major(w, shared):
            pairs = w.reshape(e // 2, 2 * i, h).transpose(0, 2, 1)
            return _np.concatenate([shared.T[None], pairs])
        downs = down.transpose(0, 2, 1).reshape(e // 2, 2 * i, h)
        downs = _np.concatenate([shared_down.T[None], downs])
        lane = _np.arange(P)
        mine = lane[None, :, None] % e == (2 * _np.arange(-1, e // 2)[:, None, None] + lane[None, None] // 64)
        mine &= lane[None, :, None] < 2 * e
        return _np.concatenate([in_major(gate, shared_gate), in_major(up, shared_up), downs,
                                mine.astype(_np.float32)], axis=2)

    qw, kw, vw = _np.split(I["L3_xattn_in_proj_weight"], 3, axis=0)
    qb, kb, vb = _np.split(I["L3_xattn_in_proj_bias"], 3)
    arrays = {
        "x_t": I["x"].reshape(T, D).T,
        "ctx_t": I["ctx_1024"].reshape(T, D).T,
        "mask": _np.broadcast_to(I["mask_BxS2_bk0"].reshape(1, T), (HEADS, T)).copy()
        .view(_np.int32),
        "gates": _np.broadcast_to(
            _np.stack([I["g_xattn"], I["g_ffn"]], axis=1).reshape(1, 8), (P, 8)),
        "mats0": _np.concatenate([
            dim_major(I["L0_xattn_Wk"]), dim_major(I["L0_xattn_Wq"]), I["L0_xattn_Wv"],
            I["L0_xattn_Wo"], padded(I["L0_ffn_router_weight"].T)], axis=1),
        "mats1": _np.concatenate([
            I["L1_xattn_Wq"], I["L1_xattn_Wk"], I["L1_xattn_Wv"], I["L1_xattn_Wg"], I["L1_xattn_Wo"],
            I["L1_ffn_W_fc"].T, row_chunks(I["L1_ffn_W_proj"].T)], axis=1),
        "lora": _np.concatenate([
            I["L1_ffn_A_fc"], I["L1_ffn_B_fc"].T, I["L1_ffn_A_proj"], I["L1_ffn_B_proj"].T], axis=1),
        "mats2": _np.concatenate([
            I["L2_xattn_Wq"], I["L2_xattn_Wkv"], row_chunks(I["L2_xattn_Wout"]),
            padded(I["L2_ffn_gate_w"].T), I["L2_ffn_sw1"].T, I["L2_ffn_sw2"].T,
            row_chunks(I["L2_ffn_sw3"].T)], axis=1),
        "mats3": _np.concatenate([
            dim_major(kw.T), dim_major(qw.T), vw.T, I["L3_xattn_out_w"].T,
            padded(I["L3_ffn_gate_w"].T)], axis=1),
        "cols": columns(
            dim_major(I["L0_xattn_bk"]), dim_major(I["L0_xattn_bq"]),
            I["L0_xattn_bv"], I["L0_xattn_bo"],
            dim_major(kb), dim_major(qb), vb, I["L3_xattn_out_b"],
            I["L1_xattn_bq"], I["L1_xattn_bk"], I["L1_xattn_bv"], I["L1_xattn_bg"], I["L1_xattn_bo"],
            *I["L1_ffn_b_fc"].reshape(4, P), I["L1_ffn_b_proj"],
            I["L2_xattn_ln_m_w"], I["L2_xattn_ln_m_b"], I["L2_xattn_ln_l_w"], I["L2_xattn_ln_l_b"],
            *I["L2_ffn_b1"], *I["L2_ffn_b2"], *I["L2_ffn_b3"]),
        "route_bias": _np.broadcast_to(_np.concatenate(
            [I["L0_ffn_e_bias"], I["L3_ffn_gate_bias"]]).reshape(1, -1), (P, 80)),
        "experts0": expert_pairs(*(I["L0_ffn_" + n] for n in (
            "gate_w", "up_w", "down_w", "sh_gate_w", "sh_up_w", "sh_down_w"))),
        "experts3": expert_pairs(*(I["L3_ffn_" + n] for n in (
            "eg_w", "eu_w", "ed_w", "sg_w", "su_w", "sd_w"))),
        "experts2": _np.concatenate([I["L2_ffn_" + n].transpose(0, 2, 1) for n in ("w1", "w3", "w2")], axis=2),
    }
    arrays.update(_constants(_np, _ml))
    arrays = {name: _np.ascontiguousarray(a) for name, a in arrays.items()}
    nc = _bacc.Bacc("TRN2", target_bir_lowering=False, num_devices=1)
    aps = {name: nc.dram_tensor("in_" + name, a.shape, _mybir.dt.from_np(a.dtype), kind="ExternalInput").ap()
           for name, a in arrays.items()}
    out = nc.dram_tensor("out_t", (D, T), _mybir.dt.float32, kind="ExternalOutput").ap()
    flamingo_kernel(nc, aps, out)
    r = _run(nc, [{"in_" + name: a for name, a in arrays.items()}], core_ids=[0])
    return _np.ascontiguousarray(r.results[0]["out_t"].T).reshape(8, 128, D)


def _constants(np, ml):
    P = 128
    bf16 = ml.bfloat16
    lane = np.arange(P)

    sel2 = np.zeros((8, 2, P, P), bf16)
    for e in range(8):
        for piece in range(3):
            sel2[e, 0, 8 * piece + e] = 1
        sel2[e, 1, 24 + e] = 1

    def earlier(n):
        return np.broadcast_to(np.tril(np.ones((n, n), np.float32), -1).reshape(1, n * n), (P, n * n))

    return {
        "ident": np.eye(P, dtype=np.float32),
        "ident_bf": np.eye(P, dtype=bf16),
        "earlier4": earlier(4), "earlier8": earlier(8),
        "select2": sel2.transpose(2, 0, 1, 3),
    }
```
